# Optimizing a Trainium2 kernel written in Bass

```python
import numpy as np
import jax
import jax.numpy as jnp

def _softmax(x, axis=-1):
    return jax.nn.softmax(x, axis=axis)

def _gelu(x):
    return jax.nn.gelu(x, approximate=True)

def _silu(x):
    return jax.nn.silu(x)

def _sigmoid(x):
    return jax.nn.sigmoid(x)

def _layernorm(x, axis=-1, eps=1e-05):
    m = jnp.mean(x, axis=axis, keepdims=True)
    v = jnp.var(x, axis=axis, keepdims=True)
    return (x - m) / jnp.sqrt(v + eps)

def _scatter_add(tgt, idx, src, axis=0):
    return tgt.at[idx].add(src)

def _segment_sum(src, seg, n):
    return jax.ops.segment_sum(src, seg, n)
kernel_name = 'mk_decoder_postln_d2_seqx_r8_5334b3'

def setup_inputs(seed: int=0):
    np.random.seed(seed)
    _w = jnp.asarray

    def _rec_inputs():
        import jax
        import jax.numpy as jnp
        _rk = jax.random.key(seed)
        x = 0.0003765 + 1 * jax.random.normal(jax.random.fold_in(_rk, 1), (16, 128, 256), jnp.float32)
        _lenS = 128 - jax.random.randint(jax.random.fold_in(_rk, 7), (16,), 0, max(1, 128 // 4) + 1, jnp.int32)
        _lenS2 = 128 - jax.random.randint(jax.random.fold_in(_rk, 8), (16,), 0, max(1, 128 // 4) + 1, jnp.int32)
        _ctx_2048P = jax.random.normal(jax.random.fold_in(_rk, 11), (16, 16, 256), jnp.float32)
        _ctx_2048c = jax.random.dirichlet(jax.random.fold_in(_rk, 511), 0.3 * jnp.ones((16,), jnp.float32), (16, 128))
        _ctx_2048t = jnp.einsum('bsk,bkd->bsd', _ctx_2048c, _ctx_2048P)
        _ctx_2048t = _ctx_2048t * jax.lax.rsqrt(jnp.mean(jnp.square(_ctx_2048t)) + 1e-12) * 0.953939
        ctx_2048 = -0.000292821 + 1.00034 * (_ctx_2048t + 0.3 * jax.random.normal(jax.random.fold_in(_rk, 611), (16, 128, 256), jnp.float32))
        return (x, ctx_2048)
    x, ctx_2048 = _rec_inputs()

    def _L0_attn_setup():
        import jax, jax.numpy as jnp
        import numpy as np
        B, T, C = (4, 512, 256)

        def _scan_op(a, bb):
            g_i, v_i = a
            g_j, v_j = bb
            return (g_j * g_i, g_j * v_i + v_j)
        key = jax.random.key(seed)
        k1, k2 = jax.random.split(key)
        x = jax.random.normal(k1, (B, T, C), dtype=jnp.float32)
        W = jax.random.normal(k2, (2 * C, C), dtype=jnp.float32) * (1.0 / np.sqrt(C))
        b = jnp.zeros((2 * C,), dtype=jnp.float32)
        return {'x': x, 'W': W, 'b': b}
    _L0_attn_all = _L0_attn_setup()
    _L0_attn_in = {k: v for k, v in _L0_attn_all.items() if k in ('W', 'b')}
    del _L0_attn_all

    def _L0_xattn_setup():
        import jax, jax.numpy as jnp
        import numpy as np
        key = jax.random.key(seed)
        k1, k2, k3, k4, k5 = jax.random.split(key, 5)
        B, D_MODEL, L = (2, 128, 256)
        HEAD_DIM = 8
        H = D_MODEL // HEAD_DIM
        return {'k': jax.random.normal(k1, (B, D_MODEL, L), dtype=jnp.float32), 'v': jax.random.normal(k2, (B, D_MODEL, L), dtype=jnp.float32), 'q': jax.random.normal(k3, (B, D_MODEL, L), dtype=jnp.float32), 'ssm_kernel': jax.random.normal(k4, (H, L), dtype=jnp.float32), 'D': jax.random.normal(k5, (H,), dtype=jnp.float32), 'head_dim': HEAD_DIM}
    _L0_xattn_all = _L0_xattn_setup()
    _L0_xattn_in = {k: v for k, v in _L0_xattn_all.items() if k in ('ssm_kernel', 'D')}
    del _L0_xattn_all

    def _L0_ffn_setup():
        import jax, jax.numpy as jnp
        import numpy as np
        B, T, D = (4, 128, 256)
        N, S, H = (8, 8, 8)
        ETA = 1.0
        key = jax.random.key(seed)
        ks = jax.random.split(key, 9)
        return {'x': jax.random.normal(ks[0], (B, T, D), jnp.float32), 'select_weight': jax.random.normal(ks[1], (N, D, S), jnp.float32) / D, 'select_mean_diff': jax.random.normal(ks[2], (N, D), jnp.float32) / D, 'imp_center': jax.random.normal(ks[3], (N,), jnp.float32), 'imp_slope': jax.random.normal(ks[4], (N,), jnp.float32) * 5.0, 'lora_update': jax.random.normal(ks[5], (N, D, H), jnp.float32) * 0.02, 'lora_degen': jax.random.normal(ks[6], (N, D, H), jnp.float32) * 0.02, 'bias_w': jax.random.normal(ks[7], (N, D), jnp.float32) * 0.02, 'debias_w': jax.random.normal(ks[8], (N, D), jnp.float32) * 0.02}
    _L0_ffn_all = _L0_ffn_setup()
    _L0_ffn_in = {k: v for k, v in _L0_ffn_all.items() if k in ('select_weight', 'select_mean_diff', 'imp_center', 'imp_slope', 'lora_update', 'lora_degen', 'bias_w', 'debias_w')}
    del _L0_ffn_all

    def _L1_attn_setup():
        import jax, jax.numpy as jnp
        import numpy as np
        B, S, D = (2, 256, 256)
        NQ, NKV = (16, 4)
        HD = D // NQ
        GROUP = NQ // NKV
        key = jax.random.key(seed)
        k_x, k_q, k_k, k_v, k_o = jax.random.split(key, 5)
        scale = 0.02
        return {'x': jax.random.normal(k_x, (B, S, D), dtype=jnp.float32), 'Wq': jax.random.normal(k_q, (D, D), dtype=jnp.float32) * scale, 'Wk': jax.random.normal(k_k, (NKV * HD, D), dtype=jnp.float32) * scale, 'Wv': jax.random.normal(k_v, (NKV * HD, D), dtype=jnp.float32) * scale, 'Wo': jax.random.normal(k_o, (D, D), dtype=jnp.float32) * scale}
    _L1_attn_all = _L1_attn_setup()
    _L1_attn_in = {k: v for k, v in _L1_attn_all.items() if k in ('Wq', 'Wk', 'Wv', 'Wo')}
    del _L1_attn_all

    def _L1_xattn_setup():
        import jax, jax.numpy as jnp
        import numpy as np
        FP8_MAX = 448.0
        EPS = 1e-05

        def _fp8_roundtrip(x):
            return x.astype(jnp.float8_e4m3fn).astype(jnp.float32)

        def _div_clamp_fp8(x, scale):
            y = jnp.clip(x.astype(jnp.float32) / scale, -FP8_MAX, FP8_MAX)
            y = y.astype(jnp.bfloat16).astype(jnp.float32)
            return _fp8_roundtrip(y)

        def _ln(x, w, b):
            mu = jnp.mean(x, axis=-1, keepdims=True)
            var = jnp.mean(jnp.square(x - mu), axis=-1, keepdims=True)
            return (x - mu) * jax.lax.rsqrt(var + EPS) * w + b

        def _fp8_linear_pertensor(x, wq, w_scale, in_scale):
            xq = _div_clamp_fp8(x, in_scale)
            return jnp.einsum('bsi,oi->bso', xq * in_scale, wq) * w_scale

        def _gqa(q, k, v):
            scale = 1.0 / np.sqrt(q.shape[-1])
            scores = jnp.einsum('bsghd,btgd->bghst', q, k) * scale
            p = jax.nn.softmax(scores, axis=-1)
            return jnp.einsum('bghst,btgd->bsghd', p, v)
        key = jax.random.key(seed)
        ks = jax.random.split(key, 8)
        B, S, SC, H, NH, G, D = (2, 256, 64, 256, 16, 8, 128)

        def qw(k, out_f, in_f):
            w = jax.random.normal(k, (out_f, in_f), jnp.float32) * 0.02
            sc = jnp.max(jnp.abs(w)) / FP8_MAX
            return (_fp8_roundtrip(w / sc), sc.astype(jnp.float32))
        wq, wq_s = qw(ks[0], NH * D, H)
        wqx, wqx_s = qw(ks[1], NH * D, H)
        wk, wk_s = qw(ks[2], G * D, H)
        wv, wv_s = qw(ks[3], G * D, H)
        wproj, wp_s = qw(ks[4], H, 2 * NH * D)
        return {'hidden_states': jax.random.normal(ks[5], (B, S, H), jnp.float32), 'cond': jax.random.normal(ks[6], (B, SC, H), jnp.float32), 'ln_w': jnp.ones((H,), jnp.float32), 'ln_b': jnp.zeros((H,), jnp.float32), 'wq': wq, 'wq_scale': wq_s, 'q_in_scale': jnp.full((H,), 0.05, jnp.float32), 'wqx': wqx, 'wqx_scale': wqx_s, 'qx_in_scale': jnp.full((H,), 0.05, jnp.float32), 'wk': wk, 'wk_scale': wk_s, 'k_in_scale': jnp.full((H,), 0.05, jnp.float32), 'wv': wv, 'wv_scale': wv_s, 'v_in_scale': jnp.full((H,), 0.05, jnp.float32), 'w_kv_x': jax.random.normal(ks[7], (2 * G * D, H), jnp.float32) * 0.02, 'qln_w': jnp.ones((D,), jnp.float32), 'qln_b': jnp.zeros((D,), jnp.float32), 'kln_w': jnp.ones((D,), jnp.float32), 'kln_b': jnp.zeros((D,), jnp.float32), 'qxln_w': jnp.ones((D,), jnp.float32), 'qxln_b': jnp.zeros((D,), jnp.float32), 'kxln_w': jnp.ones((D,), jnp.float32), 'kxln_b': jnp.zeros((D,), jnp.float32), 'wproj': wproj, 'proj_w_scale': wp_s, 'proj_in_scale': jnp.asarray(0.05, jnp.float32), 'proj_smooth': jnp.full((2 * NH * D,), 0.05, jnp.float32)}
    _L1_xattn_all = _L1_xattn_setup()
    _L1_xattn_in = {k: v for k, v in _L1_xattn_all.items() if k in ('ln_w', 'ln_b', 'wq', 'wq_scale', 'q_in_scale', 'wqx', 'wqx_scale', 'qx_in_scale', 'wk', 'wk_scale', 'k_in_scale', 'wv', 'wv_scale', 'v_in_scale', 'w_kv_x', 'qln_w', 'qln_b', 'kln_w', 'kln_b', 'qxln_w', 'qxln_b', 'kxln_w', 'kxln_b', 'wproj', 'proj_w_scale', 'proj_in_scale', 'proj_smooth')}
    del _L1_xattn_all

    def _L1_ffn_setup():
        import jax, jax.numpy as jnp
        import numpy as np
        E, TOPK, H, I = (8, 2, 256, 512)
        SOFTCAP = 30.0
        key = jax.random.key(seed)
        ks = jax.random.split(key, 5)
        s = 1.0 / np.sqrt(H)
        si = 1.0 / np.sqrt(I)
        return {'hidden_states': jax.random.normal(ks[0], (4, 256, H), jnp.float32), 'w_gate': jax.random.normal(ks[1], (H, E), jnp.float32) * s, 'w1': jax.random.normal(ks[2], (E, H, I), jnp.float32) * s, 'w3': jax.random.normal(ks[3], (E, H, I), jnp.float32) * s, 'w2': jax.random.normal(ks[4], (E, I, H), jnp.float32) * si}
    _L1_ffn_all = _L1_ffn_setup()
    _L1_ffn_in = {k: v for k, v in _L1_ffn_all.items() if k in ('w_gate', 'w1', 'w3', 'w2')}
    del _L1_ffn_all
    return {'x': x, 'ctx_2048': ctx_2048, 'L0_attn_W': _L0_attn_in['W'], 'L0_attn_b': _L0_attn_in['b'], 'L0_xattn_ssm_kernel': _L0_xattn_in['ssm_kernel'], 'L0_xattn_D': _L0_xattn_in['D'], 'L0_ffn_select_weight': _L0_ffn_in['select_weight'], 'L0_ffn_select_mean_diff': _L0_ffn_in['select_mean_diff'], 'L0_ffn_imp_center': _L0_ffn_in['imp_center'], 'L0_ffn_imp_slope': _L0_ffn_in['imp_slope'], 'L0_ffn_lora_update': _L0_ffn_in['lora_update'], 'L0_ffn_lora_degen': _L0_ffn_in['lora_degen'], 'L0_ffn_bias_w': _L0_ffn_in['bias_w'], 'L0_ffn_debias_w': _L0_ffn_in['debias_w'], 'L1_attn_Wq': _L1_attn_in['Wq'], 'L1_attn_Wk': _L1_attn_in['Wk'], 'L1_attn_Wv': _L1_attn_in['Wv'], 'L1_attn_Wo': _L1_attn_in['Wo'], 'L1_xattn_ln_w': _L1_xattn_in['ln_w'], 'L1_xattn_ln_b': _L1_xattn_in['ln_b'], 'L1_xattn_wq': _L1_xattn_in['wq'], 'L1_xattn_wq_scale': _L1_xattn_in['wq_scale'], 'L1_xattn_q_in_scale': _L1_xattn_in['q_in_scale'], 'L1_xattn_wqx': _L1_xattn_in['wqx'], 'L1_xattn_wqx_scale': _L1_xattn_in['wqx_scale'], 'L1_xattn_qx_in_scale': _L1_xattn_in['qx_in_scale'], 'L1_xattn_wk': _L1_xattn_in['wk'], 'L1_xattn_wk_scale': _L1_xattn_in['wk_scale'], 'L1_xattn_k_in_scale': _L1_xattn_in['k_in_scale'], 'L1_xattn_wv': _L1_xattn_in['wv'], 'L1_xattn_wv_scale': _L1_xattn_in['wv_scale'], 'L1_xattn_v_in_scale': _L1_xattn_in['v_in_scale'], 'L1_xattn_w_kv_x': _L1_xattn_in['w_kv_x'], 'L1_xattn_qln_w': _L1_xattn_in['qln_w'], 'L1_xattn_qln_b': _L1_xattn_in['qln_b'], 'L1_xattn_kln_w': _L1_xattn_in['kln_w'], 'L1_xattn_kln_b': _L1_xattn_in['kln_b'], 'L1_xattn_qxln_w': _L1_xattn_in['qxln_w'], 'L1_xattn_qxln_b': _L1_xattn_in['qxln_b'], 'L1_xattn_kxln_w': _L1_xattn_in['kxln_w'], 'L1_xattn_kxln_b': _L1_xattn_in['kxln_b'], 'L1_xattn_wproj': _L1_xattn_in['wproj'], 'L1_xattn_proj_w_scale': _L1_xattn_in['proj_w_scale'], 'L1_xattn_proj_in_scale': _L1_xattn_in['proj_in_scale'], 'L1_xattn_proj_smooth': _L1_xattn_in['proj_smooth'], 'L1_ffn_w_gate': _L1_ffn_in['w_gate'], 'L1_ffn_w1': _L1_ffn_in['w1'], 'L1_ffn_w3': _L1_ffn_in['w3'], 'L1_ffn_w2': _L1_ffn_in['w2']}

def reference(x, ctx_2048, L0_attn_W, L0_attn_b, L0_xattn_ssm_kernel, L0_xattn_D, L0_ffn_select_weight, L0_ffn_select_mean_diff, L0_ffn_imp_center, L0_ffn_imp_slope, L0_ffn_lora_update, L0_ffn_lora_degen, L0_ffn_bias_w, L0_ffn_debias_w, L1_attn_Wq, L1_attn_Wk, L1_attn_Wv, L1_attn_Wo, L1_xattn_ln_w, L1_xattn_ln_b, L1_xattn_wq, L1_xattn_wq_scale, L1_xattn_q_in_scale, L1_xattn_wqx, L1_xattn_wqx_scale, L1_xattn_qx_in_scale, L1_xattn_wk, L1_xattn_wk_scale, L1_xattn_k_in_scale, L1_xattn_wv, L1_xattn_wv_scale, L1_xattn_v_in_scale, L1_xattn_w_kv_x, L1_xattn_qln_w, L1_xattn_qln_b, L1_xattn_kln_w, L1_xattn_kln_b, L1_xattn_qxln_w, L1_xattn_qxln_b, L1_xattn_kxln_w, L1_xattn_kxln_b, L1_xattn_wproj, L1_xattn_proj_w_scale, L1_xattn_proj_in_scale, L1_xattn_proj_smooth, L1_ffn_w_gate, L1_ffn_w1, L1_ffn_w3, L1_ffn_w2):
    import jax
    import jax.numpy as jnp

    def _L0_attn_ref(x, W, b):
        import jax, jax.numpy as jnp
        import numpy as np
        B, T, C = (4, 512, 256)

        def _scan_op(a, bb):
            g_i, v_i = a
            g_j, v_j = bb
            return (g_j * g_i, g_j * v_i + v_j)
        params = jnp.einsum('btc,dc->btd', x, W) + b
        gates, values = jnp.split(params, 2, axis=-1)
        gates = jax.nn.sigmoid(gates)
        values = jnp.tanh(values)
        _, hidden = jax.lax.associative_scan(_scan_op, (gates, values), axis=1)
        return hidden

    def _L0_xattn_ref(k, v, q, ssm_kernel, D, head_dim):
        import jax, jax.numpy as jnp
        import numpy as np
        B, HD, L = k.shape
        H = HD // head_dim
        fft_size = 2 * L
        k_ = k.reshape(B, H, head_dim, L)
        v_ = v.reshape(B, H, head_dim, L)
        q_ = q.reshape(B, H, head_dim, L)
        kv = jnp.einsum('bhil,bhjl->bijhl', k_, v_)
        kv_f = jnp.fft.rfft(kv, n=fft_size)
        kernel_f = jnp.fft.rfft(ssm_kernel, n=fft_size)
        y = jnp.fft.irfft(kv_f * kernel_f, n=fft_size)[..., :L]
        out = y + kv * D[None, None, None, :, None]
        out = jnp.einsum('bijhl,bhil->bjhl', out, q_)
        out = jnp.transpose(out, (0, 2, 1, 3)).reshape(B, H * head_dim, L)
        return out.astype(k.dtype)

    def _L0_ffn_ref(x, select_weight, select_mean_diff, imp_center, imp_slope, lora_update, lora_degen, bias_w, debias_w):
        import jax, jax.numpy as jnp
        import numpy as np
        B, T, D = (4, 128, 256)
        N, S, H = (8, 8, 8)
        ETA = 1.0
        x_diff = x[:, None, :, :] - select_mean_diff[None, :, None, :]
        x_diff = x_diff / jnp.linalg.norm(x_diff, axis=3, keepdims=True)
        cont = jnp.einsum('nds,bntd->bnts', select_weight, x_diff) ** 2
        score = cont.sum(axis=-1)
        gate = jax.nn.sigmoid(imp_slope[None, :, None] * (score - imp_center[None, :, None]))
        sel_scale = gate.max(axis=1)[..., None]
        sel_idx = gate.argmax(axis=1)
        debias = jnp.take(debias_w, sel_idx, axis=0)
        bias = jnp.take(bias_w, sel_idx, axis=0)
        upd = jnp.take(lora_update, sel_idx, axis=0)
        dgn = jnp.take(lora_degen, sel_idx, axis=0)
        x_debias = x - debias
        mod_x = jnp.einsum('btdh,btd->bth', upd, x_debias)
        degen_up = jnp.einsum('btdh,bth->btd', dgn, mod_x)
        mod_x_bias = ETA * (bias + degen_up)
        return (1.0 - sel_scale) * x + sel_scale * mod_x_bias

    def _L1_attn_ref(x, Wq, Wk, Wv, Wo):
        import jax, jax.numpy as jnp
        import numpy as np
        B, S, D = (2, 256, 256)
        NQ, NKV = (16, 4)
        HD = D // NQ
        GROUP = NQ // NKV
        b, s, _ = x.shape
        Q = (x @ Wq.T).reshape(b, s, NQ, HD).transpose(0, 2, 1, 3)
        K = (x @ Wk.T).reshape(b, s, NKV, HD).transpose(0, 2, 1, 3)
        V = (x @ Wv.T).reshape(b, s, NKV, HD).transpose(0, 2, 1, 3)
        K = jnp.repeat(K, GROUP, axis=1)
        V = jnp.repeat(V, GROUP, axis=1)
        scores = jnp.einsum('bhqd,bhkd->bhqk', Q, K) / jnp.sqrt(jnp.float32(HD))
        causal = jnp.triu(jnp.ones((s, s), dtype=bool), k=1)
        scores = jnp.where(causal, -jnp.inf, scores)
        weights = jax.nn.softmax(scores, axis=-1)
        ctx = jnp.einsum('bhqk,bhkd->bhqd', weights, V)
        ctx = ctx.transpose(0, 2, 1, 3).reshape(b, s, D)
        return ctx @ Wo.T

    def _L1_xattn_ref(hidden_states, cond, ln_w, ln_b, wq, wq_scale, q_in_scale, wqx, wqx_scale, qx_in_scale, wk, wk_scale, k_in_scale, wv, wv_scale, v_in_scale, w_kv_x, qln_w, qln_b, kln_w, kln_b, qxln_w, qxln_b, kxln_w, kxln_b, wproj, proj_w_scale, proj_in_scale, proj_smooth):
        import jax, jax.numpy as jnp
        import numpy as np
        FP8_MAX = 448.0
        EPS = 1e-05

        def _fp8_roundtrip(x):
            return x.astype(jnp.float8_e4m3fn).astype(jnp.float32)

        def _div_clamp_fp8(x, scale):
            y = jnp.clip(x.astype(jnp.float32) / scale, -FP8_MAX, FP8_MAX)
            y = y.astype(jnp.bfloat16).astype(jnp.float32)
            return _fp8_roundtrip(y)

        def _ln(x, w, b):
            mu = jnp.mean(x, axis=-1, keepdims=True)
            var = jnp.mean(jnp.square(x - mu), axis=-1, keepdims=True)
            return (x - mu) * jax.lax.rsqrt(var + EPS) * w + b

        def _fp8_linear_pertensor(x, wq, w_scale, in_scale):
            xq = _div_clamp_fp8(x, in_scale)
            return jnp.einsum('bsi,oi->bso', xq * in_scale, wq) * w_scale

        def _gqa(q, k, v):
            scale = 1.0 / np.sqrt(q.shape[-1])
            scores = jnp.einsum('bsghd,btgd->bghst', q, k) * scale
            p = jax.nn.softmax(scores, axis=-1)
            return jnp.einsum('bghst,btgd->bsghd', p, v)
        b, s, _ = hidden_states.shape
        sc = cond.shape[1]
        d = qln_w.shape[0]
        nh = wq.shape[0] // d
        g = wk.shape[0] // d
        hpg = nh // g
        ln_out = _ln(hidden_states, ln_w, ln_b)
        q = _fp8_linear_pertensor(ln_out, wq, wq_scale, q_in_scale).reshape(b, s, g, hpg, d)
        q = _ln(q, qln_w, qln_b)
        k = _fp8_linear_pertensor(ln_out, wk, wk_scale, k_in_scale).reshape(b, s, g, d)
        k = _ln(k, kln_w, kln_b)
        v = _fp8_linear_pertensor(ln_out, wv, wv_scale, v_in_scale).reshape(b, s, g, d)
        core = _gqa(q, k, v).reshape(b, s, nh * d)
        qx = _fp8_linear_pertensor(ln_out, wqx, wqx_scale, qx_in_scale).reshape(b, s, g, hpg, d)
        qx = _ln(qx, qxln_w, qxln_b)
        kvx = jnp.einsum('bsi,oi->bso', cond, w_kv_x)
        kx, vx = jnp.split(kvx, 2, axis=-1)
        kx = _ln(kx.reshape(b, sc, g, d), kxln_w, kxln_b)
        vx = vx.reshape(b, sc, g, d)
        xout = _gqa(qx, kx, vx).reshape(b, s, nh * d)
        cat = jnp.concatenate([core, xout], axis=-1)
        catq = _div_clamp_fp8(cat, proj_smooth)
        return jnp.einsum('bsi,oi->bso', catq, wproj) * (proj_in_scale * proj_w_scale)

    def _L1_ffn_ref(hidden_states, w_gate, w1, w3, w2):
        import jax, jax.numpy as jnp
        import numpy as np
        E, TOPK, H, I = (8, 2, 256, 512)
        SOFTCAP = 30.0
        orig_shape = hidden_states.shape
        x = hidden_states.reshape(-1, H)
        logits = x @ w_gate
        logits = SOFTCAP * jnp.tanh(logits / SOFTCAP)
        probs = jax.nn.softmax(logits, axis=-1)
        _, idx = jax.lax.top_k(probs, TOPK)
        mask = jax.nn.one_hot(idx, E, dtype=probs.dtype).sum(-2)
        weights = probs * mask
        out = jnp.zeros_like(x)
        for e in range(E):
            h = jax.nn.silu(x @ w1[e]) * (x @ w3[e])
            out = out + h @ w2[e] * weights[:, e:e + 1]
        return out.reshape(orig_shape)
    x = _layernorm(x + _L0_attn_ref(x, L0_attn_W, L0_attn_b), axis=-1)
    x = _layernorm(x + _L0_xattn_ref(ctx_2048, ctx_2048, x, L0_xattn_ssm_kernel, L0_xattn_D, 8), axis=-1)
    x = _layernorm(x + _L0_ffn_ref(x, L0_ffn_select_weight, L0_ffn_select_mean_diff, L0_ffn_imp_center, L0_ffn_imp_slope, L0_ffn_lora_update, L0_ffn_lora_degen, L0_ffn_bias_w, L0_ffn_debias_w), axis=-1)
    x = _layernorm(x + _L1_attn_ref(x, L1_attn_Wq, L1_attn_Wk, L1_attn_Wv, L1_attn_Wo), axis=-1)
    x = _layernorm(x + _L1_xattn_ref(x, ctx_2048, L1_xattn_ln_w, L1_xattn_ln_b, L1_xattn_wq, L1_xattn_wq_scale, L1_xattn_q_in_scale, L1_xattn_wqx, L1_xattn_wqx_scale, L1_xattn_qx_in_scale, L1_xattn_wk, L1_xattn_wk_scale, L1_xattn_k_in_scale, L1_xattn_wv, L1_xattn_wv_scale, L1_xattn_v_in_scale, L1_xattn_w_kv_x, L1_xattn_qln_w, L1_xattn_qln_b, L1_xattn_kln_w, L1_xattn_kln_b, L1_xattn_qxln_w, L1_xattn_qxln_b, L1_xattn_kxln_w, L1_xattn_kxln_b, L1_xattn_wproj, L1_xattn_proj_w_scale, L1_xattn_proj_in_scale, L1_xattn_proj_smooth), axis=-1)
    x = _layernorm(x + _L1_ffn_ref(x, L1_ffn_w_gate, L1_ffn_w1, L1_ffn_w3, L1_ffn_w2), axis=-1)
    return x

_drawn_inputs = setup_inputs


def setup_inputs(seed=0):
    import zlib

    import numpy as np

    out = dict(_drawn_inputs(seed))
    spreads = {'L0_attn_b': (0.0, 0.1),
     'L1_xattn_ln_w': (1.0, 0.2),
     'L1_xattn_ln_b': (0.0, 0.1),
     'L1_xattn_q_in_scale': (0.05000000074505806, 0.6),
     'L1_xattn_qx_in_scale': (0.05000000074505806, 0.6),
     'L1_xattn_k_in_scale': (0.05000000074505806, 0.6),
     'L1_xattn_v_in_scale': (0.05000000074505806, 0.6),
     'L1_xattn_qln_w': (1.0, 0.6),
     'L1_xattn_qln_b': (0.0, 0.633),
     'L1_xattn_kln_w': (1.0, 0.6),
     'L1_xattn_kln_b': (0.0, 2.0),
     'L1_xattn_qxln_w': (1.0, 0.6),
     'L1_xattn_qxln_b': (0.0, 0.487),
     'L1_xattn_kxln_w': (1.0, 0.6),
     'L1_xattn_kxln_b': (0.0, 2.0),
     'L1_xattn_proj_smooth': (0.05000000074505806, 0.2)}
    factors = {'L0_ffn_select_weight': 64.0,
     'L0_ffn_debias_w': 39.116,
     'L1_attn_Wq': 6.26,
     'L1_attn_Wk': 5.762,
     'L0_ffn_select_mean_diff': 8.0}
    for name, (base, spread) in spreads.items():
        noise = np.random.default_rng([zlib.crc32(name.encode()), seed]).standard_normal(out[name].shape)
        drawn = base * np.exp(spread * noise) if base else spread * noise
        out[name] = jnp.asarray(drawn.astype(out[name].dtype))
    for name, factor in factors.items():
        out[name] = (out[name] * factor).astype(out[name].dtype)
    return out
```

```python
import numpy as np
import concourse.bass as bass
from concourse import mybir
from contextlib import ExitStack

F32, F32R, BF16 = mybir.dt.float32, mybir.dt.float32r, mybir.dt.bfloat16
I32, U16 = mybir.dt.int32, mybir.dt.uint16
ACT = mybir.ActivationFunctionType
ALU = mybir.AluOpType
AX = mybir.AxisListType

B, S, C = 16, 128, 256
P = 128
CB = C // P
TOK = B * S
W512 = 512
NTG = TOK // W512
LN_EPS = 1e-5
CH, CD = 16, 8
NE0, NS0 = 8, 8
SEL, UPD = NE0 * NS0, NE0 * NS0
FW = SEL + UPD + NE0
HQ, HKV, HD = 16, 4, 16
G, D = 8, 128
UW = 4 * D
FP8_MAX = 448.0
FP8_MIN_NORMAL = 2.0 ** -6
ROUND = 1.5 * 2.0 ** 20
E, I = 8, 512
IB = I // P
SOFTCAP = 30.0

SMALL = {}
_at = 0
for _name, _n in (("ab", 4), ("qw", 1), ("qb", 1), ("kw", 1), ("kb", 1), ("qxw", 1), ("qxb", 1),
                  ("kxw", 1), ("kxb", 1), ("lnw", 2), ("lnb", 2), ("sq", 2), ("sk", 2), ("sv", 2),
                  ("sqx", 2), ("smooth", 32), ("wsq", 1), ("wsk", 1), ("wsv", 1), ("wsqx", 1),
                  ("pin", 1), ("pw", 1), ("dskip", CH), ("center", NE0), ("slope", NE0)):
    SMALL[_name] = (_at, _at + _n)
    _at += _n
NSMALL = _at


class Links:

    def __init__(self, eng, sem):
        self.eng, self.sem, self.base, self.n, self.i, self.per = eng, sem, 0, 0, None, 0

    def enter(self, i, per):
        self.base, self.n, self.i, self.per = self.base + self.n, 0, i, per

    def leave(self, trips):
        assert self.n == self.per, (self.n, self.per)
        self.base, self.n, self.i = self.base + self.per * trips, 0, None

    def __call__(self, ins):
        ins.then_inc(self.sem, 1)
        self.n += 1
        at = self.base + self.n
        self.eng.wait_ge(self.sem, at if self.i is None else self.i * self.per + at)
        return ins


class Unit:

    def __init__(self, b, g, per, peeled, b_par=0):
        self.b, self.g, self.n, self.peeled, self.b_par = b, g, b * per + g, peeled, b_par

    def before(self, k):
        return not self.peeled or self.n >= k


def skewed(eng, outer, per, stages, peel=1):
    def step(b, j, g, in_loop):
        for stage, lag in stages:
            at, back = (g - lag) % per, -((g - lag) // per)
            if in_loop or (b - back >= 0 and b - back < outer):
                u_b = b + (j - back) if in_loop else b - back
                stage(Unit(u_b, at, per, not in_loop, (j - back) % 2 if in_loop else (b - back) % 2))

    assert outer % peel == 0
    for b in range(peel):
        for g in range(per):
            step(b, 0, g, False)
    if outer > peel:
        with eng.Fori(1, outer // peel) as i:
            for j in range(peel):
                for g in range(per):
                    step(i * peel, j, g, True)
    for g in range(max(lag for _, lag in stages)):
        step(outer + g // per, 0, g % per, False)


def build(nc, io, stop=99):
    ctx = ExitStack()
    with ctx:
        held = []

        def sem(name):
            held.append(nc.alloc_semaphore(name=name))
            return held[-1]

        def layer(f, *a, **k):
            f(*a, **k, **args)
            nc.clear_and_free_semaphores(list(held))
            held.clear()
            nc.all_engine_barrier()

        def sbuf(c, name, shape, dt):
            return c.enter_context(nc.sbuf_tensor(name, shape, dt))

        X = sbuf(ctx, "X", [P, B, C], F32)
        XT = sbuf(ctx, "XT", [P, CB, TOK], F32)
        small = sbuf(ctx, "small", [P, NSMALL], F32)
        ident = sbuf(ctx, "ident", [P, P], F32)
        ps = [ctx.enter_context(nc.psum_tensor(f"ps{i}", [P, W512], F32)) for i in range(8)]

        def col(name, k=0):
            a = SMALL[name][0] + k
            return small[:, a:a + 1]

        def cols(name):
            return small[:, slice(*SMALL[name])]

        args = dict(nc=nc, io=io, sem=sem, sbuf=sbuf, X=X, XT=XT, small=small, ident=ident, ps=ps,
                    col=col, cols=cols)
        layer(scan_layer)
        layer(norm_layer, "n0", from_channels=True)
        if stop > 1:
            layer(conv_layer)
            layer(norm_layer, "n1", from_channels=True)
        if stop > 2:
            layer(routed_layer)
            layer(norm_layer, "n2")
        if stop > 3:
            layer(causal_layer)
            layer(norm_layer, "n3")
        if stop > 4:
            layer(quant_layer)
            layer(norm_layer, "n4")
        if stop > 5:
            layer(moe_layer)
            layer(norm_layer, "n5", back=False)

        out_done = sem("out_done")
        with nc.Block() as block:
            @block.sync
            def _(sp):
                sp.dma_start(io["out"].rearrange("b t c -> t b c"), X[:, :, :]).then_inc(out_done, 16)
                sp.wait_ge(out_done, 16)


def rsqrt(dve, link, x, y, t, n):
    link(dve.tensor_scalar(y.bitcast(I32), x.bitcast(I32), 1, None, ALU.logical_shift_right))
    link(dve.tensor_scalar(y.bitcast(I32), y.bitcast(I32), -1.0, float(0x5F3759DF), ALU.mult, ALU.add))
    for _ in range(n):
        link(dve.tensor_tensor(t, y, y, ALU.mult))
        link(dve.tensor_tensor(t, t, x, ALU.mult))
        link(dve.tensor_scalar(t, t, -0.5, 1.5, ALU.mult, ALU.add))
        link(dve.tensor_tensor(y, y, t, ALU.mult))


def norm_layer(tag, nc, io, sem, sbuf, X, XT, small, ident, ps, col, cols, from_channels=False,
               back=True, dst=None, eps=LN_EPS):
    dst = X if dst is None else dst
    ctx = ExitStack()
    with ctx:
        st = sbuf(ctx, tag + "_st", [P, B, 6], F32)
        m = [sbuf(ctx, f"{tag}_m{k}", [P, B], F32) for k in range(5)]
        mean, var, rstd, tmp, nmr = m
        s_tok = sem(tag + "_tok")
        s_evac = sem(tag + "_evac")
        s_norm = sem(tag + "_norm")
        s_back = sem(tag + "_back")
        s_free = sem(tag + "_free")
        s_link = sem(tag + "_link")
        with nc.Block() as block:
            @block.tensor
            def _(pe):
                if from_channels:
                    for b in range(B):
                        for k in range(CB):
                            mm = pe.transpose(ps[b // 2][:, (b % 2) * C + k * P:(b % 2) * C + (k + 1) * P],
                                              XT[:, k, b * S:(b + 1) * S], ident[:, :])
                        if b % 2:
                            mm.then_inc(s_tok, 1)
                if back:
                    for tg in range(NTG):
                        pe.wait_ge(s_norm, tg * 4 + 4)
                        if from_channels:
                            pe.wait_ge(s_evac, B // 2)
                        for k in range(CB):
                            for j in range(4):
                                b = tg * 4 + j
                                mm = pe.transpose(ps[tg * 2 + k][:, j * P:(j + 1) * P],
                                                  dst[:, b, k * P:(k + 1) * P], ident[:, :])
                            mm.then_inc(s_back, 1)

            @block.scalar
            def _(act):
                if from_channels:
                    for h in range(B // 2):
                        act.wait_ge(s_tok, h + 1)
                        act.activation(X[:, 2 * h:2 * h + 2, :],
                                       ps[h][:, :].rearrange("p (b c) -> p b c", b=2), ACT.Copy).then_inc(s_evac, 1)
                if back:
                    for tg in range(NTG):
                        for k in range(CB):
                            act.wait_ge(s_back, tg * 2 + k + 1)
                            act.activation(XT[:, k, tg * W512:(tg + 1) * W512], ps[tg * 2 + k][:, :],
                                           ACT.Copy).then_inc(s_free, 1)
                    act.wait_ge(s_free, NTG * CB)

            @block.vector
            def _(dve):
                link = Links(dve, s_link)
                for b in range(B):
                    if from_channels and b % 2 == 0:
                        dve.wait_ge(s_evac, b // 2 + 1)
                    ins = dve.bn_stats(st[:, b, :], X[:, b, :])
                link(ins)
                even, odd = st[:, :, 1], st[:, :, 4]
                link(dve.tensor_tensor(mean[:, :], even, odd, ALU.add))
                link(dve.tensor_tensor(tmp[:, :], even, odd, ALU.subtract))
                link(dve.tensor_tensor(tmp[:, :], tmp[:, :], tmp[:, :], ALU.mult))
                link(dve.tensor_tensor(var[:, :], st[:, :, 2], st[:, :, 5], ALU.add))
                link(dve.scalar_tensor_tensor(var[:, :], tmp[:, :], C / 4.0, var[:, :], ALU.mult, ALU.add))
                link(dve.tensor_scalar(var[:, :], var[:, :], 1.0 / C, eps, ALU.mult, ALU.add))
                link(dve.tensor_scalar(mean[:, :], mean[:, :], 0.5, None, ALU.mult))
                rsqrt(dve, link, var[:, :], rstd[:, :], tmp[:, :], 3)
                for b in range(B):
                    dve.tensor_scalar(dst[:, b, :], X[:, b, :], mean[:, b:b + 1], rstd[:, b:b + 1],
                                      ALU.subtract, ALU.mult).then_inc(s_norm, 1)
                dve.wait_ge(s_norm, B)


def scan_layer(nc, io, sem, sbuf, X, XT, small, ident, ps, col, cols):
    ctx = ExitStack()
    with ctx:
        xin = sbuf(ctx, "xin", [P, CB, TOK], F32)
        wa = sbuf(ctx, "wa", [P, CB, 2 * C], F32)
        gate = sbuf(ctx, "gate", [P, 2, CB, W512], F32)
        val = sbuf(ctx, "val", [P, 2, CB, W512], F32)
        hid = sbuf(ctx, "hid", [P, 2, CB, W512], F32)
        d_x, d_w = [sem(f"a_dx{k}") for k in range(NTG)], sem("a_dw")
        s_id, s_mm, s_act, s_zero, s_scan, s_add = (sem("a_" + n) for n in
                                                    ("id", "mm", "act", "zero", "scan", "add"))
        with nc.Block() as block:
            @block.sync
            def _(sp):
                sp.dma_start(wa[:, :, :], io["wa"].rearrange("(k p) n -> p k n", p=P)).then_inc(d_w, 16)
                sp.dma_start(small[:, :], io["small"]).then_inc(d_w, 16)
                for tg in range(NTG):
                    sp.dma_start(xin[:, :, tg * W512:(tg + 1) * W512],
                                 io["xT"].rearrange("(k p) n -> p k n", p=P)[:, :, tg * W512:(tg + 1) * W512]
                                 ).then_inc(d_x[tg], 16)

            @block.tensor
            def _(pe):
                pe.wait_ge(d_w, 32)
                for tg in range(NTG):
                    pe.wait_ge(d_x[tg], 16)
                    if tg >= 2:
                        pe.wait_ge(s_act, 4 * (tg - 1))
                    for m in range(4):
                        for k in range(CB):
                            mm = pe.matmul(ps[(tg % 2) * 4 + m][:, :], wa[:, k, m * P:(m + 1) * P],
                                           xin[:, k, tg * W512:(tg + 1) * W512], start=(k == 0), stop=(k == CB - 1))
                        mm.then_inc(s_mm, 1)

            @block.scalar
            def _(act):
                for tg in range(NTG):
                    if tg >= 2:
                        act.wait_ge(s_scan, 2 * (tg - 1))
                    for m in range(4):
                        act.wait_ge(s_mm, 4 * tg + m + 1)
                        out = (gate if m < CB else val)[:, tg % 2, m % CB, :]
                        act.activation(out, ps[(tg % 2) * 4 + m][:, :], ACT.Sigmoid if m < CB else ACT.Tanh,
                                       bias=col("ab", m)).then_inc(s_act, 1)

            @block.gpsimd
            def _(pool):
                pool.memset(ident[:, :], 0.0).then_inc(s_id, 1)
                pool.wait_ge(s_id, 1)
                pool.affine_select(out=ident[:, :], in_=ident[:, :], compare_op=ALU.not_equal, fill=1.0,
                                   base=0, pattern=[[-1, P]], channel_multiplier=1).then_inc(s_id, 1)
                pool.wait_ge(s_id, 2)
                for tg in range(NTG):
                    pool.wait_ge(s_act, 4 * tg + CB)
                    g = gate[:, tg % 2, :, :].rearrange("p k (b s) -> p k b s", s=S)
                    pool.memset(g[:, :, :, 0], 0.0).then_inc(s_zero, 1)
                    pool.wait_ge(s_scan, 2 * (tg + 1))
                    pool.tensor_tensor(XT[:, :, tg * W512:(tg + 1) * W512], hid[:, tg % 2, :, :],
                                       xin[:, :, tg * W512:(tg + 1) * W512], ALU.add).then_inc(s_add, 1)
                pool.wait_ge(s_add, NTG)

            @block.vector
            def _(dve):
                for tg in range(NTG):
                    dve.wait_ge(s_zero, tg + 1)
                    dve.wait_ge(s_act, 4 * tg + 4)
                    if tg >= 2:
                        dve.wait_ge(s_add, tg - 1)
                    for k in range(CB):
                        dve.tensor_tensor_scan(hid[:, tg % 2, k, :], gate[:, tg % 2, k, :], val[:, tg % 2, k, :],
                                               0.0, ALU.mult, ALU.add).then_inc(s_scan, 1)


def conv_layer(nc, io, sem, sbuf, X, XT, small, ident, ps, col, cols):
    ctx = ExitStack()
    with ctx:
        ct = sbuf(ctx, "ct", [P, CB, TOK], F32)
        res = sbuf(ctx, "res", [P, CB, TOK], F32)
        tz = sbuf(ctx, "tz", [P, 2, C], F32)
        rev = sbuf(ctx, "rev", [P, P], F32)
        kv = sbuf(ctx, "kv", [P, 2, CB, W512], F32)
        prod = sbuf(ctx, "prod", [P, CB, W512], F32)
        d_c, d_t = sem("b_dc"), [sem("b_dt0"), sem("b_dt1")]
        s_rev, s_tz, s_kv, s_mm, s_prod, s_red, s_add = (sem("b_" + n) for n in
                                                        ("rev", "tz", "kv", "mm", "prod", "red", "add"))
        HB = B // 2
        ct_v = ct[:, :, :].rearrange("p k (b t) -> p k b t", t=S)
        xt_v = XT[:, :, :].rearrange("p k (b t) -> p k b t", t=S)
        res_v = res[:, :, :].rearrange("p k (b t) -> p k b t", t=S)

        def head(u):
            return u.b * 2 + u.g // 2

        with nc.Block() as block:
            @block.sync
            def _(sp):
                sp.dma_start(ct[:, :, :], io["ctxR"].rearrange("k p n -> p k n")).then_inc(d_c, 16)

                def load(u):
                    if u.g % 2 == 0:
                        if u.before(4):
                            sp.wait_ge(s_mm, u.n - 2)
                        sp.dma_start(tz[:, u.g // 2, :], io["toep"][bass.ds(head(u), 1), :, :].rearrange(
                            "a p n -> (a p) n")).then_inc(d_t[u.g // 2], 16)
                skewed(sp, CH // 2, 4, [(load, 0)])

            @block.gpsimd
            def _(pool):
                pool.memset(rev[:, :], 0.0).then_inc(s_rev, 1)
                pool.wait_ge(s_rev, 1)
                pool.affine_select(out=rev[:, :], in_=rev[:, :], compare_op=ALU.not_equal, fill=1.0,
                                   base=-(P - 1), pattern=[[1, P]], channel_multiplier=1).then_inc(s_rev, 1)
                pool.wait_ge(d_c, 16)

                def products(u):
                    if u.before(2):
                        pool.wait_ge(s_mm, u.n - 1)
                    half = (u.g % 2) * HB
                    for k in range(CB):
                        c = ct_v[:, k, half:half + HB, bass.ds(head(u) * CD, CD)]
                        ins = pool.tensor_tensor(kv[:, u.g % 2, k, :].rearrange("p (b j i) -> p b j i", j=CD, i=CD),
                                                 c.unsqueeze(3).to_broadcast([P, HB, CD, CD]),
                                                 c.unsqueeze(2).to_broadcast([P, HB, CD, CD]), ALU.mult)
                    ins.then_inc(s_kv, 1)
                skewed(pool, CH // 2, 4, [(products, 0)])

            @block.tensor
            def _(pe):
                def conv(u):
                    pe.wait_ge(s_kv, u.n + 1)
                    if u.g % 2 == 0:
                        pe.wait_ge(s_tz, head(u) + 1)
                    if u.before(2):
                        pe.wait_ge(s_prod, u.n - 1)
                    t, lo, hi = tz[:, u.g // 2, :], ps[(u.g % 2) * 2], ps[(u.g % 2) * 2 + 1]
                    pe.matmul(lo[:, :], t[:, 0:P], kv[:, u.g % 2, 0, :], start=True, stop=True)
                    pe.matmul(hi[:, :], t[:, P:C], kv[:, u.g % 2, 0, :], start=True, stop=False)
                    pe.matmul(hi[:, :], t[:, 0:P], kv[:, u.g % 2, 1, :], start=False, stop=True).then_inc(s_mm, 1)
                skewed(pe, CH // 2, 4, [(conv, 0)])

            @block.vector
            def _(dve):
                dve.wait_ge(s_rev, 2)

                def diagonal(u):
                    if u.g % 2 == 0:
                        dve.wait_ge(d_t[u.g // 2], u.b * 16 + 16)
                        t = tz[:, u.g // 2, 0:P]
                        d = cols("dskip")[:, bass.ds(head(u), 1)]
                        dve.scalar_tensor_tensor(t, rev[:, :], d, t, ALU.mult, ALU.add).then_inc(s_tz, 1)

                def queries(u):
                    dve.wait_ge(s_mm, u.n + 1)
                    half = (u.g % 2) * HB
                    if u.before(1):
                        dve.wait_ge(s_red, u.n)
                    for k in range(CB):
                        q = xt_v[:, k, half:half + HB, bass.ds(head(u) * CD, CD)]
                        ins = dve.tensor_tensor(prod[:, k, :].rearrange("p (b j i) -> p b j i", j=CD, i=CD),
                                                ps[(u.g % 2) * 2 + k][:, :].rearrange("p (b j i) -> p b j i", j=CD, i=CD),
                                                q.unsqueeze(2).to_broadcast([P, HB, CD, CD]), ALU.mult)
                    ins.then_inc(s_prod, 1)
                    dve.wait_ge(s_prod, u.n + 1)
                    for k in range(CB):
                        o = res_v[:, k, half:half + HB, bass.ds(head(u) * CD, CD)]
                        ins = dve.tensor_reduce(o, prod[:, k, :].rearrange("p (b j i) -> p b j i", j=CD, i=CD),
                                                AX.X, ALU.add)
                    ins.then_inc(s_red, 1)
                skewed(dve, CH // 2, 4, [(diagonal, 0), (queries, 1)])
                dve.wait_ge(s_red, 2 * CH)
                dve.tensor_tensor(XT[:, :, :], XT[:, :, :], res[:, :, :], ALU.add).then_inc(s_add, 1)
                dve.wait_ge(s_add, 1)


def routed_layer(nc, io, sem, sbuf, X, XT, small, ident, ps, col, cols):
    ctx = ExitStack()
    with ctx:
        wf = sbuf(ctx, "wf", [P, CB, FW], F32)
        deb = sbuf(ctx, "deb", [P, CB, NE0], F32)
        lw = sbuf(ctx, "lw", [SEL + NE0, C], F32)
        pr = sbuf(ctx, "pr", [P, CB, FW], F32)
        cst = sbuf(ctx, "cst", [P, FW], F32)
        ones = sbuf(ctx, "c_ones", [P, P], F32)
        prio = sbuf(ctx, "prio", [P, NE0], F32)
        u_ = sbuf(ctx, "u_", [P, B, SEL + UPD], F32)
        xm = sbuf(ctx, "xm", [P, B, NE0], F32)
        sq = sbuf(ctx, "sq_", [P, B, C], F32)
        xx = sbuf(ctx, "xx", [P, B], F32)
        sc = sbuf(ctx, "sc", [P, B, NE0], F32)
        gt = sbuf(ctx, "gt", [P, B, NE0], F32)
        eq = sbuf(ctx, "eq", [P, B, NE0], F32)
        mx = sbuf(ctx, "mx", [P, B], F32)
        pm = sbuf(ctx, "pm", [P, B], F32)
        keep = sbuf(ctx, "keep", [P, B], F32)
        mk = sbuf(ctx, "mk", [P, B, UPD + NE0], F32)
        mkt = sbuf(ctx, "mkt", [UPD + NE0, B, P], F32)
        d_w = sem("c_dw")
        s_one, s_pr, s_cm, s_cst, s_mm, s_u, s_z, s_ex, s_mk, s_t, s_te, s_o, s_x, s_link = (
            sem("c_" + n) for n in ("one", "pr", "cm", "cst", "mm", "u", "z", "ex", "mk", "t", "te", "o", "x", "link"))

        def over(a, n):
            return a.unsqueeze(2).to_broadcast([P, B, n])

        with nc.Block() as block:
            @block.sync
            def _(sp):
                sp.dma_start(wf[:, :, :], io["wf"].rearrange("(k p) n -> p k n", p=P)).then_inc(d_w, 16)
                sp.dma_start(deb[:, :, :], io["deb"].rearrange("(k p) n -> p k n", p=P)).then_inc(d_w, 16)
                sp.dma_start(lw[:, :], io["lw"]).then_inc(d_w, 16)

            @block.gpsimd
            def _(pool):
                pool.memset(ones[:, :], 1.0)
                for n in range(NE0):
                    ins = pool.memset(prio[:, n:n + 1], float(NE0 - n))
                ins.then_inc(s_one, 1)

            @block.tensor
            def _(pe):
                pe.wait_ge(d_w, 48)
                pe.wait_ge(s_one, 1)
                pe.wait_ge(s_pr, 3)
                for k in range(CB):
                    mm = pe.matmul(ps[0][:, 0:FW], ones[:, :], pr[:, k, :], start=(k == 0), stop=(k == CB - 1))
                mm.then_inc(s_cm, 1)
                pe.wait_ge(s_cst, 1)
                for b in range(B):
                    for k in range(CB):
                        mm = pe.matmul(ps[b // 2][:, (b % 2) * C:(b % 2) * C + FW], XT[:, k, b * S:(b + 1) * S],
                                       wf[:, k, :], start=(k == 0), stop=(k == CB - 1))
                mm.then_inc(s_mm, 1)
                pe.wait_ge(s_mk, 1)
                for q in range(B // 4):
                    for j in range(4):
                        mm = pe.transpose(ps[q][0:UPD + NE0, j * P:(j + 1) * P], mk[:, 4 * q + j, :], ident[:, :])
                    mm.then_inc(s_t, 1)
                for b in range(B):
                    pe.wait_ge(s_te, b // 4 + 1)
                    if b >= 8 and b % 2 == 0:
                        pe.wait_ge(s_x, b - 6)
                    mm = pe.matmul(ps[4 + (b // 2) % 4][:, (b % 2) * C:(b % 2 + 1) * C], mkt[:, b, :], lw[:, :],
                                   start=True, stop=True)
                    if b % 2:
                        mm.then_inc(s_o, 1)

            @block.scalar
            def _(act):
                act.wait_ge(s_z, 1)
                act.activation(gt[:, :, :], sc[:, :, :], ACT.Exp, scale=-1.0).then_inc(s_ex, 1)
                for q in range(B // 4):
                    act.wait_ge(s_t, q + 1)
                    act.activation(mkt[:, 4 * q:4 * q + 4, :],
                                   ps[q][0:UPD + NE0, :].rearrange("p (b s) -> p b s", b=4), ACT.Copy).then_inc(s_te, 1)

            @block.vector
            def _(dve):
                link = Links(dve, s_link)
                dve.wait_ge(d_w, 48)
                m = wf[:, :, SEL + UPD:FW]

                def pairs(a):
                    return a.rearrange("p k (n s) -> p k n s", s=NS0)

                dve.tensor_tensor(pairs(pr[:, :, 0:SEL]), pairs(wf[:, :, 0:SEL]),
                                  m.unsqueeze(3).to_broadcast([P, CB, NE0, NS0]), ALU.mult).then_inc(s_pr, 1)
                dve.tensor_tensor(pairs(pr[:, :, SEL:SEL + UPD]), pairs(wf[:, :, SEL:SEL + UPD]),
                                  deb[:, :, :].unsqueeze(3).to_broadcast([P, CB, NE0, NS0]), ALU.mult).then_inc(s_pr, 1)
                dve.tensor_tensor(pr[:, :, SEL + UPD:FW], m, m, ALU.mult).then_inc(s_pr, 1)
                dve.wait_ge(s_cm, 1)
                dve.tensor_copy(cst[:, :], ps[0][:, 0:FW]).then_inc(s_cst, 1)
                link(dve.tensor_tensor(sq[:, :, :], X[:, :, :], X[:, :, :], ALU.mult))
                link(dve.tensor_reduce(xx[:, :], sq[:, :, :], AX.X, ALU.add))
                dve.wait_ge(s_cst, 1)
                dve.wait_ge(s_one, 1)
                dve.wait_ge(s_mm, 1)
                for q in range(B // 2):
                    bank = ps[q][:, :].rearrange("p (b c) -> p b c", b=2)
                    dve.tensor_tensor(u_[:, 2 * q:2 * q + 2, :], bank[:, :, 0:SEL + UPD],
                                      cst[:, 0:SEL + UPD].unsqueeze(1).to_broadcast([P, 2, SEL + UPD]), ALU.subtract)
                    ins = dve.tensor_copy(xm[:, 2 * q:2 * q + 2, :], bank[:, :, SEL + UPD:FW])
                link(ins)
                s2 = sq[:, :, 0:SEL]
                link(dve.tensor_tensor(s2, u_[:, :, 0:SEL], u_[:, :, 0:SEL], ALU.mult))
                link(dve.tensor_reduce(sc[:, :, :], s2.rearrange("p b (n s) -> p b n s", s=NS0), AX.X, ALU.add))
                mm_ = cst[:, SEL + UPD:FW].unsqueeze(1).to_broadcast([P, B, NE0])
                link(dve.scalar_tensor_tensor(xm[:, :, :], xm[:, :, :], -2.0, mm_, ALU.mult, ALU.add))
                link(dve.tensor_tensor(xm[:, :, :], xm[:, :, :], over(xx[:, :], NE0), ALU.add))
                link(dve.reciprocal(xm[:, :, :], xm[:, :, :]))
                link(dve.tensor_tensor(sc[:, :, :], sc[:, :, :], xm[:, :, :], ALU.mult))
                link(dve.tensor_tensor(sc[:, :, :], sc[:, :, :],
                                       cols("center").unsqueeze(1).to_broadcast([P, B, NE0]), ALU.subtract))
                link(dve.tensor_tensor(sc[:, :, :], sc[:, :, :],
                                       cols("slope").unsqueeze(1).to_broadcast([P, B, NE0]), ALU.mult))
                dve.tensor_scalar(sc[:, :, :], sc[:, :, :], -87.0, None, ALU.max).then_inc(s_z, 1)
                dve.wait_ge(s_ex, 1)
                link(dve.tensor_scalar(gt[:, :, :], gt[:, :, :], 1.0, None, ALU.add))
                link(dve.reciprocal(gt[:, :, :], gt[:, :, :]))
                link(dve.tensor_reduce(mx[:, :], gt[:, :, :], AX.X, ALU.max))
                link(dve.tensor_tensor(eq[:, :, :], gt[:, :, :], over(mx[:, :], NE0), ALU.is_ge))
                link(dve.tensor_tensor(eq[:, :, :], eq[:, :, :],
                                       prio[:, :].unsqueeze(1).to_broadcast([P, B, NE0]), ALU.mult))
                link(dve.tensor_reduce(pm[:, :], eq[:, :, :], AX.X, ALU.max))
                link(dve.tensor_tensor(eq[:, :, :], eq[:, :, :], over(pm[:, :], NE0), ALU.is_equal))
                link(dve.tensor_scalar(keep[:, :], mx[:, :], -1.0, 2.0, ALU.mult, ALU.add))
                link(dve.tensor_tensor(mk[:, :, UPD:UPD + NE0], eq[:, :, :], over(mx[:, :], NE0), ALU.mult))
                for h in range(2):
                    bs = slice(h * 8, h * 8 + 8)
                    ins = dve.tensor_tensor(mk[:, bs, 0:UPD].rearrange("p b (n s) -> p b n s", s=NS0),
                                            u_[:, bs, SEL:SEL + UPD].rearrange("p b (n s) -> p b n s", s=NS0),
                                            mk[:, bs, UPD:UPD + NE0].unsqueeze(3).to_broadcast([P, 8, NE0, NS0]), ALU.mult)
                ins.then_inc(s_mk, 1)
                for b in range(B):
                    dve.wait_ge(s_o, b // 2 + 1)
                    dve.scalar_tensor_tensor(X[:, b, :], X[:, b, :], keep[:, b:b + 1],
                                             ps[4 + (b // 2) % 4][:, (b % 2) * C:(b % 2 + 1) * C],
                                             ALU.mult, ALU.add).then_inc(s_x, 1)
                dve.wait_ge(s_x, B)


def causal_layer(nc, io, sem, sbuf, X, XT, small, ident, ps, col, cols):
    ctx = ExitStack()
    with ctx:
        QB = HQ // HKV
        PAD = P // HKV
        wq = sbuf(ctx, "d_wq", [P, CB, QB * P], F32)
        wk = sbuf(ctx, "d_wk", [P, CB, P], F32)
        wv = sbuf(ctx, "d_wv", [P, CB, HKV * HD], F32)
        wo = sbuf(ctx, "d_wo", [P, CB, C], F32)
        identb = sbuf(ctx, "identb", [P, P], BF16)
        mask = sbuf(ctx, "mask", [P, HKV, P], BF16)
        xs = sbuf(ctx, "xs", [P, 2, CB, S], F32)
        qt = sbuf(ctx, "qt_", [P, 2, QB * P], F32)
        kd = sbuf(ctx, "kd", [P, 2, HKV, P], F32)
        v = sbuf(ctx, "d_v", [P, 2, HKV, HD + 1], F32)
        neg = sbuf(ctx, "neg", [P, 2, HKV], F32)
        sb_ = sbuf(ctx, "sb_", [P, 2, HKV, P], F32)
        pt = sbuf(ctx, "pt_", [P, 2, HKV, P], F32)
        rec = sbuf(ctx, "rec", [P, QB, HKV], F32)
        cx = sbuf(ctx, "cx", [P, C], F32)
        cxt = sbuf(ctx, "cxt", [P, CB, P], F32)
        d_w = sem("d_dw")
        (s_cst, s_xs, s_mm, s_q, s_k, s_s, s_mx, s_sub, s_ex, s_tp, s_cp, s_c, s_rc, s_cn, s_ct, s_cc, s_o, s_x) = (
            sem("d_" + n) for n in ("cst", "xs", "mm", "q", "k", "s", "mx", "sub", "ex", "tp", "cp", "c", "rc", "cn",
                                    "ct", "cc", "o", "x"))
        bQ, bK, bS, bT, bC, bF = ps[0], ps[1], ps[2:4], ps[4:6], ps[6], ps[7]
        PER = 2 * QB

        def batch(u):
            return u.b * 2 + u.g // QB

        with nc.Block() as block:
            @block.sync
            def _(sp):
                sp.dma_start(wq[:, :, :], io["d_wq"].rearrange("(k p) n -> p k n", p=P)).then_inc(d_w, 16)
                sp.dma_start(wk[:, :, :], io["d_wk"].rearrange("(k p) n -> p k n", p=P)).then_inc(d_w, 16)
                sp.dma_start(wv[:, :, :], io["d_wv"].rearrange("(k p) n -> p k n", p=P)).then_inc(d_w, 16)
                sp.dma_start(wo[:, :, :], io["d_wo"].rearrange("(k p) n -> p k n", p=P)).then_inc(d_w, 16)

            @block.gpsimd
            def _(pool):
                pool.memset(mask[:, :, :], 0.0).then_inc(s_cst, 1)
                pool.memset(identb[:, :], 0.0).then_inc(s_cst, 1)
                pool.memset(kd[:, :, :, :], 0.0).then_inc(s_cst, 1)
                pool.memset(v[:, :, :, :], 1.0).then_inc(s_cst, 1)
                pool.wait_ge(s_cst, 4)
                pool.affine_select(out=mask[:, :, :], in_=mask[:, :, :], compare_op=ALU.is_ge, fill=-1e30,
                                   base=0, pattern=[[0, HKV], [-1, P]], channel_multiplier=1).then_inc(s_cst, 1)
                pool.affine_select(out=identb[:, :], in_=identb[:, :], compare_op=ALU.not_equal, fill=1.0,
                                   base=0, pattern=[[-1, P]], channel_multiplier=1).then_inc(s_cst, 1)

            @block.tensor
            def _(pe):
                pe.wait_ge(d_w, 64)
                pe.wait_ge(s_cst, 6)

                def project(u):
                    if u.g % QB:
                        return
                    b, par = batch(u), u.g // QB
                    pe.wait_ge(s_xs, b + 1)
                    if u.before(QB):
                        pe.wait_ge(s_q, b)
                        pe.wait_ge(s_k, b)
                    for t in range(QB):
                        for k in range(CB):
                            pe.matmul(bQ[:, t * P:(t + 1) * P], wq[:, k, t * P:(t + 1) * P], xs[:, par, k, :],
                                      start=(k == 0), stop=(k == CB - 1))
                    for k in range(CB):
                        pe.matmul(bK[:, 0:P], wk[:, k, :], xs[:, par, k, :], start=(k == 0), stop=(k == CB - 1))
                    for k in range(CB):
                        mm = pe.matmul(bK[:, P:P + HKV * HD], xs[:, par, k, :], wv[:, k, :],
                                       start=(k == 0), stop=(k == CB - 1))
                    mm.then_inc(s_mm, 1)

                def scores(u):
                    t, par = u.g % QB, u.g // QB
                    pe.wait_ge(s_q, batch(u) + 1)
                    pe.wait_ge(s_k, batch(u) + 1)
                    if u.before(2):
                        pe.wait_ge(s_sub, u.n - 1)
                    pe.matmul(bS[u.g % 2][:, :], qt[:, par, t * P:(t + 1) * P],
                              kd[:, par, :, :].rearrange("p h k -> p (h k)"), start=True, stop=False)
                    pe.matmul(bS[u.g % 2][:, :], identb[:, :], mask[:, :, :].rearrange("p h k -> p (h k)"),
                              start=False, stop=True).then_inc(s_s, 1)

                def turn(u):
                    pe.wait_ge(s_ex, u.n + 1)
                    if u.before(2):
                        pe.wait_ge(s_cp, u.n - 1)
                    for h in range(HKV):
                        mm = pe.transpose(bT[u.g % 2][:, h * P:(h + 1) * P], sb_[:, u.g % 2, h, :], ident[:, :])
                    mm.then_inc(s_tp, 1)

                def context(u):
                    t, par = u.g % QB, u.g // QB
                    pe.wait_ge(s_cp, u.n + 1)
                    if t == 0 and u.before(QB):
                        pe.wait_ge(s_cn, batch(u))
                    for h in range(HKV):
                        at = (t * HKV + h) * (HD + 1)
                        mm = pe.matmul(bC[:, at:at + HD + 1], pt[:, u.g % 2, h, :], v[:, par, h, :],
                                       start=True, stop=True)
                    mm.then_inc(s_c, 1)

                def out(u):
                    if u.g % QB != QB - 1:
                        return
                    b = batch(u)
                    pe.wait_ge(s_cn, b + 1)
                    if u.before(QB):
                        pe.wait_ge(s_x, b)
                    for k in range(CB):
                        mm = pe.transpose(bF[:, k * P:(k + 1) * P], cx[:, k * P:(k + 1) * P], ident[:, :])
                    mm.then_inc(s_ct, 1)
                    pe.wait_ge(s_cc, b + 1)
                    for k in range(CB):
                        mm = pe.matmul(bF[:, C:2 * C], cxt[:, k, :], wo[:, k, :], start=(k == 0), stop=(k == CB - 1))
                    mm.then_inc(s_o, 1)
                skewed(pe, B // 2, PER, [(project, 0), (scores, 1), (context, 3), (turn, 2), (out, 4)])

            @block.scalar
            def _(act):
                def columns(u):
                    if u.g % QB:
                        return
                    b, par = batch(u), u.g // QB
                    if u.before(2 * QB):
                        act.wait_ge(s_mm, b - 1)
                    act.activation(xs[:, par, :, :], XT[:, :, bass.ds(b * S, S)], ACT.Copy).then_inc(s_xs, 1)

                def queries(u):
                    if u.g % QB:
                        return
                    b, par = batch(u), u.g // QB
                    act.wait_ge(s_mm, b + 1)
                    if u.before(2 * QB):
                        act.wait_ge(s_s, u.n - QB)
                    act.activation(qt[:, par, :], bQ[:, :], ACT.Copy).then_inc(s_q, 1)

                def exps(u):
                    act.wait_ge(s_sub, u.n + 1)
                    act.activation(sb_[:, u.g % 2, :, :], sb_[:, u.g % 2, :, :], ACT.Exp,
                                   scale=float(HD) ** -0.5).then_inc(s_ex, 1)

                def turned(u):
                    act.wait_ge(s_tp, u.n + 1)
                    if u.before(2):
                        act.wait_ge(s_c, u.n - 1)
                    act.activation(pt[:, u.g % 2, :, :], bT[u.g % 2][:, :].rearrange("p (h k) -> p h k", h=HKV),
                                   ACT.Copy).then_inc(s_cp, 1)

                def context(u):
                    if u.g % QB != QB - 1:
                        return
                    act.wait_ge(s_ct, batch(u) + 1)
                    if u.before(QB):
                        act.wait_ge(s_o, batch(u))
                    act.activation(cxt[:, :, :], bF[:, 0:C].rearrange("p (k s) -> p k s", k=CB),
                                   ACT.Copy).then_inc(s_cc, 1)
                skewed(act, B // 2, PER, [(columns, 0), (queries, 0), (exps, 1), (turned, 2), (context, 4)])

            @block.vector
            def _(dve):
                dve.wait_ge(s_cst, 4)

                def keys(u):
                    if u.g % QB:
                        return
                    b, par = batch(u), u.g // QB
                    dve.wait_ge(s_mm, b + 1)
                    if u.before(2 * QB):
                        dve.wait_ge(s_c, u.n - QB)
                    for h in range(HKV):
                        rows = slice(h * PAD, (h + 1) * PAD)
                        dve.tensor_copy(kd[rows, par, h, :], bK[rows, 0:P])
                    dve.tensor_copy(v[:, par, :, 0:HD],
                                    bK[:, P:P + HKV * HD].rearrange("p (h d) -> p h d", h=HKV)).then_inc(s_k, 1)

                def maxima(u):
                    dve.wait_ge(s_s, u.n + 1)
                    bank = bS[u.g % 2][:, :].rearrange("p (h k) -> p h k", h=HKV)
                    dve.tensor_reduce(neg[:, u.g % 2, :], bank, AX.X, ALU.max).then_inc(s_mx, 1)
                    dve.wait_ge(s_mx, u.n + 1)
                    if u.before(2):
                        dve.wait_ge(s_tp, u.n - 1)
                    dve.tensor_tensor(sb_[:, u.g % 2, :, :], bank,
                                      neg[:, u.g % 2, :].unsqueeze(2).to_broadcast([P, HKV, P]),
                                      ALU.subtract).then_inc(s_sub, 1)

                def normal(u):
                    if u.g % QB != QB - 1:
                        return
                    b = batch(u)
                    dve.wait_ge(s_c, u.n + 1)
                    c = bC[:, 0:HQ * (HD + 1)].rearrange("p (t h d) -> p t h d", t=QB, h=HKV)
                    dve.reciprocal(rec[:, :, :], c[:, :, :, HD]).then_inc(s_rc, 1)
                    dve.wait_ge(s_rc, b + 1)
                    if u.before(QB):
                        dve.wait_ge(s_ct, b)
                    dve.tensor_tensor(cx[:, :].rearrange("p (h t d) -> p t h d", h=HKV, t=QB), c[:, :, :, 0:HD],
                                      rec[:, :, :].unsqueeze(3).to_broadcast([P, QB, HKV, HD]),
                                      ALU.mult).then_inc(s_cn, 1)

                def residual(u):
                    if u.g % QB != QB - 1:
                        return
                    b = batch(u)
                    dve.wait_ge(s_o, b + 1)
                    x = X[:, bass.ds(b, 1), :].rearrange("p a c -> p (a c)")
                    dve.tensor_tensor(x, x, bF[:, C:2 * C], ALU.add).then_inc(s_x, 1)
                skewed(dve, B // 2, PER, [(keys, 0), (maxima, 1), (normal, 3), (residual, 4)])
                dve.wait_ge(s_x, B)


def quantise(dve, link, src, inv, y, p2, t, m, n):
    link(dve.tensor_scalar(y, src, inv, FP8_MAX, ALU.mult, ALU.min))
    link(dve.tensor_scalar(y, y, -FP8_MAX, None, ALU.max))
    link(dve.tensor_scalar(p2.bitcast(U16), y.bitcast(U16), 0x7F80, None, ALU.bitwise_and))
    link(dve.tensor_scalar(m, p2, FP8_MIN_NORMAL, ROUND, ALU.max, ALU.mult))
    return dve.tensor_tensor(t, y, m, ALU.add)


def quant_layer(nc, io, sem, sbuf, **args):
    args = dict(nc=nc, io=io, sem=sem, sbuf=sbuf, **args)
    XT, cols, col = args["XT"], args["cols"], args["col"]
    ctx = ExitStack()
    with ctx:
        xq = sbuf(ctx, "xq", [P, 4, CB, TOK], BF16)
        fold = sbuf(ctx, "fold", [P, 4, CB], F32)
        inv = sbuf(ctx, "inv", [P, 4, CB], F32)
        invsm = sbuf(ctx, "invsm", [P, 4 * G], F32)
        aff = sbuf(ctx, "aff", [P, 2, 4], F32)
        pscale = sbuf(ctx, "pscale", [P, 1], F32)
        s_t, s_z, s_link = sem("e_t"), sem("e_z"), sem("e_link")
        with ExitStack() as inner:
            lnx = sbuf(inner, "lnx", [P, B, C], F32)
            norm_layer("ln", dst=lnx, **args)
        with ExitStack() as inner:
            y = sbuf(inner, "y0", [P, 2, TOK], BF16)
            p2 = sbuf(inner, "p20", [P, 2, TOK], BF16)
            m = sbuf(inner, "m0", [P, 2, TOK], BF16)
            t = sbuf(inner, "t0", [P, 2, TOK], F32)
            with nc.Block() as block:
                @block.vector
                def _(dve):
                    link = Links(dve, s_link)
                    for j, (si, sw) in enumerate((("sq", "wsq"), ("sk", "wsk"), ("sv", "wsv"), ("sqx", "wsqx"))):
                        dve.tensor_scalar(fold[:, j, :], cols(si), col(sw), None, ALU.mult)
                        dve.reciprocal(inv[:, j, :], cols(si))
                    dve.reciprocal(invsm[:, :], cols("smooth"))
                    dve.tensor_scalar(pscale[:, :], col("pin"), col("pw"), None, ALU.mult)
                    for h, names in enumerate((("qw", "qb", "kw", "kb"), ("qxw", "qxb", "kxw", "kxb"))):
                        for j, name in enumerate(names):
                            k = (float(D) ** -0.5 if j < 2 else 1.0) * (1.0 if j % 2 else float(D) ** 0.5)
                            dve.tensor_scalar(aff[:, h, j:j + 1], col(name), k, None, ALU.mult)
                    for k in range(CB):
                        ins = dve.tensor_scalar(XT[:, k, :], XT[:, k, :], col("lnw", k), col("lnb", k),
                                                ALU.mult, ALU.add)
                    link(ins)
                    for j in range(4):
                        for k in range(CB):
                            n = j * CB + k
                            if n >= 2:
                                dve.wait_ge(s_z, n - 1)
                            quantise(dve, link, XT[:, k, :], inv[:, j, k:k + 1], y[:, n % 2, :], p2[:, n % 2, :],
                                     t[:, n % 2, :], m[:, n % 2, :], n).then_inc(s_t, 1)

                @block.gpsimd
                def _(pool):
                    for n in range(4 * CB):
                        pool.wait_ge(s_t, n + 1)
                        pool.tensor_tensor(xq[:, n // CB, n % CB, :], t[:, n % 2, :], m[:, n % 2, :],
                                           ALU.subtract).then_inc(s_z, 1)
                    pool.wait_ge(s_z, 4 * CB)
        for cross in (False, True):
            attention_pass(cross, xq, fold, invsm, aff, pscale, **args)


def attention_pass(cross, xq, fold, invsm, aff, pscale, nc, io, sem, sbuf, X, XT, small, ident, ps, col, cols):
    tag = "cross_" if cross else "self_"
    ctx = ExitStack()
    NQ = 1 if cross else 3
    QW = 2 * D
    W = QW if cross else UW
    HC = 2 if cross else 3
    with ctx:
        whi = sbuf(ctx, tag + "whi", [P, G, CB, W], F32R)
        wlo = sbuf(ctx, tag + "wlo", [P, G, CB, W], F32R)
        phi = sbuf(ctx, tag + "phi", [P, 2 * G, C], F32R)
        plo = sbuf(ctx, tag + "plo", [P, 2 * G, C], F32R)
        if cross:
            wkv = sbuf(ctx, "wkv", [P, G, CB, QW], F32)
            ct = sbuf(ctx, "xct", [P, CB, TOK], F32)
            cs = sbuf(ctx, "cs", [P, 2, CB, S], F32)
        WQ = sem(tag + "_wq")
        d_w, d_p = [sem(f"{tag}_dw{i}") for i in range(2)], [sem(f"{tag}_dp{i}") for i in range(2)]
        d_c = sem(tag + "_dc")
        s_ctr, s_hi, s_lo, s_phi, s_plo, s_link, s_kv = (sem(f"{tag}_{n}") for n in
                                                         ("ctr", "hi", "lo", "phi", "plo", "link", "kv"))
        with ExitStack() as inner:
            st = sbuf(inner, tag + "st", [P, 2, CB, W], F32)
            pst = sbuf(inner, tag + "pst", [P, 2, 4, C], F32)
            mean = sbuf(inner, tag + "mean", [P, 2, CB, 3], F32)
            with nc.Block() as block:
                @block.sync
                def _(sp):
                    if cross:
                        sp.dma_start(wkv[:, :, :, :], io["wkvx"].rearrange("g (k p) n -> p g k n", p=P)).then_inc(d_c, 16)
                    for g in range(G):
                        if g >= 2:
                            sp.wait_ge(s_lo, g - 1)
                        sp.dma_start(st[:, g % 2, :, :], io["wqx" if cross else "wself"][g, :, :].rearrange(
                            "(k p) n -> p k n", p=P)).then_inc(d_w[g % 2], 16)
                        if g % 2:
                            c = g // 2
                            if c >= 2:
                                sp.wait_ge(s_plo, c - 1)
                            sp.dma_start(pst[:, c % 2, :, :], io["wproj"][int(cross), 4 * c:4 * c + 4, :, :].rearrange(
                                "h p n -> p h n")).then_inc(d_p[c % 2], 16)
                    if cross:
                        sp.dma_start(ct[:, :, :], io["ctxT"].rearrange("(k p) n -> p k n", p=P)).then_inc(d_c, 16)

                @block.vector
                def _(dve):
                    link = Links(dve, s_link)

                    def centre(w, mean_, heads):
                        hd = w.rearrange("p k (h d) -> p k h d", d=D)
                        link(dve.tensor_reduce(mean_, hd, AX.X, ALU.add))
                        link(dve.tensor_scalar(mean_, mean_, -1.0 / D, None, ALU.mult))
                        return dve.tensor_tensor(hd, hd, mean_.unsqueeze(3).to_broadcast([P, CB, heads, D]), ALU.add)

                    for g in range(G):
                        dve.wait_ge(d_w[g % 2], 16 * (g // 2) + 16)
                        w = st[:, g % 2, :, :]
                        for k in range(CB):
                            parts = ((0, QW, 3),) if cross else ((0, QW, 0), (QW, QW + D, 1), (QW + D, UW, 2))
                            for a, z, j in parts:
                                ins = dve.tensor_scalar(w[:, k, a:z], w[:, k, a:z], fold[:, j, k:k + 1], None, ALU.mult)
                        link(ins)
                        centre(w[:, :, 0:HC * D], mean[:, g % 2, :, 0:HC], HC).then_inc(s_ctr, 1)
                    if cross:
                        dve.wait_ge(d_c, 16)
                        for g in range(G):
                            link(centre(wkv[:, g, :, 0:D], mean[:, g % 2, :, 0:1], 1))

                @block.scalar
                def _(act):
                    for g in range(G):
                        act.wait_ge(s_ctr, g + 1)
                        act.activation(whi[:, g, :, :], st[:, g % 2, :, :], ACT.Copy).then_inc(s_hi, 1)
                        if g % 2:
                            c = g // 2
                            act.wait_ge(d_p[c % 2], 16 * (c // 2) + 16)
                            act.activation(phi[:, 4 * c:4 * c + 4, :], pst[:, c % 2, :, :], ACT.Copy).then_inc(s_phi, 1)

                @block.gpsimd
                def _(pool):
                    for g in range(G):
                        pool.wait_ge(s_hi, g + 1)
                        pool.tensor_tensor(wlo[:, g, :, :], st[:, g % 2, :, :], whi[:, g, :, :].bitcast(F32),
                                           ALU.subtract).then_inc(s_lo, 1)
                        if g % 2:
                            c = g // 2
                            pool.wait_ge(s_phi, c + 1)
                            pool.tensor_tensor(plo[:, 4 * c:4 * c + 4, :], pst[:, c % 2, :, :],
                                               phi[:, 4 * c:4 * c + 4, :].bitcast(F32), ALU.subtract).then_inc(s_plo, 1)
        xs = sbuf(ctx, tag + "xs", [P, 2, NQ, CB, S], F32R)
        stat = sbuf(ctx, tag + "stat", [P, 2, 12], F32)
        var = sbuf(ctx, tag + "var", [P, 2, 3], F32)
        half = sbuf(ctx, tag + "half", [P, 3], F32)
        deps = sbuf(ctx, tag + "deps", [P, 3], F32)
        rstd = sbuf(ctx, tag + "rstd", [P, 2, 4], F32)
        qkv = sbuf(ctx, tag + "qkv", [P, G, 4, D], F32)
        qkt = sbuf(ctx, tag + "qkt", [P, 2, 3, S], F32)
        neg = sbuf(ctx, tag + "neg", [P, 2, 2], F32)
        pr = sbuf(ctx, tag + "pr", [P, 2, 2, S], F32)
        tot = sbuf(ctx, tag + "tot", [P, 2, 2], F32)
        rec = sbuf(ctx, tag + "rec", [P, 2, 2], F32)
        pt = sbuf(ctx, tag + "pt", [P, 2, 2 * S], F32)
        y = sbuf(ctx, tag + "y", [P, 2, 2 * S], BF16)
        p2 = sbuf(ctx, tag + "p2", [P, 2, 2 * S], BF16)
        m = sbuf(ctx, tag + "m", [P, 2, 2 * S], BF16)
        t = sbuf(ctx, tag + "t", [P, 2, 2 * S], F32)
        z = sbuf(ctx, tag + "z", [P, 2, 2 * S], F32R)
        names = ("cst", "xs", "cs", "proj", "stat", "var", "rstd", "qn", "tr", "qkt", "sc", "neg", "ex", "rec", "pn",
                 "tp", "pt", "o", "y", "yc", "p2", "m", "t", "z", "w", "x")
        (s_cst, s_xs, s_cs, s_proj, s_stat, s_var, s_rstd, s_qn, s_tr, s_qkt, s_sc, s_neg, s_ex, s_rec, s_pn,
         s_tp, s_pt, s_o, s_y, s_yc, s_p2, s_m, s_t, s_z, s_w, s_x) = (sem(f"{tag}u_{n}") for n in names)
        bP, bT, bS, bR, bO, bW = ps[0:2], ps[2], ps[3:5], ps[5], ps[6], ps[7]
        PEEL = 2

        with nc.Block() as block:
            @block.tensor
            def _(pe):
                pe.wait_ge(s_cst, 3)
                if cross:
                    pe.wait_ge(d_c, 32)

                def project(u):
                    xb = xs[:, u.b_par, :, :, :]
                    if u.g == 0:
                        pe.wait_ge(s_xs, u.b + 1)
                        if cross:
                            pe.wait_ge(s_cs, u.b + 1)
                    if u.before(2):
                        pe.wait_ge(s_qn, u.n - 1)
                    bank = bP[u.g % 2]
                    if cross:
                        parts = ((0, QW, 0),)
                    else:
                        parts = ((0, QW, 0), (QW, QW + D, 1), (QW + D, UW, 2))
                    for a, e, j in parts:
                        for k in range(CB):
                            pe.matmul(bank[:, a:e], xb[:, j, k, :], whi[:, u.g, k, a:e], start=(k == 0), stop=False)
                            mm = pe.matmul(bank[:, a:e], xb[:, j, k, :], wlo[:, u.g, k, a:e], start=False,
                                           stop=(k == CB - 1))
                    if cross:
                        for k in range(CB):
                            mm = pe.matmul(bank[:, QW:UW], cs[:, u.b_par, k, :], wkv[:, u.g, k, :],
                                           start=(k == 0), stop=(k == CB - 1))
                    mm.then_inc(s_proj, 1)

                def turn_qk(u):
                    pe.wait_ge(s_qn, u.n + 1)
                    if u.before(1):
                        pe.wait_ge(s_qkt, u.n)
                    for h in range(3):
                        mm = pe.transpose(bT[:, h * S:(h + 1) * S], qkv[:, u.g, h, :], ident[:, :])
                    mm.then_inc(s_tr, 1)

                def scores(u):
                    pe.wait_ge(s_qkt, u.n + 1)
                    if u.before(2):
                        pe.wait_ge(s_ex, u.n - 1)
                    for h in range(2):
                        mm = pe.matmul(bS[u.g % 2][:, h * S:(h + 1) * S], qkt[:, u.g % 2, h, :], qkt[:, u.g % 2, 2, :],
                                       start=True, stop=True)
                    mm.then_inc(s_sc, 1)

                def turn_p(u):
                    pe.wait_ge(s_pn, u.n + 1)
                    if u.before(1):
                        pe.wait_ge(s_pt, u.n)
                    for h in range(2):
                        mm = pe.transpose(bR[:, h * S:(h + 1) * S], pr[:, u.g % 2, h, :], ident[:, :])
                    mm.then_inc(s_tp, 1)

                def values(u):
                    pe.wait_ge(s_pt, u.n + 1)
                    if u.before(1):
                        pe.wait_ge(s_y, u.n)
                    pe.matmul(bO[:, 0:2 * S], qkv[:, u.g, 3, :], pt[:, u.g % 2, :], start=True, stop=True).then_inc(s_o, 1)

                def output(u):
                    pe.wait_ge(s_z, u.n + 1)
                    if u.g == 0 and u.before(G):
                        pe.wait_ge(s_x, u.b)
                    for h in range(2):
                        for w in (phi, plo):
                            mm = pe.matmul(bW[:, 0:C], z[:, u.g % 2, h * S:(h + 1) * S], w[:, 2 * u.g + h, :],
                                           start=(u.g == 0 and h == 0 and w is phi),
                                           stop=(u.g == G - 1 and h == 1 and w is plo))
                    mm.then_inc(s_w, 1)
                skewed(pe, B, G, [(turn_p, 5), (project, 0), (turn_qk, 2), (values, 6), (output, 8), (scores, 3)], PEEL)

            @block.scalar
            def _(act):
                if cross:
                    act.wait_ge(d_c, 32)

                def columns(u):
                    if u.g:
                        return
                    if u.before(2 * G):
                        act.wait_ge(s_proj, (u.b - 1) * G)
                    j = slice(3, 4) if cross else slice(0, 3)
                    act.activation(xs[:, u.b_par, :, :, :], xq[:, j, :, bass.ds(u.b * S, S)], ACT.Copy).then_inc(s_xs, 1)
                    if cross:
                        act.activation(cs[:, u.b_par, :, :], ct[:, :, bass.ds(u.b * S, S)], ACT.Copy).then_inc(s_cs, 1)

                def turned_qk(u):
                    act.wait_ge(s_tr, u.n + 1)
                    if u.before(2):
                        act.wait_ge(s_sc, u.n - 1)
                    a = aff[:, int(cross), :]
                    act.activation(qkt[:, u.g % 2, 0:2, :], bT[:, 0:2 * S].rearrange("p (h s) -> p h s", h=2),
                                   ACT.Identity, bias=a[:, 1:2], scale=a[:, 0:1])
                    act.activation(qkt[:, u.g % 2, 2, :], bT[:, 2 * S:3 * S], ACT.Identity, bias=a[:, 3:4],
                                   scale=a[:, 2:3]).then_inc(s_qkt, 1)

                def exps(u):
                    act.wait_ge(s_neg, u.n + 1)
                    if u.before(2):
                        act.wait_ge(s_tp, u.n - 1)
                    for h in range(2):
                        ins = act.activation(pr[:, u.g % 2, h, :], bS[u.g % 2][:, h * S:(h + 1) * S], ACT.Exp,
                                             bias=neg[:, u.g % 2, h:h + 1], accum_out=tot[:, u.g % 2, h:h + 1])
                    ins.then_inc(s_ex, 1)

                def turned_p(u):
                    act.wait_ge(s_tp, u.n + 1)
                    if u.before(2):
                        act.wait_ge(s_o, u.n - 1)
                    act.activation(pt[:, u.g % 2, :], bR[:, 0:2 * S], ACT.Copy).then_inc(s_pt, 1)
                skewed(act, B, G, [(columns, 0), (turned_p, 5), (turned_qk, 2), (exps, 3)], PEEL)

            @block.gpsimd
            def _(pool):
                pool.memset(half[:, :], -0.5).then_inc(s_cst, 1)
                pool.memset(rstd[:, :, :], 1.0).then_inc(s_cst, 1)
                pool.memset(deps[:, :], D * LN_EPS).then_inc(s_cst, 1)
                pool.wait_ge(s_cst, 3)

                def normalise(u):
                    pool.wait_ge(s_rec, u.n + 1)
                    pool.tensor_tensor(pr[:, u.g % 2, :, :], pr[:, u.g % 2, :, :],
                                       rec[:, u.g % 2, :].unsqueeze(2).to_broadcast([P, 2, S]), ALU.mult).then_inc(s_pn, 1)

                def deviation(u):
                    pool.wait_ge(s_stat, u.n + 1)
                    v = var[:, u.g % 2, :]
                    pool.tensor_tensor(v, stat[:, u.g % 2, 2:9:3], deps[:, :], ALU.add).then_inc(s_var, 1)
                    pool.wait_ge(s_var, u.n + 1)
                    if u.before(2):
                        pool.wait_ge(s_qn, u.n - 1)
                    pool.tensor_tensor(rstd[:, u.g % 2, 0:3], v, half[:, :], ALU.pow).then_inc(s_rstd, 1)

                def rounded(u):
                    pool.wait_ge(s_t, u.n + 1)
                    if u.before(2):
                        pool.wait_ge(s_w, u.n - 1)
                    pool.tensor_tensor(z[:, u.g % 2, :], t[:, u.g % 2, :], m[:, u.g % 2, :], ALU.subtract).then_inc(s_z, 1)
                skewed(pool, B, G, [(normalise, 4), (deviation, 0), (rounded, 7)], PEEL)

            @block.vector
            def _(dve):
                dve.wait_ge(s_cst, 3)

                def statistics(u):
                    dve.wait_ge(s_proj, u.n + 1)
                    if u.before(2):
                        dve.wait_ge(s_var, u.n - 1)
                    for h in range(2):
                        pair = bP[u.g % 2][:, h * QW:(h + 1) * QW].rearrange("p (h d) -> p d h", h=2)
                        ins = dve.bn_stats(stat[:, u.g % 2, 6 * h:6 * h + 6], pair)
                    ins.then_inc(s_stat, 1)

                def apply(u):
                    dve.wait_ge(s_rstd, u.n + 1)
                    if u.before(G):
                        dve.wait_ge(s_o, u.n - G + 1)
                    dve.tensor_tensor(qkv[:, u.g, :, :], bP[u.g % 2][:, :].rearrange("p (h d) -> p h d", h=4),
                                      rstd[:, u.g % 2, :].unsqueeze(2).to_broadcast([P, 4, D]), ALU.mult).then_inc(s_qn, 1)

                def maxima(u):
                    dve.wait_ge(s_sc, u.n + 1)
                    if u.before(2):
                        dve.wait_ge(s_ex, u.n - 1)
                    dve.tensor_reduce(neg[:, u.g % 2, :], bS[u.g % 2][:, 0:2 * S].rearrange("p (h s) -> p h s", h=2),
                                      AX.X, ALU.max, negate=True).then_inc(s_neg, 1)

                def reciprocals(u):
                    dve.wait_ge(s_ex, u.n + 1)
                    if u.before(2):
                        dve.wait_ge(s_pn, u.n - 1)
                    dve.reciprocal(rec[:, u.g % 2, :], tot[:, u.g % 2, :]).then_inc(s_rec, 1)

                def rounding(u):
                    dve.wait_ge(s_o, u.n + 1)
                    if u.before(2):
                        dve.wait_ge(s_z, u.n - 1)
                    yu, pu, mu, tu = (a[:, u.g % 2, :] for a in (y, p2, m, t))
                    for h in range(2):
                        head = 2 * G * int(cross) + 2 * u.g + h
                        ins = dve.tensor_scalar(yu[:, h * S:(h + 1) * S], bO[:, h * S:(h + 1) * S],
                                                invsm[:, head:head + 1], FP8_MAX, ALU.mult, ALU.min)
                    ins.then_inc(s_y, 1)
                    dve.wait_ge(s_y, u.n + 1)
                    dve.tensor_scalar(yu, yu, -FP8_MAX, None, ALU.max).then_inc(s_yc, 1)
                    dve.wait_ge(s_yc, u.n + 1)
                    dve.tensor_scalar(pu.bitcast(U16), yu.bitcast(U16), 0x7F80, None, ALU.bitwise_and).then_inc(s_p2, 1)
                    dve.wait_ge(s_p2, u.n + 1)
                    dve.tensor_scalar(mu, pu, FP8_MIN_NORMAL, ROUND, ALU.max, ALU.mult).then_inc(s_m, 1)
                    dve.wait_ge(s_m, u.n + 1)
                    dve.tensor_tensor(tu, yu, mu, ALU.add).then_inc(s_t, 1)

                def residual(u):
                    if u.g != G - 1:
                        return
                    dve.wait_ge(s_w, u.n + 1)
                    x = X[:, bass.ds(u.b, 1), :].rearrange("p a c -> p (a c)")
                    dve.scalar_tensor_tensor(x, bW[:, 0:C], pscale[:, 0:1], x, ALU.mult, ALU.add).then_inc(s_x, 1)
                skewed(dve, B, G, [(reciprocals, 4), (apply, 1), (rounding, 7), (statistics, 0), (maxima, 3),
                                   (residual, 8)], PEEL)
                dve.wait_ge(s_x, B)


def moe_layer(nc, io, sem, sbuf, X, XT, small, ident, ps, col, cols):
    ctx = ExitStack()
    with ctx:
        xhi = sbuf(ctx, "xhi", [P, CB, TOK], F32R)
        xlo = sbuf(ctx, "xlo", [P, CB, TOK], F32R)
        wg = sbuf(ctx, "wg", [P, CB, E], F32)
        st = [sbuf(ctx, f"st{i}", [P, 2 * I], F32) for i in range(3)]
        whi = [sbuf(ctx, f"w{i}hi", [P, 2, 2 * I], F32R) for i in range(3)]
        wlo = [sbuf(ctx, f"w{i}lo", [P, 2, 2 * I], F32R) for i in range(3)]
        sa = sbuf(ctx, "sa", [P, 2, W512], F32)
        h = sbuf(ctx, "h", [P, 2, W512], F32)
        hhi = sbuf(ctx, "hhi", [P, 2, IB, W512], F32R)
        hlo = sbuf(ctx, "hlo", [P, 2, IB, W512], F32R)
        lg = sbuf(ctx, "lg", [P, B, E], F32)
        ex = sbuf(ctx, "ex", [P, B, E], F32)
        p_ = sbuf(ctx, "p_", [P, B, E], F32)
        one = sbuf(ctx, "one", [P, B, E], F32)
        two = sbuf(ctx, "two", [P, B, E], F32)
        wt = sbuf(ctx, "wt", [P, B, E], F32)
        mx = sbuf(ctx, "f_mx", [P, B], F32)
        pm = sbuf(ctx, "f_pm", [P, B], F32)
        prio = sbuf(ctx, "f_prio", [P, E], F32)
        d_g, d_s = sem("f_dg"), [sem(f"f_ds{i}") for i in range(3)]
        (s_pr, s_lg, s_th, s_d, s_ex, s_wt, s_xhi, s_xlo, s_whi, s_wlo, s_up, s_si, s_mu, s_hhi, s_hlo, s_y, s_acc,
         s_link) = (sem("f_" + n) for n in ("pr", "lg", "th", "d", "ex", "wt", "xhi", "xlo", "whi", "wlo", "up", "si",
                                            "mu", "hhi", "hlo", "y", "acc", "link"))
        UE = NTG * IB
        PER = 2 * UE
        SPLITS = (8, 10, 12)
        UP, DOWN = UE, UE + IB + 1

        def expert(u):
            return u.b * 2 + u.g // UE

        def place(u):
            return u.g // UE, u.g % UE // IB, u.g % IB

        with nc.Block() as block:
            @block.sync
            def _(sp):
                sp.dma_start(wg[:, :, :], io["w_gate"].rearrange("(k p) n -> p k n", p=P)).then_inc(d_g, 16)

                def load(u):
                    if u.g % UE >= 3:
                        return
                    i = u.g % UE
                    if u.before(UE):
                        sp.wait_ge(s_wlo, expert(u) * 3 - 2 + i)
                    name, k = (("w1", CB), ("w3", CB), ("w2", IB))[i]
                    sp.dma_start(st[i][:, :].rearrange("p (k n) -> p k n", k=k),
                                 io[name][bass.ds(expert(u), 1), :, :].rearrange("a (k p) n -> p (a k) n", p=P)
                                 ).then_inc(d_s[i], 16)
                skewed(sp, E // 2, PER, [(load, 0)])

            @block.tensor
            def _(pe):
                pe.wait_ge(d_g, 16)
                for b in range(B):
                    for k in range(CB):
                        mm = pe.matmul(ps[7][:, b * E:(b + 1) * E], XT[:, k, b * S:(b + 1) * S], wg[:, k, :],
                                       start=(k == 0), stop=(k == CB - 1))
                mm.then_inc(s_lg, 1)
                pe.wait_ge(s_xlo, NTG)
                pe.wait_ge(s_th, 1)

                def up(u):
                    par, tg, ib = place(u)
                    if u.g % UE == 0:
                        pe.wait_ge(s_wlo, 3 * expert(u) + 3)
                    if u.before(2):
                        pe.wait_ge(s_mu, u.n - 1)
                    cols_ = slice(tg * W512, (tg + 1) * W512)
                    for i in range(2):
                        bank = ps[2 * (u.g % 2) + i]
                        for k in range(CB):
                            a = k * I + ib * P
                            hi, lo = whi[i][:, par, a:a + P], wlo[i][:, par, a:a + P]
                            pe.matmul(bank[:, :], hi, xhi[:, k, cols_], start=(k == 0), stop=False)
                            pe.matmul(bank[:, :], hi, xlo[:, k, cols_], start=False, stop=False)
                            mm = pe.matmul(bank[:, :], lo, xhi[:, k, cols_], start=False, stop=(k == CB - 1))
                        mm.then_inc(s_up, 1)

                def down(u):
                    par, tg, j = place(u)
                    pe.wait_ge(s_hlo, u.n - j + IB)
                    if u.before(4):
                        pe.wait_ge(s_acc, u.n - 3)
                    for ib in range(IB):
                        hi, lo = (a[:, tg % 2, ib, j * P:(j + 1) * P] for a in (hhi, hlo))
                        w_hi, w_lo = (a[2][:, par, ib * C:(ib + 1) * C] for a in (whi, wlo))
                        bank = ps[4 + u.g % 4][:, 0:C]
                        pe.matmul(bank, hi, w_hi, start=(ib == 0), stop=False)
                        pe.matmul(bank, hi, w_lo, start=False, stop=False)
                        mm = pe.matmul(bank, lo, w_hi, start=False, stop=(ib == IB - 1))
                    mm.then_inc(s_y, 1)
                skewed(pe, E // 2, PER, [(up, UP), (down, DOWN)])

            @block.scalar
            def _(act):
                act.wait_ge(s_lg, 1)
                act.activation(lg[:, :, :], ps[7][:, 0:B * E].rearrange("p (b e) -> p b e", e=E), ACT.Tanh,
                               scale=1.0 / SOFTCAP).then_inc(s_th, 1)
                for tg in range(NTG):
                    c = slice(tg * W512, (tg + 1) * W512)
                    act.activation(xhi[:, :, c], XT[:, :, c], ACT.Copy).then_inc(s_xhi, 1)
                act.wait_ge(s_d, 1)
                act.activation(ex[:, :, :], p_[:, :, :], ACT.Exp, scale=SOFTCAP).then_inc(s_ex, 1)

                def weights(u):
                    if u.g % UE not in SPLITS:
                        return
                    par, i = u.g // UE, SPLITS.index(u.g % UE)
                    act.wait_ge(d_s[i], 16 * expert(u) + 16)
                    if u.before(PER):
                        act.wait_ge(s_y, UE * expert(u) - UE)
                    act.activation(whi[i][:, par, :], st[i][:, :], ACT.Copy).then_inc(s_whi, 1)

                def silu(u):
                    act.wait_ge(s_up, 2 * u.n + 1)
                    if u.before(2):
                        act.wait_ge(s_mu, u.n - 1)
                    act.activation(sa[:, u.g % 2, :], ps[2 * (u.g % 2)][:, :], ACT.Silu).then_inc(s_si, 1)

                def high(u):
                    par, tg, ib = place(u)
                    act.wait_ge(s_mu, u.n + 1)
                    if u.before(2 * IB):
                        act.wait_ge(s_y, u.n - ib - IB)
                    act.activation(hhi[:, tg % 2, ib, :], h[:, u.g % 2, :], ACT.Copy).then_inc(s_hhi, 1)
                skewed(act, E // 2, PER, [(weights, 0), (high, UP + 1), (silu, UP)])

            @block.gpsimd
            def _(pool):
                for n in range(E):
                    ins = pool.memset(prio[:, n:n + 1], float(E - n))
                ins.then_inc(s_pr, 1)

                def weights(u):
                    if u.g % UE not in SPLITS:
                        return
                    par, i = u.g // UE, SPLITS.index(u.g % UE)
                    pool.wait_ge(s_whi, 3 * expert(u) + i + 1)
                    pool.tensor_tensor(wlo[i][:, par, :], st[i][:, :], whi[i][:, par, :].bitcast(F32),
                                       ALU.subtract).then_inc(s_wlo, 1)

                def low(u):
                    par, tg, ib = place(u)
                    pool.wait_ge(s_hhi, u.n + 1)
                    pool.tensor_tensor(hlo[:, tg % 2, ib, :], h[:, u.g % 2, :], hhi[:, tg % 2, ib, :].bitcast(F32),
                                       ALU.subtract).then_inc(s_hlo, 1)
                skewed(pool, E // 2, PER, [(weights, 0), (low, UP + 1)])

            @block.vector
            def _(dve):
                link = Links(dve, s_link)
                for tg in range(NTG):
                    c = slice(tg * W512, (tg + 1) * W512)
                    dve.wait_ge(s_xhi, tg + 1)
                    dve.tensor_tensor(xlo[:, :, c], XT[:, :, c], xhi[:, :, c].bitcast(F32), ALU.subtract).then_inc(s_xlo, 1)
                over = lambda a: a.unsqueeze(2).to_broadcast([P, B, E])
                dve.wait_ge(s_th, 1)
                dve.wait_ge(s_pr, 1)
                link(dve.tensor_reduce(mx[:, :], lg[:, :, :], AX.X, ALU.max))
                dve.tensor_tensor(p_[:, :, :], lg[:, :, :], over(mx[:, :]), ALU.subtract).then_inc(s_d, 1)
                dve.wait_ge(s_ex, 1)
                link(dve.tensor_reduce(mx[:, :], ex[:, :, :], AX.X, ALU.add))
                link(dve.reciprocal(mx[:, :], mx[:, :]))
                link(dve.tensor_tensor(p_[:, :, :], ex[:, :, :], over(mx[:, :]), ALU.mult))

                def first_of_best(out, a):
                    link(dve.tensor_reduce(mx[:, :], a, AX.X, ALU.max))
                    link(dve.tensor_tensor(out, a, over(mx[:, :]), ALU.is_ge))
                    link(dve.tensor_tensor(out, out, prio[:, :].unsqueeze(1).to_broadcast([P, B, E]), ALU.mult))
                    link(dve.tensor_reduce(pm[:, :], out, AX.X, ALU.max))
                    link(dve.tensor_tensor(out, out, over(pm[:, :]), ALU.is_equal))

                first_of_best(one[:, :, :], p_[:, :, :])
                link(dve.scalar_tensor_tensor(ex[:, :, :], one[:, :, :], -4.0, p_[:, :, :], ALU.mult, ALU.add))
                first_of_best(two[:, :, :], ex[:, :, :])
                link(dve.tensor_tensor(one[:, :, :], one[:, :, :], two[:, :, :], ALU.add))
                link(dve.tensor_tensor(wt[:, :, :], one[:, :, :], p_[:, :, :], ALU.mult))

                def gated(u):
                    dve.wait_ge(s_si, u.n + 1)
                    dve.wait_ge(s_up, 2 * u.n + 2)
                    if u.before(2):
                        dve.wait_ge(s_hlo, u.n - 1)
                    dve.tensor_tensor(h[:, u.g % 2, :], sa[:, u.g % 2, :], ps[2 * (u.g % 2) + 1][:, :],
                                      ALU.mult).then_inc(s_mu, 1)

                def weighted(u):
                    par, tg, j = place(u)
                    dve.wait_ge(s_y, u.n + 1)
                    x = X[:, tg * IB + j, :]
                    w = wt[:, tg * IB + j, bass.ds(expert(u), 1)]
                    dve.scalar_tensor_tensor(x, ps[4 + u.g % 4][:, 0:C], w, x, ALU.mult, ALU.add).then_inc(s_acc, 1)
                skewed(dve, E // 2, PER, [(weighted, DOWN), (gated, UP)])
                dve.wait_ge(s_acc, E * UE)


def _launch_arrays(i):
    f = np.float32
    a = {k: np.asarray(v) for k, v in i.items()}
    io = {}
    io["xT"] = a["x"].reshape(TOK, C).T
    io["wa"] = a["L0_attn_W"].T
    rep = lambda v: np.broadcast_to(v.reshape(1, -1), (P, v.size))
    blk = lambda v: v.reshape(-1, P).T
    n = "L1_xattn_"
    small = [blk(a["L0_attn_b"])] + [blk(a[n + k]) for k in ("qln_w", "qln_b", "kln_w", "kln_b", "qxln_w", "qxln_b",
                                                            "kxln_w", "kxln_b", "ln_w", "ln_b", "q_in_scale",
                                                            "k_in_scale", "v_in_scale", "qx_in_scale", "proj_smooth")]
    small += [rep(a[n + k]) for k in ("wq_scale", "wk_scale", "wv_scale", "wqx_scale", "proj_in_scale", "proj_w_scale")]
    small += [rep(a["L0_xattn_D"]), rep(a["L0_ffn_imp_center"]), rep(a["L0_ffn_imp_slope"])]
    io["small"] = np.concatenate(small, axis=1)
    ctx = a["ctx_2048"].reshape(TOK, C)
    io["ctxR"] = ctx.T.reshape(CB, P, TOK)[:, ::-1]
    pad = np.zeros((CH, P - 1 + C), f)
    pad[:, P - 1:] = a["L0_xattn_ssm_kernel"]
    io["toep"] = np.stack([pad[:, m:m + C] for m in range(P)], axis=1)
    io["wf"] = np.concatenate([a["L0_ffn_select_weight"].transpose(1, 0, 2).reshape(C, SEL),
                               a["L0_ffn_lora_update"].transpose(1, 0, 2).reshape(C, UPD),
                               a["L0_ffn_select_mean_diff"].T], axis=1)
    io["deb"] = a["L0_ffn_debias_w"].T
    io["lw"] = np.concatenate([a["L0_ffn_lora_degen"].transpose(0, 2, 1).reshape(UPD, C), a["L0_ffn_bias_w"]])
    QB, PAD = HQ // HKV, P // HKV
    wq = np.zeros((C, QB, HKV, PAD), f)
    wq[..., :HD] = a["L1_attn_Wq"].reshape(HKV, QB, HD, C).transpose(3, 1, 0, 2)
    wk = np.zeros((C, HKV, PAD), f)
    wk[..., :HD] = a["L1_attn_Wk"].reshape(HKV, HD, C).transpose(2, 0, 1)
    io["d_wq"], io["d_wk"] = wq.reshape(C, QB * P), wk.reshape(C, P)
    io["d_wv"], io["d_wo"] = a["L1_attn_Wv"].T, a["L1_attn_Wo"].T
    q2 = lambda w: w.T.reshape(C, G, 2 * D)
    k1 = lambda w: w.T.reshape(C, G, D)
    io["wself"] = np.concatenate([q2(a[n + "wq"]), k1(a[n + "wk"]), k1(a[n + "wv"])], axis=2).transpose(1, 0, 2)
    kv = a[n + "w_kv_x"].reshape(2, G, D, C)
    io["wqx"] = q2(a[n + "wqx"]).transpose(1, 0, 2)
    io["wkvx"] = kv.transpose(1, 3, 0, 2).reshape(G, C, 2 * D)
    io["wproj"] = a[n + "wproj"].T.reshape(2, 2 * G, D, C)
    io["ctxT"] = ctx.T
    io["w_gate"] = a["L1_ffn_w_gate"]
    io["w1"], io["w3"], io["w2"] = a["L1_ffn_w1"], a["L1_ffn_w3"], a["L1_ffn_w2"]
    return {k: np.ascontiguousarray(v) for k, v in io.items()}


STOP = 99


def kernel(**inputs):
    import concourse.bacc as bacc
    from concourse.bass_utils import run_bass_kernel_spmd

    nc = bacc.Bacc("TRN2", target_bir_lowering=False, num_devices=1)
    arrays = _launch_arrays(inputs)
    io = {k: nc.dram_tensor(k + "_dram", v.shape, mybir.dt.from_np(v.dtype), kind="ExternalInput").ap()
          for k, v in arrays.items()}
    io["out"] = nc.dram_tensor("out_dram", (B, S, C), F32, kind="ExternalOutput").ap()
    build(nc, io, STOP)
    r = run_bass_kernel_spmd(nc, [{k + "_dram": v for k, v in arrays.items()}], core_ids=[0])
    return r.results[0]["out_dram"]
```

```python
import numpy as np
import concourse.bass as bass
from concourse import mybir
from contextlib import ExitStack

F32, F32R, BF16 = mybir.dt.float32, mybir.dt.float32r, mybir.dt.bfloat16
I32, U16 = mybir.dt.int32, mybir.dt.uint16
ACT = mybir.ActivationFunctionType
ALU = mybir.AluOpType
AX = mybir.AxisListType

B, S, C = 16, 128, 256
P = 128
CB = C // P
TOK = B * S
W512 = 512
NTG = TOK // W512
LN_EPS = 1e-5
CH, CD = 16, 8
NE0, NS0 = 8, 8
SEL, UPD = NE0 * NS0, NE0 * NS0
FW = SEL + UPD + NE0
HQ, HKV, HD = 16, 4, 16
G, D = 8, 128
UW = 4 * D
FP8_MAX = 448.0
FP8_MIN_NORMAL = 2.0 ** -6
ROUND = 1.5 * 2.0 ** 20
E, I = 8, 512
IB = I // P
SOFTCAP = 30.0
WHOLE = 1.5 * 2.0 ** 23

SMALL = {}
_at = 0
for _name, _n in (("ab", 4), ("qw", 1), ("qb", 1), ("kw", 1), ("kb", 1), ("qxw", 1), ("qxb", 1),
                  ("kxw", 1), ("kxb", 1), ("lnw", 2), ("lnb", 2), ("sq", 2), ("sk", 2), ("sv", 2),
                  ("sqx", 2), ("smooth", 32), ("wsq", 1), ("wsk", 1), ("wsv", 1), ("wsqx", 1),
                  ("pin", 1), ("pw", 1), ("dskip", CH), ("center", NE0), ("slope", NE0)):
    SMALL[_name] = (_at, _at + _n)
    _at += _n
NSMALL = _at


class Links:

    def __init__(self, eng, sem):
        self.eng, self.sem, self.base, self.n, self.i, self.per = eng, sem, 0, 0, None, 0

    def enter(self, i, per):
        self.base, self.n, self.i, self.per = self.base + self.n, 0, i, per

    def leave(self, trips):
        assert self.n == self.per, (self.n, self.per)
        self.base, self.n, self.i = self.base + self.per * trips, 0, None

    def __call__(self, ins):
        ins.then_inc(self.sem, 1)
        self.n += 1
        at = self.base + self.n
        self.eng.wait_ge(self.sem, at if self.i is None else self.i * self.per + at)
        return ins


class Unit:

    def __init__(self, b, g, per, peeled, b_par=0):
        self.b, self.g, self.n, self.peeled, self.b_par = b, g, b * per + g, peeled, b_par

    def before(self, k):
        return not self.peeled or self.n >= k


def skewed(eng, outer, per, stages, peel=1):
    def step(b, j, g, in_loop):
        for stage, lag in stages:
            at, back = (g - lag) % per, -((g - lag) // per)
            if in_loop or (b - back >= 0 and b - back < outer):
                u_b = b + (j - back) if in_loop else b - back
                stage(Unit(u_b, at, per, not in_loop, (j - back) % 2 if in_loop else (b - back) % 2))

    assert outer % peel == 0
    for b in range(peel):
        for g in range(per):
            step(b, 0, g, False)
    if outer > peel:
        with eng.Fori(1, outer // peel) as i:
            for j in range(peel):
                for g in range(per):
                    step(i * peel, j, g, True)
    for g in range(max(lag for _, lag in stages)):
        step(outer + g // per, 0, g % per, False)


def build(nc, io, stop=99):
    ctx = ExitStack()
    with ctx:
        held = []

        def sem(name):
            held.append(nc.alloc_semaphore(name=name))
            return held[-1]

        def layer(f, *a, **k):
            f(*a, **k, **args)
            nc.clear_and_free_semaphores(list(held))
            held.clear()
            nc.all_engine_barrier()

        def sbuf(c, name, shape, dt):
            return c.enter_context(nc.sbuf_tensor(name, shape, dt))

        X = sbuf(ctx, "X", [P, B, C], F32)
        XT = sbuf(ctx, "XT", [P, CB, TOK], F32)
        small = sbuf(ctx, "small", [P, NSMALL], F32)
        ident = sbuf(ctx, "ident", [P, P], F32)
        ps = [ctx.enter_context(nc.psum_tensor(f"ps{i}", [P, W512], F32)) for i in range(8)]

        def col(name, k=0):
            a = SMALL[name][0] + k
            return small[:, a:a + 1]

        def cols(name):
            return small[:, slice(*SMALL[name])]

        if stop > 5:
            NT = moe_tiles()
            for name in ("sorted_x", "sorted_y"):
                io[name] = nc.dram_tensor(name, (NT * P, C), F32, kind="Internal").ap()
        args = dict(nc=nc, io=io, sem=sem, sbuf=sbuf, X=X, XT=XT, small=small, ident=ident, ps=ps,
                    col=col, cols=cols)
        layer(scan_layer)
        layer(norm_layer, "n0", from_channels=True)
        if stop > 1:
            layer(conv_layer)
            layer(norm_layer, "n1", from_channels=True)
        if stop > 2:
            layer(routed_layer)
            layer(norm_layer, "n2")
        with ExitStack() as quant_ctx:
            quant = Quant(quant_ctx, sbuf) if stop > 3 else None
            if stop > 3:
                layer(causal_layer, quant)
                layer(norm_layer, "n3", back=False)
            if stop > 4:
                layer(quant_layer, quant)
        if stop > 4:
            layer(norm_layer, "n4")
        if stop > 5:
            layer(moe_layer)
            layer(norm_layer, "n5", back=False)

        out_done = sem("out_done")
        with nc.Block() as block:
            @block.sync
            def _(sp):
                sp.dma_start(io["out"].rearrange("b t c -> t b c"), X[:, :, :]).then_inc(out_done, 16)
                sp.wait_ge(out_done, 16)


def rsqrt(dve, link, x, y, t, n):
    link(dve.tensor_scalar(y.bitcast(I32), x.bitcast(I32), 1, None, ALU.logical_shift_right))
    link(dve.tensor_scalar(y.bitcast(I32), y.bitcast(I32), -1.0, float(0x5F3759DF), ALU.mult, ALU.add))
    for _ in range(n):
        link(dve.tensor_tensor(t, y, y, ALU.mult))
        link(dve.tensor_tensor(t, t, x, ALU.mult))
        link(dve.tensor_scalar(t, t, -0.5, 1.5, ALU.mult, ALU.add))
        link(dve.tensor_tensor(y, y, t, ALU.mult))


def norm_layer(tag, nc, io, sem, sbuf, X, XT, small, ident, ps, col, cols, from_channels=False,
               back=True, dst=None, eps=LN_EPS):
    dst = X if dst is None else dst
    ctx = ExitStack()
    with ctx:
        st = sbuf(ctx, tag + "_st", [P, B, 6], F32)
        m = [sbuf(ctx, f"{tag}_m{k}", [P, B], F32) for k in range(5)]
        mean, var, rstd, tmp, nmr = m
        s_tok = sem(tag + "_tok")
        s_evac = sem(tag + "_evac")
        s_norm = sem(tag + "_norm")
        s_back = sem(tag + "_back")
        s_free = sem(tag + "_free")
        s_link = sem(tag + "_link")
        with nc.Block() as block:
            @block.tensor
            def _(pe):
                if from_channels:
                    for b in range(B):
                        for k in range(CB):
                            mm = pe.transpose(ps[b // 2][:, (b % 2) * C + k * P:(b % 2) * C + (k + 1) * P],
                                              XT[:, k, b * S:(b + 1) * S], ident[:, :])
                        if b % 2:
                            mm.then_inc(s_tok, 1)
                if back:
                    for tg in range(NTG):
                        pe.wait_ge(s_norm, tg * 4 + 4)
                        if from_channels:
                            pe.wait_ge(s_evac, B // 2)
                        for k in range(CB):
                            for j in range(4):
                                b = tg * 4 + j
                                mm = pe.transpose(ps[tg * 2 + k][:, j * P:(j + 1) * P],
                                                  dst[:, b, k * P:(k + 1) * P], ident[:, :])
                            mm.then_inc(s_back, 1)

            @block.scalar
            def _(act):
                if from_channels:
                    for h in range(B // 2):
                        act.wait_ge(s_tok, h + 1)
                        act.activation(X[:, 2 * h:2 * h + 2, :],
                                       ps[h][:, :].rearrange("p (b c) -> p b c", b=2), ACT.Copy).then_inc(s_evac, 1)
                if back:
                    for tg in range(NTG):
                        for k in range(CB):
                            act.wait_ge(s_back, tg * 2 + k + 1)
                            act.activation(XT[:, k, tg * W512:(tg + 1) * W512], ps[tg * 2 + k][:, :],
                                           ACT.Copy).then_inc(s_free, 1)
                    act.wait_ge(s_free, NTG * CB)

            @block.vector
            def _(dve):
                link = Links(dve, s_link)
                for b in range(B):
                    if from_channels and b % 2 == 0:
                        dve.wait_ge(s_evac, b // 2 + 1)
                    ins = dve.bn_stats(st[:, b, :], X[:, b, :])
                link(ins)
                even, odd = st[:, :, 1], st[:, :, 4]
                link(dve.tensor_tensor(mean[:, :], even, odd, ALU.add))
                link(dve.tensor_tensor(tmp[:, :], even, odd, ALU.subtract))
                link(dve.tensor_tensor(tmp[:, :], tmp[:, :], tmp[:, :], ALU.mult))
                link(dve.tensor_tensor(var[:, :], st[:, :, 2], st[:, :, 5], ALU.add))
                link(dve.scalar_tensor_tensor(var[:, :], tmp[:, :], C / 4.0, var[:, :], ALU.mult, ALU.add))
                link(dve.tensor_scalar(var[:, :], var[:, :], 1.0 / C, eps, ALU.mult, ALU.add))
                link(dve.tensor_scalar(mean[:, :], mean[:, :], 0.5, None, ALU.mult))
                rsqrt(dve, link, var[:, :], rstd[:, :], tmp[:, :], 3)
                for b in range(B):
                    dve.tensor_scalar(dst[:, b, :], X[:, b, :], mean[:, b:b + 1], rstd[:, b:b + 1],
                                      ALU.subtract, ALU.mult).then_inc(s_norm, 1)
                dve.wait_ge(s_norm, B)


def scan_layer(nc, io, sem, sbuf, X, XT, small, ident, ps, col, cols):
    ctx = ExitStack()
    with ctx:
        xin = sbuf(ctx, "xin", [P, CB, TOK], F32)
        wa = sbuf(ctx, "wa", [P, CB, 2 * C], F32)
        gate = sbuf(ctx, "gate", [P, 2, CB, W512], F32)
        val = sbuf(ctx, "val", [P, 2, CB, W512], F32)
        hid = sbuf(ctx, "hid", [P, 2, CB, W512], F32)
        d_x, d_w = [sem(f"a_dx{k}") for k in range(NTG)], sem("a_dw")
        s_id, s_mm, s_act, s_zero, s_scan, s_add = (sem("a_" + n) for n in
                                                    ("id", "mm", "act", "zero", "scan", "add"))
        with nc.Block() as block:
            @block.sync
            def _(sp):
                sp.dma_start(wa[:, :, :], io["wa"].rearrange("(k p) n -> p k n", p=P)).then_inc(d_w, 16)
                sp.dma_start(small[:, :], io["small"]).then_inc(d_w, 16)
                for tg in range(NTG):
                    sp.dma_start(xin[:, :, tg * W512:(tg + 1) * W512],
                                 io["xT"].rearrange("(k p) n -> p k n", p=P)[:, :, tg * W512:(tg + 1) * W512]
                                 ).then_inc(d_x[tg], 16)

            @block.tensor
            def _(pe):
                pe.wait_ge(d_w, 32)
                for tg in range(NTG):
                    pe.wait_ge(d_x[tg], 16)
                    if tg >= 2:
                        pe.wait_ge(s_act, 4 * (tg - 1))
                    for m in range(4):
                        for k in range(CB):
                            mm = pe.matmul(ps[(tg % 2) * 4 + m][:, :], wa[:, k, m * P:(m + 1) * P],
                                           xin[:, k, tg * W512:(tg + 1) * W512], start=(k == 0), stop=(k == CB - 1))
                        mm.then_inc(s_mm, 1)

            @block.scalar
            def _(act):
                for tg in range(NTG):
                    if tg >= 2:
                        act.wait_ge(s_scan, 2 * (tg - 1))
                    for m in range(4):
                        act.wait_ge(s_mm, 4 * tg + m + 1)
                        out = (gate if m < CB else val)[:, tg % 2, m % CB, :]
                        act.activation(out, ps[(tg % 2) * 4 + m][:, :], ACT.Sigmoid if m < CB else ACT.Tanh,
                                       bias=col("ab", m)).then_inc(s_act, 1)

            @block.gpsimd
            def _(pool):
                pool.memset(ident[:, :], 0.0).then_inc(s_id, 1)
                pool.wait_ge(s_id, 1)
                pool.affine_select(out=ident[:, :], in_=ident[:, :], compare_op=ALU.not_equal, fill=1.0,
                                   base=0, pattern=[[-1, P]], channel_multiplier=1).then_inc(s_id, 1)
                pool.wait_ge(s_id, 2)
                for tg in range(NTG):
                    pool.wait_ge(s_act, 4 * tg + CB)
                    g = gate[:, tg % 2, :, :].rearrange("p k (b s) -> p k b s", s=S)
                    pool.memset(g[:, :, :, 0], 0.0).then_inc(s_zero, 1)
                    pool.wait_ge(s_scan, 2 * (tg + 1))
                    pool.tensor_tensor(XT[:, :, tg * W512:(tg + 1) * W512], hid[:, tg % 2, :, :],
                                       xin[:, :, tg * W512:(tg + 1) * W512], ALU.add).then_inc(s_add, 1)
                pool.wait_ge(s_add, NTG)

            @block.vector
            def _(dve):
                for tg in range(NTG):
                    dve.wait_ge(s_zero, tg + 1)
                    dve.wait_ge(s_act, 4 * tg + 4)
                    if tg >= 2:
                        dve.wait_ge(s_add, tg - 1)
                    for k in range(CB):
                        dve.tensor_tensor_scan(hid[:, tg % 2, k, :], gate[:, tg % 2, k, :], val[:, tg % 2, k, :],
                                               0.0, ALU.mult, ALU.add).then_inc(s_scan, 1)


def conv_layer(nc, io, sem, sbuf, X, XT, small, ident, ps, col, cols):
    ctx = ExitStack()
    with ctx:
        ct = sbuf(ctx, "ct", [P, CB, TOK], F32)
        res = sbuf(ctx, "res", [P, CB, TOK], F32)
        tz = sbuf(ctx, "tz", [P, 2, C], F32)
        rev = sbuf(ctx, "rev", [P, P], F32)
        kv = sbuf(ctx, "kv", [P, 2, CB, W512], F32)
        prod = sbuf(ctx, "prod", [P, CB, W512], F32)
        d_c, d_t = sem("b_dc"), [sem("b_dt0"), sem("b_dt1")]
        s_rev, s_tz, s_kv, s_mm, s_prod, s_red, s_add = (sem("b_" + n) for n in
                                                        ("rev", "tz", "kv", "mm", "prod", "red", "add"))
        HB = B // 2
        ct_v = ct[:, :, :].rearrange("p k (b t) -> p k b t", t=S)
        xt_v = XT[:, :, :].rearrange("p k (b t) -> p k b t", t=S)
        res_v = res[:, :, :].rearrange("p k (b t) -> p k b t", t=S)

        def head(u):
            return u.b * 2 + u.g // 2

        with nc.Block() as block:
            @block.sync
            def _(sp):
                sp.dma_start(ct[:, :, :], io["ctxR"].rearrange("k p n -> p k n")).then_inc(d_c, 16)

                def load(u):
                    if u.g % 2 == 0:
                        if u.before(4):
                            sp.wait_ge(s_mm, u.n - 2)
                        sp.dma_start(tz[:, u.g // 2, :], io["toep"][bass.ds(head(u), 1), :, :].rearrange(
                            "a p n -> (a p) n")).then_inc(d_t[u.g // 2], 16)
                skewed(sp, CH // 2, 4, [(load, 0)])

            @block.gpsimd
            def _(pool):
                pool.memset(rev[:, :], 0.0).then_inc(s_rev, 1)
                pool.wait_ge(s_rev, 1)
                pool.affine_select(out=rev[:, :], in_=rev[:, :], compare_op=ALU.not_equal, fill=1.0,
                                   base=-(P - 1), pattern=[[1, P]], channel_multiplier=1).then_inc(s_rev, 1)
                pool.wait_ge(d_c, 16)

                def products(u):
                    if u.before(2):
                        pool.wait_ge(s_mm, u.n - 1)
                    half = (u.g % 2) * HB
                    for k in range(CB):
                        c = ct_v[:, k, half:half + HB, bass.ds(head(u) * CD, CD)]
                        ins = pool.tensor_tensor(kv[:, u.g % 2, k, :].rearrange("p (b j i) -> p b j i", j=CD, i=CD),
                                                 c.unsqueeze(3).to_broadcast([P, HB, CD, CD]),
                                                 c.unsqueeze(2).to_broadcast([P, HB, CD, CD]), ALU.mult)
                    ins.then_inc(s_kv, 1)
                skewed(pool, CH // 2, 4, [(products, 0)])

            @block.tensor
            def _(pe):
                def conv(u):
                    pe.wait_ge(s_kv, u.n + 1)
                    if u.g % 2 == 0:
                        pe.wait_ge(s_tz, head(u) + 1)
                    if u.before(2):
                        pe.wait_ge(s_prod, u.n - 1)
                    t, lo, hi = tz[:, u.g // 2, :], ps[(u.g % 2) * 2], ps[(u.g % 2) * 2 + 1]
                    pe.matmul(lo[:, :], t[:, 0:P], kv[:, u.g % 2, 0, :], start=True, stop=True)
                    pe.matmul(hi[:, :], t[:, P:C], kv[:, u.g % 2, 0, :], start=True, stop=False)
                    pe.matmul(hi[:, :], t[:, 0:P], kv[:, u.g % 2, 1, :], start=False, stop=True).then_inc(s_mm, 1)
                skewed(pe, CH // 2, 4, [(conv, 0)])

            @block.vector
            def _(dve):
                dve.wait_ge(s_rev, 2)

                def diagonal(u):
                    if u.g % 2 == 0:
                        dve.wait_ge(d_t[u.g // 2], u.b * 16 + 16)
                        t = tz[:, u.g // 2, 0:P]
                        d = cols("dskip")[:, bass.ds(head(u), 1)]
                        dve.scalar_tensor_tensor(t, rev[:, :], d, t, ALU.mult, ALU.add).then_inc(s_tz, 1)

                def queries(u):
                    dve.wait_ge(s_mm, u.n + 1)
                    half = (u.g % 2) * HB
                    if u.before(1):
                        dve.wait_ge(s_red, u.n)
                    for k in range(CB):
                        q = xt_v[:, k, half:half + HB, bass.ds(head(u) * CD, CD)]
                        ins = dve.tensor_tensor(prod[:, k, :].rearrange("p (b j i) -> p b j i", j=CD, i=CD),
                                                ps[(u.g % 2) * 2 + k][:, :].rearrange("p (b j i) -> p b j i", j=CD, i=CD),
                                                q.unsqueeze(2).to_broadcast([P, HB, CD, CD]), ALU.mult)
                    ins.then_inc(s_prod, 1)
                    dve.wait_ge(s_prod, u.n + 1)
                    for k in range(CB):
                        o = res_v[:, k, half:half + HB, bass.ds(head(u) * CD, CD)]
                        ins = dve.tensor_reduce(o, prod[:, k, :].rearrange("p (b j i) -> p b j i", j=CD, i=CD),
                                                AX.X, ALU.add)
                    ins.then_inc(s_red, 1)
                skewed(dve, CH // 2, 4, [(diagonal, 0), (queries, 1)])
                dve.wait_ge(s_red, 2 * CH)
                dve.tensor_tensor(XT[:, :, :], XT[:, :, :], res[:, :, :], ALU.add).then_inc(s_add, 1)
                dve.wait_ge(s_add, 1)


def routed_layer(nc, io, sem, sbuf, X, XT, small, ident, ps, col, cols):
    ctx = ExitStack()
    with ctx:
        wf = sbuf(ctx, "wf", [P, CB, FW], F32)
        deb = sbuf(ctx, "deb", [P, CB, NE0], F32)
        lw = sbuf(ctx, "lw", [SEL + NE0, C], F32)
        pr = sbuf(ctx, "pr", [P, CB, FW], F32)
        cst = sbuf(ctx, "cst", [P, FW], F32)
        ones = sbuf(ctx, "c_ones", [P, P], F32)
        prio = sbuf(ctx, "prio", [P, NE0], F32)
        u_ = sbuf(ctx, "u_", [P, B, SEL + UPD], F32)
        xm = sbuf(ctx, "xm", [P, B, NE0], F32)
        sq = sbuf(ctx, "sq_", [P, B, C], F32)
        xx = sbuf(ctx, "xx", [P, B], F32)
        sc = sbuf(ctx, "sc", [P, B, NE0], F32)
        gt = sbuf(ctx, "gt", [P, B, NE0], F32)
        eq = sbuf(ctx, "eq", [P, B, NE0], F32)
        mx = sbuf(ctx, "mx", [P, B], F32)
        pm = sbuf(ctx, "pm", [P, B], F32)
        keep = sbuf(ctx, "keep", [P, B], F32)
        mk = sbuf(ctx, "mk", [P, B, UPD + NE0], F32)
        mkt = sbuf(ctx, "mkt", [UPD + NE0, B, P], F32)
        d_w = sem("c_dw")
        s_one, s_pr, s_cm, s_cst, s_mm, s_u, s_z, s_ex, s_mk, s_t, s_te, s_o, s_x, s_link = (
            sem("c_" + n) for n in ("one", "pr", "cm", "cst", "mm", "u", "z", "ex", "mk", "t", "te", "o", "x", "link"))

        def over(a, n):
            return a.unsqueeze(2).to_broadcast([P, B, n])

        with nc.Block() as block:
            @block.sync
            def _(sp):
                sp.dma_start(wf[:, :, :], io["wf"].rearrange("(k p) n -> p k n", p=P)).then_inc(d_w, 16)
                sp.dma_start(deb[:, :, :], io["deb"].rearrange("(k p) n -> p k n", p=P)).then_inc(d_w, 16)
                sp.dma_start(lw[:, :], io["lw"]).then_inc(d_w, 16)

            @block.gpsimd
            def _(pool):
                pool.memset(ones[:, :], 1.0)
                for n in range(NE0):
                    ins = pool.memset(prio[:, n:n + 1], float(NE0 - n))
                ins.then_inc(s_one, 1)

            @block.tensor
            def _(pe):
                pe.wait_ge(d_w, 48)
                pe.wait_ge(s_one, 1)
                pe.wait_ge(s_pr, 3)
                for k in range(CB):
                    mm = pe.matmul(ps[0][:, 0:FW], ones[:, :], pr[:, k, :], start=(k == 0), stop=(k == CB - 1))
                mm.then_inc(s_cm, 1)
                pe.wait_ge(s_cst, 1)
                for b in range(B):
                    for k in range(CB):
                        mm = pe.matmul(ps[b // 2][:, (b % 2) * C:(b % 2) * C + FW], XT[:, k, b * S:(b + 1) * S],
                                       wf[:, k, :], start=(k == 0), stop=(k == CB - 1))
                mm.then_inc(s_mm, 1)
                pe.wait_ge(s_mk, 1)
                for q in range(B // 4):
                    for j in range(4):
                        mm = pe.transpose(ps[q][0:UPD + NE0, j * P:(j + 1) * P], mk[:, 4 * q + j, :], ident[:, :])
                    mm.then_inc(s_t, 1)
                for b in range(B):
                    pe.wait_ge(s_te, b // 4 + 1)
                    if b >= 8 and b % 2 == 0:
                        pe.wait_ge(s_x, b - 6)
                    mm = pe.matmul(ps[4 + (b // 2) % 4][:, (b % 2) * C:(b % 2 + 1) * C], mkt[:, b, :], lw[:, :],
                                   start=True, stop=True)
                    if b % 2:
                        mm.then_inc(s_o, 1)

            @block.scalar
            def _(act):
                act.wait_ge(s_z, 1)
                act.activation(gt[:, :, :], sc[:, :, :], ACT.Exp, scale=-1.0).then_inc(s_ex, 1)
                for q in range(B // 4):
                    act.wait_ge(s_t, q + 1)
                    act.activation(mkt[:, 4 * q:4 * q + 4, :],
                                   ps[q][0:UPD + NE0, :].rearrange("p (b s) -> p b s", b=4), ACT.Copy).then_inc(s_te, 1)

            @block.vector
            def _(dve):
                link = Links(dve, s_link)
                dve.wait_ge(d_w, 48)
                m = wf[:, :, SEL + UPD:FW]

                def pairs(a):
                    return a.rearrange("p k (n s) -> p k n s", s=NS0)

                dve.tensor_tensor(pairs(pr[:, :, 0:SEL]), pairs(wf[:, :, 0:SEL]),
                                  m.unsqueeze(3).to_broadcast([P, CB, NE0, NS0]), ALU.mult).then_inc(s_pr, 1)
                dve.tensor_tensor(pairs(pr[:, :, SEL:SEL + UPD]), pairs(wf[:, :, SEL:SEL + UPD]),
                                  deb[:, :, :].unsqueeze(3).to_broadcast([P, CB, NE0, NS0]), ALU.mult).then_inc(s_pr, 1)
                dve.tensor_tensor(pr[:, :, SEL + UPD:FW], m, m, ALU.mult).then_inc(s_pr, 1)
                dve.wait_ge(s_cm, 1)
                dve.tensor_copy(cst[:, :], ps[0][:, 0:FW]).then_inc(s_cst, 1)
                link(dve.tensor_tensor(sq[:, :, :], X[:, :, :], X[:, :, :], ALU.mult))
                link(dve.tensor_reduce(xx[:, :], sq[:, :, :], AX.X, ALU.add))
                dve.wait_ge(s_cst, 1)
                dve.wait_ge(s_one, 1)
                dve.wait_ge(s_mm, 1)
                for q in range(B // 2):
                    bank = ps[q][:, :].rearrange("p (b c) -> p b c", b=2)
                    dve.tensor_tensor(u_[:, 2 * q:2 * q + 2, :], bank[:, :, 0:SEL + UPD],
                                      cst[:, 0:SEL + UPD].unsqueeze(1).to_broadcast([P, 2, SEL + UPD]), ALU.subtract)
                    ins = dve.tensor_copy(xm[:, 2 * q:2 * q + 2, :], bank[:, :, SEL + UPD:FW])
                link(ins)
                s2 = sq[:, :, 0:SEL]
                link(dve.tensor_tensor(s2, u_[:, :, 0:SEL], u_[:, :, 0:SEL], ALU.mult))
                link(dve.tensor_reduce(sc[:, :, :], s2.rearrange("p b (n s) -> p b n s", s=NS0), AX.X, ALU.add))
                mm_ = cst[:, SEL + UPD:FW].unsqueeze(1).to_broadcast([P, B, NE0])
                link(dve.scalar_tensor_tensor(xm[:, :, :], xm[:, :, :], -2.0, mm_, ALU.mult, ALU.add))
                link(dve.tensor_tensor(xm[:, :, :], xm[:, :, :], over(xx[:, :], NE0), ALU.add))
                link(dve.reciprocal(xm[:, :, :], xm[:, :, :]))
                link(dve.tensor_tensor(sc[:, :, :], sc[:, :, :], xm[:, :, :], ALU.mult))
                link(dve.tensor_tensor(sc[:, :, :], sc[:, :, :],
                                       cols("center").unsqueeze(1).to_broadcast([P, B, NE0]), ALU.subtract))
                link(dve.tensor_tensor(sc[:, :, :], sc[:, :, :],
                                       cols("slope").unsqueeze(1).to_broadcast([P, B, NE0]), ALU.mult))
                dve.tensor_scalar(sc[:, :, :], sc[:, :, :], -87.0, None, ALU.max).then_inc(s_z, 1)
                dve.wait_ge(s_ex, 1)
                link(dve.tensor_scalar(gt[:, :, :], gt[:, :, :], 1.0, None, ALU.add))
                link(dve.reciprocal(gt[:, :, :], gt[:, :, :]))
                link(dve.tensor_reduce(mx[:, :], gt[:, :, :], AX.X, ALU.max))
                link(dve.tensor_tensor(eq[:, :, :], gt[:, :, :], over(mx[:, :], NE0), ALU.is_ge))
                link(dve.tensor_tensor(eq[:, :, :], eq[:, :, :],
                                       prio[:, :].unsqueeze(1).to_broadcast([P, B, NE0]), ALU.mult))
                link(dve.tensor_reduce(pm[:, :], eq[:, :, :], AX.X, ALU.max))
                link(dve.tensor_tensor(eq[:, :, :], eq[:, :, :], over(pm[:, :], NE0), ALU.is_equal))
                link(dve.tensor_scalar(keep[:, :], mx[:, :], -1.0, 2.0, ALU.mult, ALU.add))
                link(dve.tensor_tensor(mk[:, :, UPD:UPD + NE0], eq[:, :, :], over(mx[:, :], NE0), ALU.mult))
                for h in range(2):
                    bs = slice(h * 8, h * 8 + 8)
                    ins = dve.tensor_tensor(mk[:, bs, 0:UPD].rearrange("p b (n s) -> p b n s", s=NS0),
                                            u_[:, bs, SEL:SEL + UPD].rearrange("p b (n s) -> p b n s", s=NS0),
                                            mk[:, bs, UPD:UPD + NE0].unsqueeze(3).to_broadcast([P, 8, NE0, NS0]), ALU.mult)
                ins.then_inc(s_mk, 1)
                for b in range(B):
                    dve.wait_ge(s_o, b // 2 + 1)
                    dve.scalar_tensor_tensor(X[:, b, :], X[:, b, :], keep[:, b:b + 1],
                                             ps[4 + (b // 2) % 4][:, (b % 2) * C:(b % 2 + 1) * C],
                                             ALU.mult, ALU.add).then_inc(s_x, 1)
                dve.wait_ge(s_x, B)


def causal_layer(quant, nc, io, sem, sbuf, X, XT, small, ident, ps, col, cols):
    ctx = ExitStack()
    with ctx:
        QB = HQ // HKV
        PAD = P // HKV
        wq = sbuf(ctx, "d_wq", [P, CB, QB * P], F32)
        wk = sbuf(ctx, "d_wk", [P, CB, P], F32)
        wv = sbuf(ctx, "d_wv", [P, CB, HKV * HD], F32)
        wo = sbuf(ctx, "d_wo", [P, CB, C], F32)
        identb = sbuf(ctx, "identb", [P, P], BF16)
        mask = sbuf(ctx, "mask", [P, HKV, P], BF16)
        xs = sbuf(ctx, "xs", [P, 2, CB, S], F32)
        qt = sbuf(ctx, "qt_", [P, 2, QB * P], F32)
        kd = sbuf(ctx, "kd", [P, 2, HKV, P], F32)
        v = sbuf(ctx, "d_v", [P, 2, HKV, HD + 1], F32)
        neg = sbuf(ctx, "neg", [P, 2, HKV], F32)
        sb_ = sbuf(ctx, "sb_", [P, 2, HKV, P], F32)
        pt = sbuf(ctx, "pt_", [P, 2, HKV, P], F32)
        rec = sbuf(ctx, "rec", [P, QB, HKV], F32)
        cx = sbuf(ctx, "cx", [P, C], F32)
        cxt = sbuf(ctx, "cxt", [P, CB, P], F32)
        d_w = sem("d_dw")
        split = Split("ss_", False, quant.dst, nc, io, sem, sbuf, ctx)
        s_const = sem("d_const")

        (s_cst, s_xs, s_mm, s_q, s_k, s_s, s_mx, s_sub, s_ex, s_tp, s_cp, s_c, s_rc, s_cn, s_ct, s_cc, s_o, s_x) = (
            sem("d_" + n) for n in ("cst", "xs", "mm", "q", "k", "s", "mx", "sub", "ex", "tp", "cp", "c", "rc", "cn",
                                    "ct", "cc", "o", "x"))
        bQ, bK, bS, bT, bC, bF = ps[0], ps[1], ps[2:4], ps[4:6], ps[6], ps[7]
        PEEL = 2
        PER = 2 * QB

        def batch(u):
            return u.b * 2 + u.g // QB

        with nc.Block() as block:
            @block.sync
            def _(sp):
                sp.dma_start(wq[:, :, :], io["d_wq"].rearrange("(k p) n -> p k n", p=P)).then_inc(d_w, 16)
                sp.dma_start(wk[:, :, :], io["d_wk"].rearrange("(k p) n -> p k n", p=P)).then_inc(d_w, 16)
                sp.dma_start(wv[:, :, :], io["d_wv"].rearrange("(k p) n -> p k n", p=P)).then_inc(d_w, 16)
                sp.dma_start(wo[:, :, :], io["d_wo"].rearrange("(k p) n -> p k n", p=P)).then_inc(d_w, 16)

                def load(u):
                    if u.g == 0:
                        split.load(sp, u.b, u.peeled and u.b == 0, u.peeled and u.b == 0)
                skewed(sp, B // 2, PER, [(load, 0)], PEEL)

            @block.gpsimd
            def _(pool):
                pool.memset(mask[:, :, :], 0.0).then_inc(s_cst, 1)
                pool.memset(identb[:, :], 0.0).then_inc(s_cst, 1)
                pool.memset(kd[:, :, :, :], 0.0).then_inc(s_cst, 1)
                pool.memset(v[:, :, :, :], 1.0).then_inc(s_cst, 1)
                pool.wait_ge(s_cst, 4)
                pool.affine_select(out=mask[:, :, :], in_=mask[:, :, :], compare_op=ALU.is_ge, fill=-1e30,
                                   base=0, pattern=[[0, HKV], [-1, P]], channel_multiplier=1).then_inc(s_cst, 1)
                pool.affine_select(out=identb[:, :], in_=identb[:, :], compare_op=ALU.not_equal, fill=1.0,
                                   base=0, pattern=[[-1, P]], channel_multiplier=1).then_inc(s_cst, 1)

                def low(u):
                    if u.g == 5:
                        split.low(pool, u.b)
                skewed(pool, B // 2, PER, [(low, 0)], PEEL)

            @block.tensor
            def _(pe):
                pe.sem_inc(s_o, 1)
                pe.wait_ge(d_w, 64)
                pe.wait_ge(s_cst, 6)

                def project(u):
                    b, par, t = batch(u), u.g // QB, u.g % QB
                    if t == 0:
                        pe.wait_ge(s_xs, b + 1)
                        if u.before(QB):
                            pe.wait_ge(s_q, b)
                    for k in range(CB):
                        pe.matmul(bQ[:, t * P:(t + 1) * P], wq[:, k, t * P:(t + 1) * P], xs[:, par, k, :],
                                  start=(k == 0), stop=(k == CB - 1))
                    if t < QB - 1:
                        return
                    if u.before(QB):
                        pe.wait_ge(s_k, b)
                    for k in range(CB):
                        pe.matmul(bK[:, 0:P], wk[:, k, :], xs[:, par, k, :], start=(k == 0), stop=(k == CB - 1))
                    for k in range(CB):
                        mm = pe.matmul(bK[:, P:P + HKV * HD], xs[:, par, k, :], wv[:, k, :],
                                       start=(k == 0), stop=(k == CB - 1))
                    mm.then_inc(s_mm, 1)

                def scores(u):
                    t, par = u.g % QB, u.g // QB
                    pe.wait_ge(s_q, batch(u) + 1)
                    pe.wait_ge(s_k, batch(u) + 1)
                    if u.before(2):
                        pe.wait_ge(s_sub, u.n - 1)
                    pe.matmul(bS[u.g % 2][:, :], qt[:, par, t * P:(t + 1) * P],
                              kd[:, par, :, :].rearrange("p h k -> p (h k)"), start=True, stop=False)
                    pe.matmul(bS[u.g % 2][:, :], identb[:, :], mask[:, :, :].rearrange("p h k -> p (h k)"),
                              start=False, stop=True).then_inc(s_s, 1)

                def turn(u):
                    pe.wait_ge(s_ex, u.n + 1)
                    if u.before(2):
                        pe.wait_ge(s_cp, u.n - 1)
                    for h in range(HKV):
                        mm = pe.transpose(bT[u.g % 2][:, h * P:(h + 1) * P], sb_[:, u.g % 2, h, :], ident[:, :])
                    mm.then_inc(s_tp, 1)

                def context(u):
                    t, par = u.g % QB, u.g // QB
                    pe.wait_ge(s_cp, u.n + 1)
                    if t == 0 and u.before(QB):
                        pe.wait_ge(s_cn, batch(u))
                    for h in range(HKV):
                        at = (t * HKV + h) * (HD + 1)
                        mm = pe.matmul(bC[:, at:at + HD + 1], pt[:, u.g % 2, h, :], v[:, par, h, :],
                                       start=True, stop=True)
                    mm.then_inc(s_c, 1)

                def turn_context(u):
                    if u.g % QB != QB - 1:
                        return
                    b = batch(u)
                    pe.wait_ge(s_cn, b + 1)
                    pe.wait_ge(s_x, b + 1)
                    for k in range(CB):
                        mm = pe.transpose(bF[:, k * P:(k + 1) * P], cx[:, k * P:(k + 1) * P], ident[:, :])
                    mm.then_inc(s_ct, 1)

                def out(u):
                    if u.g % QB != QB - 1:
                        return
                    b = batch(u)
                    pe.wait_ge(s_cc, b + 1)
                    for k in range(CB):
                        mm = pe.matmul(bF[:, C:2 * C], cxt[:, k, :], wo[:, k, :], start=(k == 0), stop=(k == CB - 1))
                    mm.then_inc(s_o, 1)
                skewed(pe, B // 2, PER, [(scores, 7), (turn, 8), (context, 9), (turn_context, 11), (out, 12), (project, 2)], PEEL)

            @block.scalar
            def _(act):
                def columns(u):
                    if u.g % QB:
                        return
                    b, par = batch(u), u.g // QB
                    if u.before(2 * QB):
                        act.wait_ge(s_mm, b - 1)
                    act.activation(xs[:, par, :, :], XT[:, :, bass.ds(b * S, S)], ACT.Copy).then_inc(s_xs, 1)

                def queries(u):
                    if u.g % QB != QB - 1:
                        return
                    b, par = batch(u), u.g // QB
                    act.wait_ge(s_mm, b + 1)
                    if u.before(2 * QB):
                        act.wait_ge(s_s, QB * (b - 1))
                    act.activation(qt[:, par, :], bQ[:, :], ACT.Copy).then_inc(s_q, 1)

                def exps(u):
                    act.wait_ge(s_sub, u.n + 1)
                    act.activation(sb_[:, u.g % 2, :, :], sb_[:, u.g % 2, :, :], ACT.Exp,
                                   scale=float(HD) ** -0.5).then_inc(s_ex, 1)

                def turned(u):
                    act.wait_ge(s_tp, u.n + 1)
                    if u.before(2):
                        act.wait_ge(s_c, u.n - 1)
                    act.activation(pt[:, u.g % 2, :, :], bT[u.g % 2][:, :].rearrange("p (h k) -> p h k", h=HKV),
                                   ACT.Copy).then_inc(s_cp, 1)

                def context(u):
                    if u.g % QB != QB - 1:
                        return
                    act.wait_ge(s_ct, batch(u) + 1)
                    act.wait_ge(s_o, batch(u) + 1)
                    act.activation(cxt[:, :, :], bF[:, 0:C].rearrange("p (k s) -> p k s", k=CB),
                                   ACT.Copy).then_inc(s_cc, 1)

                def high(u):
                    if u.g == 4:
                        split.high(act, u.b)
                skewed(act, B // 2, PER, [(exps, 8), (queries, 3), (columns, 0), (turned, 8), (context, 11), (high, 0)], PEEL)

            @block.vector
            def _(dve):
                dve.sem_inc(s_x, 1)
                quant.constants(dve, col, cols).then_inc(s_const, 1)
                dve.wait_ge(s_const, 1)
                dve.wait_ge(s_cst, 4)

                def keys(u):
                    if u.g % QB != QB - 1:
                        return
                    b, par = batch(u), u.g // QB
                    dve.wait_ge(s_mm, b + 1)
                    if u.before(2 * QB):
                        dve.wait_ge(s_c, QB * (b - 1))
                    for h in range(HKV):
                        rows = slice(h * PAD, (h + 1) * PAD)
                        dve.tensor_copy(kd[rows, par, h, :], bK[rows, 0:P])
                    dve.tensor_copy(v[:, par, :, 0:HD],
                                    bK[:, P:P + HKV * HD].rearrange("p (h d) -> p h d", h=HKV)).then_inc(s_k, 1)

                def maxima(u):
                    dve.wait_ge(s_s, u.n + 1)
                    bank = bS[u.g % 2][:, :].rearrange("p (h k) -> p h k", h=HKV)
                    dve.tensor_reduce(neg[:, u.g % 2, :], bank, AX.X, ALU.max).then_inc(s_mx, 1)
                    dve.wait_ge(s_mx, u.n + 1)
                    if u.before(2):
                        dve.wait_ge(s_tp, u.n - 1)
                    dve.tensor_tensor(sb_[:, u.g % 2, :, :], bank,
                                      neg[:, u.g % 2, :].unsqueeze(2).to_broadcast([P, HKV, P]),
                                      ALU.subtract).then_inc(s_sub, 1)

                def normal(u):
                    if u.g % QB != QB - 1:
                        return
                    b = batch(u)
                    dve.wait_ge(s_c, u.n + 1)
                    c = bC[:, 0:HQ * (HD + 1)].rearrange("p (t h d) -> p t h d", t=QB, h=HKV)
                    dve.reciprocal(rec[:, :, :], c[:, :, :, HD]).then_inc(s_rc, 1)
                    dve.wait_ge(s_rc, b + 1)
                    if u.before(QB):
                        dve.wait_ge(s_ct, b)
                    dve.tensor_tensor(cx[:, :].rearrange("p (h t d) -> p t h d", h=HKV, t=QB), c[:, :, :, 0:HD],
                                      rec[:, :, :].unsqueeze(3).to_broadcast([P, QB, HKV, HD]),
                                      ALU.mult).then_inc(s_cn, 1)

                def residual(u):
                    if u.g % QB != QB - 1:
                        return
                    b = batch(u)
                    dve.wait_ge(s_o, b + 2)
                    x = X[:, bass.ds(b, 1), :].rearrange("p a c -> p (a c)")
                    dve.tensor_tensor(x, x, bF[:, C:2 * C], ALU.add).then_inc(s_x, 1)

                def centre(u):
                    if u.g == 2:
                        split.centre(dve, u.b, u.b_par)
                skewed(dve, B // 2, PER, [(keys, 3), (normal, 10), (residual, 13), (maxima, 7), (centre, 0)], PEEL)
                dve.wait_ge(s_x, B + 1)


class Split:

    def __init__(self, tag, cross, dst, nc, io, sem, sbuf, ctx, buffers=1):
        self.buffers = buffers
        self.cross, self.io = cross, io
        self.whi, self.wlo, self.phi, self.plo, self.fold = dst
        self.st = sbuf(ctx, tag + "st", [P, buffers, CB, UW], F32)
        self.pst = sbuf(ctx, tag + "pst", [P, 2, C], F32)
        self.mean = sbuf(ctx, tag + "mean", [P, CB, 4], F32)
        self.d_w = [sem(f"{tag}dw{k}") for k in range(buffers)]
        (self.d_p, self.s_scl, self.s_sum, self.s_avg, self.s_ctr, self.s_hi, self.s_lo, self.s_phi,
         self.s_plo) = (sem(f"{tag}{n}") for n in ("dp", "scl", "sum", "avg", "ctr", "hi", "lo", "phi", "plo"))

    def staged(self, g):
        k, turn = (0, g) if self.buffers == 1 else (g % self.buffers, g // self.buffers)
        return self.st[:, k, :, :], k, turn

    def load(self, sp, g, first, first_rows):
        st, place, _ = self.staged(g)
        if not first:
            sp.wait_ge(self.s_lo, g - self.buffers + 1)
        sp.dma_start(st, self.io["wcross" if self.cross else "wself"][bass.ds(g, 1), :, :].rearrange(
            "a (k p) n -> p (a k) n", p=P)).then_inc(self.d_w[place], 16)
        if not first_rows:
            sp.wait_ge(self.s_plo, g)
        sp.dma_start(self.pst[:, :, :], self.io["wproj"][int(self.cross), bass.ds(2 * g, 2), :, :].rearrange(
            "h p n -> p h n")).then_inc(self.d_p, 16)

    def centre(self, dve, g, odd):
        st, place, turn = self.staged(g)
        if self.buffers > 1 and g:
            dve.wait_ge(self.s_ctr, g)
        dve.wait_ge(self.d_w[place], 16 * turn + 16)
        heads = 2 if odd else 4
        for k in range(CB):
            if odd and self.cross:
                continue
            parts = ((0, UW, 3 if self.cross else 0),) if not odd else ((0, 2 * D, 1), (2 * D, UW, 2))
            for a, z, j in parts:
                ins = dve.tensor_scalar(st[:, k, a:z], st[:, k, a:z], self.fold[:, j, k:k + 1], None, ALU.mult)
        if odd and self.cross:
            dve.sem_inc(self.s_scl, 1)
        else:
            ins.then_inc(self.s_scl, 1)
        dve.wait_ge(self.s_scl, g + 1)
        hd = st[:, :, 0:heads * D].rearrange("p k (h d) -> p k h d", d=D)
        mean = self.mean[:, :, 0:heads]
        dve.tensor_reduce(mean, hd, AX.X, ALU.add).then_inc(self.s_sum, 1)
        dve.wait_ge(self.s_sum, g + 1)
        dve.tensor_scalar(mean, mean, -1.0 / D, None, ALU.mult).then_inc(self.s_avg, 1)
        dve.wait_ge(self.s_avg, g + 1)
        dve.tensor_tensor(hd, hd, mean.unsqueeze(3).to_broadcast([P, CB, heads, D]), ALU.add).then_inc(self.s_ctr, 1)

    def high(self, act, g):
        at = bass.ds(g, 1)
        st, place, turn = self.staged(g)
        act.wait_ge(self.s_ctr, g + 1)
        act.activation(self.whi[:, at, :, :], st.unsqueeze(1), ACT.Copy).then_inc(self.s_hi, 1)
        act.wait_ge(self.d_p, 16 * g + 16)
        act.activation(self.phi[:, at, :, :], self.pst[:, :, :].unsqueeze(1), ACT.Copy).then_inc(self.s_phi, 1)

    def low(self, pool, g):
        at = bass.ds(g, 1)
        st, place, turn = self.staged(g)
        pool.wait_ge(self.s_hi, g + 1)
        pool.tensor_tensor(self.wlo[:, at, :, :], st.unsqueeze(1), self.whi[:, at, :, :].bitcast(F32),
                           ALU.subtract).then_inc(self.s_lo, 1)
        pool.wait_ge(self.s_phi, g + 1)
        pool.tensor_tensor(self.plo[:, at, :, :], self.pst[:, :, :].unsqueeze(1), self.phi[:, at, :, :].bitcast(F32),
                           ALU.subtract).then_inc(self.s_plo, 1)


def quantise(dve, link, y, p2, t, m):
    link(dve.tensor_scalar(y, y, FP8_MAX, -FP8_MAX, ALU.min, ALU.max))
    link(dve.tensor_scalar(p2.bitcast(U16), y.bitcast(U16), 0x7F80, None, ALU.bitwise_and))
    link(dve.tensor_scalar(m, p2, FP8_MIN_NORMAL, ROUND, ALU.max, ALU.mult))
    return dve.tensor_tensor(t, y, m, ALU.add)


class Quant:

    def __init__(self, ctx, sbuf):
        self.whi = sbuf(ctx, "whi", [P, G, CB, UW], F32R)
        self.wlo = sbuf(ctx, "wlo", [P, G, CB, UW], F32R)
        self.phi = sbuf(ctx, "phi", [P, G, 2, C], F32R)
        self.plo = sbuf(ctx, "plo", [P, G, 2, C], F32R)
        self.fold = sbuf(ctx, "fold", [P, 4, CB], F32)
        self.inv = sbuf(ctx, "inv", [P, 4, CB], F32)
        self.invsm = sbuf(ctx, "invsm", [P, 4 * G], F32)
        self.aff = sbuf(ctx, "aff", [P, 2, 4], F32)
        self.pscale = sbuf(ctx, "pscale", [P, 1], F32)
        self.dst = (self.whi, self.wlo, self.phi, self.plo, self.fold)

    def constants(self, dve, col, cols):
        for j, (si, sw) in enumerate((("sq", "wsq"), ("sk", "wsk"), ("sv", "wsv"), ("sqx", "wsqx"))):
            dve.tensor_scalar(self.fold[:, j, :], cols(si), col(sw), None, ALU.mult)
            dve.reciprocal(self.inv[:, j, :], cols(si))
        dve.reciprocal(self.invsm[:, :], cols("smooth"))
        dve.tensor_scalar(self.pscale[:, :], col("pin"), col("pw"), None, ALU.mult)
        for h, names in enumerate((("qw", "qb", "kw", "kb"), ("qxw", "qxb", "kxw", "kxb"))):
            for j, name in enumerate(names):
                k = (float(D) ** -0.5 if j < 2 else 1.0) * (1.0 if j % 2 else float(D) ** 0.5)
                ins = dve.tensor_scalar(self.aff[:, h, j:j + 1], col(name), k, None, ALU.mult)
        return ins


def quant_layer(quant, nc, io, sem, sbuf, **args):
    args = dict(nc=nc, io=io, sem=sem, sbuf=sbuf, **args)
    XT, cols, col = args["XT"], args["cols"], args["col"]
    ctx = ExitStack()
    with ctx:
        xq = sbuf(ctx, "xq", [P, 4, CB, TOK], BF16)
        s_y, s_t, s_z, s_link = sem("e_y"), sem("e_t"), sem("e_z"), sem("e_link")
        with ExitStack() as inner:
            lnx = sbuf(inner, "lnx", [P, B, C], F32)
            norm_layer("ln", dst=lnx, **args)
        with ExitStack() as inner:
            y = sbuf(inner, "y0", [P, 2, TOK], BF16)
            p2 = sbuf(inner, "p20", [P, 2, TOK], BF16)
            m = sbuf(inner, "m0", [P, 2, TOK], BF16)
            t = sbuf(inner, "t0", [P, 2, TOK], F32)
            with nc.Block() as block:
                @block.scalar
                def _(act):
                    for k in range(CB):
                        act.activation(XT[:, k, :], XT[:, k, :], ACT.Identity, bias=col("lnb", k), scale=col("lnw", k)
                                       ).then_inc(s_y, 1)
                    act.wait_ge(s_y, CB)
                    for n in range(4 * CB):
                        if n >= 2:
                            act.wait_ge(s_t, n - 1)
                        act.activation(y[:, n % 2, :], XT[:, n % CB, :], ACT.Copy,
                                       scale=quant.inv[:, n // CB, n % CB:n % CB + 1]).then_inc(s_y, 1)

                @block.vector
                def _(dve):
                    link = Links(dve, s_link)
                    for n in range(4 * CB):
                        dve.wait_ge(s_y, CB + n + 1)
                        if n >= 2:
                            dve.wait_ge(s_z, n - 1)
                        quantise(dve, link, y[:, n % 2, :], p2[:, n % 2, :], t[:, n % 2, :], m[:, n % 2, :]
                                 ).then_inc(s_t, 1)

                @block.gpsimd
                def _(pool):
                    for n in range(4 * CB):
                        pool.wait_ge(s_t, n + 1)
                        pool.tensor_tensor(xq[:, n // CB, n % CB, :], t[:, n % 2, :], m[:, n % 2, :],
                                           ALU.subtract).then_inc(s_z, 1)
                    pool.wait_ge(s_z, 4 * CB)
        split = Split("xs_", True, quant.dst, nc, io, sem, sbuf, ctx, buffers=2)
        d_c = sem("cross_dc")
        for cross in (False, True):
            attention_pass(cross, xq, quant, split, d_c, **args)


def attention_pass(cross, xq, quant, split, d_c, nc, io, sem, sbuf, X, XT, small, ident, ps, col, cols):
    tag = "cross_" if cross else "self_"
    ctx = ExitStack()
    NQ = 1 if cross else 3
    QW = 2 * D
    fold, invsm, aff, pscale = quant.fold, quant.invsm, quant.aff, quant.pscale
    whi, wlo, phi, plo = quant.whi, quant.wlo, quant.phi, quant.plo
    LEAD = 2 if cross else 0
    with ctx:
        if cross:
            chi = sbuf(ctx, "chi", [P, 2, CB, S], F32R)
            clo = sbuf(ctx, "clo", [P, 2, CB, S], F32R)
        xs = sbuf(ctx, tag + "xs", [P, 2, NQ, CB, S], F32R)
        stat = sbuf(ctx, tag + "stat", [P, 2, 12], F32)
        var = sbuf(ctx, tag + "var", [P, 2, 4], F32)
        half = sbuf(ctx, tag + "half", [P, 4], F32)
        deps = sbuf(ctx, tag + "deps", [P, 4], F32)
        HN = (4, 2)
        rstd = sbuf(ctx, tag + "rstd", [P, 2, 4], F32)
        qkv = sbuf(ctx, tag + "qkv", [P, G, 4, D], F32)
        qkt = sbuf(ctx, tag + "qkt", [P, 2, 3, S], F32)
        neg = sbuf(ctx, tag + "neg", [P, 2, 2], F32)
        pr = sbuf(ctx, tag + "pr", [P, 2, 2, S], F32)
        tot = sbuf(ctx, tag + "tot", [P, 2, 2], F32)
        rec = sbuf(ctx, tag + "rec", [P, 2, 2], F32)
        pt = sbuf(ctx, tag + "pt", [P, 2, 2 * S], F32)
        y = sbuf(ctx, tag + "y", [P, 2, 2 * S], BF16)
        m = sbuf(ctx, tag + "m", [P, 2, 2 * S], BF16)
        t = sbuf(ctx, tag + "t", [P, 2, 2 * S], F32)
        z = sbuf(ctx, tag + "z", [P, 2, 2 * S], F32R)
        names = ("cst", "xs", "chi", "clo", "proj", "stat", "var", "rstd", "qn", "tr", "qkt", "sc", "neg", "ex", "rec", "pn",
                 "tp", "pt", "o", "y", "yc", "p2", "m", "t", "z", "w", "x")
        (s_cst, s_xs, s_chi, s_clo, s_proj, s_stat, s_var, s_rstd, s_qn, s_tr, s_qkt, s_sc, s_neg, s_ex, s_rec, s_pn,
         s_tp, s_pt, s_o, s_y, s_yc, s_p2, s_m, s_t, s_z, s_w, s_x) = (sem(f"{tag}u_{n}") for n in names)
        bP, bT, bS, bR, bO, bW = ps[0:2], ps[2], ps[3:5], ps[5], ps[6], ps[7]
        PEEL = 2

        with nc.Block() as block:
            @block.sync
            def _(sp):
                if not cross:
                    sp.dma_start(XT[:, :, :], io["ctxT"].rearrange("(k p) n -> p k n", p=P)).then_inc(d_c, 16)
                    split.load(sp, 0, True, True)
                else:
                    for g in range(1, G):
                        split.load(sp, g, g < split.buffers, False)

            @block.tensor
            def _(pe):
                pe.wait_ge(s_cst, 3)

                def project(u):
                    xb, bank, odd = xs[:, u.b_par, :, :, :], bP[u.g % 2], u.g % 2
                    if u.g == 0:
                        pe.wait_ge(s_xs, u.b + 1)
                        if cross:
                            pe.wait_ge(s_clo, u.b + 1)
                    if u.before(2):
                        pe.wait_ge(s_qn, u.n - 1)
                    if cross and u.peeled and u.n < G:
                        pe.wait_ge(split.s_lo, u.n + 1)
                    if odd and cross:
                        for k in range(CB):
                            hi, lo = chi[:, u.b_par, k, :], clo[:, u.b_par, k, :]
                            pe.matmul(bank[:, :], hi, whi[:, u.g, k, :], start=(k == 0), stop=False)
                            pe.matmul(bank[:, :], hi, wlo[:, u.g, k, :], start=False, stop=False)
                            mm = pe.matmul(bank[:, :], lo, whi[:, u.g, k, :], start=False, stop=(k == CB - 1))
                    else:
                        for a, e, j in ((0, QW, 1), (QW, UW, 2)) if odd else ((0, UW, 0),):
                            for k in range(CB):
                                pe.matmul(bank[:, a:e], xb[:, j, k, :], whi[:, u.g, k, a:e], start=(k == 0), stop=False)
                                mm = pe.matmul(bank[:, a:e], xb[:, j, k, :], wlo[:, u.g, k, a:e], start=False,
                                               stop=(k == CB - 1))
                    mm.then_inc(s_proj, 1)

                def turn_qk(u):
                    pe.wait_ge(s_qn, u.n + 2 - u.g % 2)
                    if u.before(1):
                        pe.wait_ge(s_qkt, u.n)
                    pair, w = u.g - u.g % 2, u.g % 2
                    for h, src in enumerate((qkv[:, pair, 2 * w, :], qkv[:, pair, 2 * w + 1, :], qkv[:, pair + 1, w, :])):
                        mm = pe.transpose(bT[:, h * S:(h + 1) * S], src, ident[:, :])
                    mm.then_inc(s_tr, 1)

                def scores(u):
                    pe.wait_ge(s_qkt, u.n + 1)
                    if u.before(2):
                        pe.wait_ge(s_ex, u.n - 1)
                    for h in range(2):
                        mm = pe.matmul(bS[u.g % 2][:, h * S:(h + 1) * S], qkt[:, u.g % 2, h, :], qkt[:, u.g % 2, 2, :],
                                       start=True, stop=True)
                    mm.then_inc(s_sc, 1)

                def turn_p(u):
                    pe.wait_ge(s_pn, u.n + 1)
                    if u.before(1):
                        pe.wait_ge(s_pt, u.n)
                    for h in range(2):
                        mm = pe.transpose(bR[:, h * S:(h + 1) * S], pr[:, u.g % 2, h, :], ident[:, :])
                    mm.then_inc(s_tp, 1)

                def values(u):
                    pe.wait_ge(s_pt, u.n + 1)
                    if u.before(1):
                        pe.wait_ge(s_y, u.n)
                    pe.matmul(bO[:, 0:2 * S], qkv[:, u.g | 1, 2 + u.g % 2, :], pt[:, u.g % 2, :], start=True, stop=True).then_inc(s_o, 1)

                def output(u):
                    pe.wait_ge(s_z, u.n + 1)
                    if u.g == 0 and u.before(G):
                        pe.wait_ge(s_x, u.b)
                    if cross and u.peeled and u.n < G:
                        pe.wait_ge(split.s_plo, u.n + 1)
                    for h in range(2):
                        for w in (phi, plo):
                            mm = pe.matmul(bW[:, 0:C], z[:, u.g % 2, h * S:(h + 1) * S], w[:, u.g, h, :],
                                           start=(u.g == 0 and h == 0 and w is phi),
                                           stop=(u.g == G - 1 and h == 1 and w is plo))
                    mm.then_inc(s_w, 1)
                skewed(pe, B, G, [(project, LEAD), (scores, LEAD + 3), (values, LEAD + 6), (turn_qk, LEAD + 2), (turn_p, LEAD + 5),
                                  (output, LEAD + 8)], PEEL)

            @block.scalar
            def _(act):
                def columns(u):
                    if u.g:
                        return
                    if u.before(2 * G):
                        act.wait_ge(s_proj, (u.b - 1) * G)
                    j = slice(3, 4) if cross else slice(0, 3)
                    act.activation(xs[:, u.b_par, :, :, :], xq[:, j, :, bass.ds(u.b * S, S)], ACT.Copy).then_inc(s_xs, 1)
                    if cross:
                        if u.peeled and u.b == 0:
                            act.wait_ge(d_c, 16)
                        act.activation(chi[:, u.b_par, :, :], XT[:, :, bass.ds(u.b * S, S)], ACT.Copy).then_inc(s_chi, 1)

                def splitting(u):
                    if u.peeled and u.n < G:
                        split.high(act, u.n)

                def turned_qk(u):
                    act.wait_ge(s_tr, u.n + 1)
                    if u.before(2):
                        act.wait_ge(s_sc, u.n - 1)
                    a = aff[:, int(cross), :]
                    act.activation(qkt[:, u.g % 2, 0:2, :], bT[:, 0:2 * S].rearrange("p (h s) -> p h s", h=2),
                                   ACT.Identity, bias=a[:, 1:2], scale=a[:, 0:1])
                    act.activation(qkt[:, u.g % 2, 2, :], bT[:, 2 * S:3 * S], ACT.Identity, bias=a[:, 3:4],
                                   scale=a[:, 2:3]).then_inc(s_qkt, 1)

                def exps(u):
                    act.wait_ge(s_neg, u.n + 1)
                    if u.before(2):
                        act.wait_ge(s_tp, u.n - 1)
                    for h in range(2):
                        ins = act.activation(pr[:, u.g % 2, h, :], bS[u.g % 2][:, h * S:(h + 1) * S], ACT.Exp,
                                             bias=neg[:, u.g % 2, h:h + 1], accum_out=tot[:, u.g % 2, h:h + 1])
                    ins.then_inc(s_ex, 1)

                def turned_p(u):
                    act.wait_ge(s_tp, u.n + 1)
                    if u.before(2):
                        act.wait_ge(s_o, u.n - 1)
                    act.activation(pt[:, u.g % 2, :], bR[:, 0:2 * S], ACT.Copy).then_inc(s_pt, 1)

                def scaled(u):
                    act.wait_ge(s_o, u.n + 1)
                    if u.before(2):
                        act.wait_ge(s_t, u.n - 1)
                    for h in range(2):
                        head = 2 * G * int(cross) + 2 * u.g + h
                        ins = act.activation(y[:, u.g % 2, h * S:(h + 1) * S], bO[:, h * S:(h + 1) * S], ACT.Copy,
                                             scale=invsm[:, head:head + 1])
                    ins.then_inc(s_y, 1)
                stages = [(columns, LEAD), (scaled, LEAD + 7), (exps, LEAD + 4), (turned_qk, LEAD + 2), (turned_p, LEAD + 5)]
                if cross:
                    stages = [(columns, LEAD - 1)] + stages[1:] + [(splitting, 0)]
                skewed(act, B, G, stages, PEEL)

            @block.gpsimd
            def _(pool):
                pool.memset(half[:, :], -0.5).then_inc(s_cst, 1)
                pool.memset(rstd[:, :, :], 1.0).then_inc(s_cst, 1)
                pool.memset(deps[:, :], D * LN_EPS).then_inc(s_cst, 1)
                pool.wait_ge(s_cst, 3)

                def normalise(u):
                    pool.wait_ge(s_rec, u.n + 1)
                    pool.tensor_tensor(pr[:, u.g % 2, :, :], pr[:, u.g % 2, :, :],
                                       rec[:, u.g % 2, :].unsqueeze(2).to_broadcast([P, 2, S]), ALU.mult).then_inc(s_pn, 1)

                def deviation(u):
                    pool.wait_ge(s_stat, u.n + 1)
                    v = var[:, u.g % 2, :]
                    w = HN[u.g % 2]
                    pool.tensor_tensor(v[:, 0:w], stat[:, u.g % 2, 2:3 * w:3], deps[:, 0:w], ALU.add).then_inc(s_var, 1)
                    pool.wait_ge(s_var, u.n + 1)
                    if u.before(2):
                        pool.wait_ge(s_qn, u.n - 1)
                    pool.tensor_tensor(rstd[:, u.g % 2, 0:w], v[:, 0:w], half[:, 0:w], ALU.pow).then_inc(s_rstd, 1)

                def rounded(u):
                    pool.wait_ge(s_t, u.n + 1)
                    if u.before(2):
                        pool.wait_ge(s_w, u.n - 1)
                    pool.tensor_tensor(z[:, u.g % 2, :], t[:, u.g % 2, :], m[:, u.g % 2, :], ALU.subtract).then_inc(s_z, 1)

                def context_low(u):
                    if u.g == 0:
                        at = bass.ds(u.b * S, S)
                        pool.wait_ge(s_chi, u.b + 1)
                        pool.tensor_tensor(clo[:, u.b_par, :, :], XT[:, :, at], chi[:, u.b_par, :, :].bitcast(F32),
                                           ALU.subtract).then_inc(s_clo, 1)

                def splitting(u):
                    if u.peeled and u.n < G:
                        split.low(pool, u.n)
                stages = [(rounded, LEAD + 8), (deviation, LEAD), (normalise, LEAD + 4)]
                if cross:
                    stages += [(context_low, LEAD - 1), (splitting, 0)]
                skewed(pool, B, G, stages, PEEL)

            @block.vector
            def _(dve):
                dve.wait_ge(s_cst, 3)

                def statistics(u):
                    dve.wait_ge(s_proj, u.n + 1)
                    if u.before(2):
                        dve.wait_ge(s_var, u.n - 1)
                    for h in range(HN[u.g % 2] // 2):
                        pair = bP[u.g % 2][:, h * QW:(h + 1) * QW].rearrange("p (h d) -> p d h", h=2)
                        ins = dve.bn_stats(stat[:, u.g % 2, 6 * h:6 * h + 6], pair)
                    ins.then_inc(s_stat, 1)

                def apply(u):
                    dve.wait_ge(s_rstd, u.n + 1)
                    if u.before(G):
                        dve.wait_ge(s_o, u.n - u.g % 2 - G + 2)
                    dve.tensor_tensor(qkv[:, u.g, :, :], bP[u.g % 2][:, :].rearrange("p (h d) -> p h d", h=4),
                                      rstd[:, u.g % 2, :].unsqueeze(2).to_broadcast([P, 4, D]), ALU.mult).then_inc(s_qn, 1)

                def maxima(u):
                    dve.wait_ge(s_sc, u.n + 1)
                    if u.before(2):
                        dve.wait_ge(s_ex, u.n - 1)
                    dve.tensor_reduce(neg[:, u.g % 2, :], bS[u.g % 2][:, 0:2 * S].rearrange("p (h s) -> p h s", h=2),
                                      AX.X, ALU.max, negate=True).then_inc(s_neg, 1)

                def reciprocals(u):
                    dve.wait_ge(s_ex, u.n + 1)
                    if u.before(2):
                        dve.wait_ge(s_pn, u.n - 1)
                    dve.reciprocal(rec[:, u.g % 2, :], tot[:, u.g % 2, :]).then_inc(s_rec, 1)

                def clamp(u):
                    dve.wait_ge(s_y, u.n + 1)
                    dve.tensor_scalar(y[:, u.g % 2, :], y[:, u.g % 2, :], FP8_MAX, -FP8_MAX, ALU.min, ALU.max
                                      ).then_inc(s_yc, 1)

                def power(u):
                    dve.wait_ge(s_yc, u.n + 1)
                    if u.before(2):
                        dve.wait_ge(s_z, u.n - 1)
                    dve.tensor_scalar(m[:, u.g % 2, :].bitcast(U16), y[:, u.g % 2, :].bitcast(U16), 0x7F80, None,
                                      ALU.bitwise_and).then_inc(s_p2, 1)

                def magic(u):
                    dve.wait_ge(s_p2, u.n + 1)
                    dve.tensor_scalar(m[:, u.g % 2, :], m[:, u.g % 2, :], FP8_MIN_NORMAL, ROUND, ALU.max, ALU.mult
                                      ).then_inc(s_m, 1)

                def rounding(u):
                    dve.wait_ge(s_m, u.n + 1)
                    dve.tensor_tensor(t[:, u.g % 2, :], y[:, u.g % 2, :], m[:, u.g % 2, :], ALU.add).then_inc(s_t, 1)

                def residual(u):
                    if u.g != G - 1:
                        return
                    dve.wait_ge(s_w, u.n + 1)
                    x = X[:, bass.ds(u.b, 1), :].rearrange("p a c -> p (a c)")
                    dve.scalar_tensor_tensor(x, bW[:, 0:C], pscale[:, 0:1], x, ALU.mult, ALU.add).then_inc(s_x, 1)

                def splitting(u):
                    if u.peeled and u.n < G:
                        split.centre(dve, u.n, u.g % 2)
                stages = [(apply, 1), (clamp, 7), (statistics, 0), (power, 7), (reciprocals, 4), (magic, 7),
                          (maxima, 3), (rounding, 7), (residual, 8)]
                stages = [(stage, LEAD + lag) for stage, lag in stages]
                skewed(dve, B, G, stages + [(splitting, 0)] if cross else stages, PEEL)
                dve.wait_ge(s_x, B)


def moe_tiles():
    return -(-((2 * TOK + E * (P - 1)) // P) // 4) * 4


def moe_layer(nc, io, sem, sbuf, X, XT, small, ident, ps, col, cols):
    ctx = ExitStack()
    NT = moe_tiles()
    XB = 4
    NG = 4
    sorted_x, sorted_y = io["sorted_x"], io["sorted_y"]
    with ctx:
        wg = sbuf(ctx, "wg", [P, CB, E], F32)
        w = [sbuf(ctx, f"w{i}", [P, E, 2 * I], F32) for i in range(3)]
        zero = sbuf(ctx, "zero", [P, C], F32)
        xin = sbuf(ctx, "f_xin", [P, XB, C], F32)
        xt = sbuf(ctx, "f_xt", [P, 2, C], F32)
        sa = sbuf(ctx, "sa", [P, 2, I], F32)
        h = sbuf(ctx, "h", [P, 2, I], F32)
        ht = sbuf(ctx, "ht", [P, 2, I], F32)
        ys = sbuf(ctx, "ys", [P, XB, C], F32)
        lg = sbuf(ctx, "lg", [P, B, E], F32)
        ex = sbuf(ctx, "ex", [P, B, E], F32)
        p_ = sbuf(ctx, "p_", [P, B, E], F32)
        one = sbuf(ctx, "one", [P, B, E], F32)
        two = sbuf(ctx, "two", [P, B, E], F32)
        mask = sbuf(ctx, "f_mask", [P, B, E], F32)
        mx = sbuf(ctx, "f_mx", [P, B], F32)
        pm = sbuf(ctx, "f_pm", [P, B], F32)
        wt = sbuf(ctx, "wt", [P, 2, B], F32)
        prio = sbuf(ctx, "f_prio", [P, E], F32)
        tri = sbuf(ctx, "f_tri", [P, P], F32)
        ones = sbuf(ctx, "f_ones", [P, P], F32)
        count = sbuf(ctx, "f_count", [P, E, B], F32)
        upto = sbuf(ctx, "f_upto", [P, 1 + E * B], F32)
        tiles = sbuf(ctx, "f_tiles", [P, E], F32)
        end = sbuf(ctx, "f_end", [P, E], F32)
        base = sbuf(ctx, "f_base", [P, E], F32)
        pos = sbuf(ctx, "f_pos", [P, B, E], F32)
        row = sbuf(ctx, "f_row", [P, 2, B], F32)
        rows = sbuf(ctx, "f_rows", [P, 2, B], I32)
        tile_no = sbuf(ctx, "f_tile_no", [P, NT + 1], F32)
        past = sbuf(ctx, "f_past", [P, NT + 1, E], F32)
        owner = sbuf(ctx, "f_owner", [P, NT + 1], F32)
        owners = sbuf(ctx, "f_owners", [P, NT + 1], I32)
        all_ones = sbuf(ctx, "f_all_ones", [P, E * B], F32)
        got = w[0][:, :, :].rearrange("p e n -> p (e n)").rearrange("p (j b c) -> p j b c", j=2, b=B)
        d_g, d_w, d_zero, d_sc = (sem("f_" + n) for n in ("dg", "dw", "dzero", "dsc"))
        d_x = [sem(f"f_dx{i}") for i in range(XB)]
        d_y = [sem(f"f_dy{i}") for i in range(XB)]
        d_ga = [sem(f"f_dga{i}") for i in range(NG)]
        (s_cst, s_z, s_lg, s_th, s_d, s_ex, s_mask, s_cnt, s_row, s_own, s_xt, s_xe, s_up, s_si, s_mu, s_ht, s_he,
         s_y, s_ye, s_link, s_fin) = (sem("f_" + n) for n in (
             "cst", "z", "lg", "th", "d", "ex", "mask", "cnt", "row", "own", "xt", "xe", "up", "si", "mu", "ht", "he",
             "y", "ye", "link", "fin"))
        bX, bU, bH, bY = ps[0], (ps[1:3], ps[3:5]), ps[5], ps[6:8]
        PER, PEEL = 4, 2
        TURN_X, UP, DOWN, STORE = 2, 3, 4, 5

        def tile_rows(dram, u):
            return dram[bass.ds(u.n * P, P), :]

        with nc.Block() as block:
            @block.sync
            def _(sp):
                sp.dma_start(wg[:, :, :], io["w_gate"].rearrange("(k p) n -> p k n", p=P)).then_inc(d_g, 16)
                sp.wait_ge(s_z, 1)
                sp.dma_start(sorted_x.rearrange("(p r) c -> p r c", p=P),
                             zero[:, :].unsqueeze(1).to_broadcast([P, NT, C])).then_inc(d_zero, 16)
                for e in range(E):
                    for i, (name, k) in enumerate((("w1", CB), ("w3", CB), ("w2", IB))):
                        sp.dma_start(w[i][:, e, :].rearrange("p (k n) -> p k n", k=k),
                                     io[name][e].rearrange("(k p) n -> p k n", p=P)).then_inc(d_w, 16)
                sp.wait_ge(d_sc, 2 * B * 16)

                def load(u):
                    if u.before(XB):
                        sp.wait_ge(s_xt, u.n - XB + 1)
                    sp.dma_start(xin[:, u.g, :], tile_rows(sorted_x, u)).then_inc(d_x[u.g], 16)

                def store(u):
                    sp.wait_ge(s_ye, u.n + 1)
                    sp.dma_start(tile_rows(sorted_y, u), ys[:, u.g, :]).then_inc(d_y[u.g], 16)
                skewed(sp, NT // PER, PER, [(store, STORE), (load, 0)], PEEL)

            @block.tensor
            def _(pe):
                pe.wait_ge(d_g, 16)
                for b in range(B):
                    for k in range(CB):
                        mm = pe.matmul(ps[7][:, b * E:(b + 1) * E], XT[:, k, b * S:(b + 1) * S], wg[:, k, :],
                                       start=(k == 0), stop=(k == CB - 1))
                mm.then_inc(s_lg, 1)
                pe.wait_ge(s_cst, 4)
                pe.wait_ge(s_mask, 1)
                choice = mask[:, :, :].rearrange("p b e -> p (b e)")
                pe.matmul(ps[6][:, 0:B * E], tri[:, :], choice, start=True, stop=True)
                pe.matmul(ps[6][:, B * E:2 * B * E], ones[:, :], choice, start=True, stop=True).then_inc(s_cnt, 1)
                pe.wait_ge(s_own, 1)
                pe.wait_ge(d_w, 3 * E * 16)
                loaded = [pe.alloc_register(f"expert{i}") for i in range(PER + 1)]
                expert = {}

                pe.load([loaded[PER]], owners[0:1, 0:1])
                expert[PER] = pe.snap(loaded[PER], min_val=0, max_val=E - 1)

                def experts(u):
                    if u.g == 0:
                        pe.load(loaded, owners[0:1, bass.ds(u.n, PER + 1)])
                        for i, register in enumerate(loaded):
                            expert[i] = pe.snap(register, min_val=0, max_val=E - 1)

                def turn_x(u):
                    pe.wait_ge(d_x[u.g], 16 * u.b + 16)
                    if u.before(1):
                        pe.wait_ge(s_xe, u.n)
                    for k in range(CB):
                        mm = pe.transpose(bX[:, k * P:(k + 1) * P], xin[:, u.g, k * P:(k + 1) * P], ident[:, :])
                    mm.then_inc(s_xt, 1)

                def up(u):
                    pe.wait_ge(s_xe, u.n + 1)
                    if u.before(2):
                        pe.wait_ge(s_mu, u.n - 1)
                    for i in range(2):
                        for k in range(CB):
                            mm = pe.matmul(bU[u.g % 2][i][:, :], xt[:, u.g % 2, k * P:(k + 1) * P],
                                           w[i][:, bass.ds(expert[(u.g + UP) % PER + 1], 1), k * I:(k + 1) * I], start=(k == 0), stop=(k == CB - 1))
                        mm.then_inc(s_up, 1)

                def turn_h(u):
                    pe.wait_ge(s_mu, u.n + 1)
                    if u.before(1):
                        pe.wait_ge(s_he, u.n)
                    for j in range(IB):
                        mm = pe.transpose(bH[:, j * P:(j + 1) * P], h[:, u.g % 2, j * P:(j + 1) * P], ident[:, :])
                    mm.then_inc(s_ht, 1)

                def down(u):
                    pe.wait_ge(s_he, u.n + 1)
                    if u.before(2):
                        pe.wait_ge(s_ye, u.n - 1)
                    for j in range(IB):
                        mm = pe.matmul(bY[u.g % 2][:, 0:C], ht[:, u.g % 2, j * P:(j + 1) * P],
                                       w[2][:, bass.ds(expert[(u.g + DOWN) % PER], 1), j * C:(j + 1) * C], start=(j == 0), stop=(j == IB - 1))
                    mm.then_inc(s_y, 1)
                skewed(pe, NT // PER, PER, [(experts, PER), (turn_h, DOWN), (turn_x, TURN_X), (up, UP), (down, DOWN)], PEEL)

            @block.scalar
            def _(act):
                act.wait_ge(s_lg, 1)
                act.activation(lg[:, :, :], ps[7][:, 0:B * E].rearrange("p (b e) -> p b e", e=E), ACT.Tanh,
                               scale=1.0 / SOFTCAP).then_inc(s_th, 1)
                act.wait_ge(s_d, 1)
                act.activation(ex[:, :, :], p_[:, :, :], ACT.Exp, scale=SOFTCAP).then_inc(s_ex, 1)

                def turned_x(u):
                    act.wait_ge(s_xt, u.n + 1)
                    if u.before(2):
                        act.wait_ge(s_up, 2 * u.n - 2)
                    act.activation(xt[:, u.g % 2, :], bX[:, 0:C], ACT.Copy).then_inc(s_xe, 1)

                def silu(u):
                    act.wait_ge(s_up, 2 * u.n + 1)
                    if u.before(2):
                        act.wait_ge(s_mu, u.n - 1)
                    act.activation(sa[:, u.g % 2, :], bU[u.g % 2][0][:, :], ACT.Silu).then_inc(s_si, 1)

                def turned_h(u):
                    act.wait_ge(s_ht, u.n + 1)
                    if u.before(2):
                        act.wait_ge(s_y, u.n - 1)
                    act.activation(ht[:, u.g % 2, :], bH[:, :], ACT.Copy).then_inc(s_he, 1)
                skewed(act, NT // PER, PER, [(turned_h, DOWN), (turned_x, TURN_X), (silu, UP)], PEEL)

            @block.gpsimd
            def _(pool):
                pool.memset(zero[:, :], 0.0).then_inc(s_z, 1)
                for n in range(E):
                    ins = pool.memset(prio[:, n:n + 1], float(E - n))
                ins.then_inc(s_cst, 1)
                pool.memset(ones[:, :], 1.0).then_inc(s_cst, 1)
                pool.memset(tri[:, :], 1.0).then_inc(s_cst, 1)
                pool.wait_ge(s_cst, 3)
                pool.affine_select(out=tri[:, :], in_=tri[:, :], compare_op=ALU.is_ge, fill=0.0,
                                   base=-1, pattern=[[1, P]], channel_multiplier=-1).then_inc(s_cst, 1)
                pool.wait_ge(s_row, 1)
                pool.wait_ge(d_zero, 16)
                for j in range(2):
                    for b in range(B):
                        pool.indirect_dma_start(
                            out=sorted_x, out_offset=bass.IndirectOffsetOnAxis(ap=rows[:, j, b:b + 1], axis=0),
                            in_=X[:, b, :], in_offset=None).then_inc(d_sc, 16)
                pool.wait_ge(d_sc, 2 * B * 16)
                for i in range(XB):
                    pool.wait_ge(d_y[i], 16 * NT // XB)
                for b in range(B):
                    for j in range(2):
                        pool.indirect_dma_start(
                            out=got[:, j, b, :], out_offset=None, in_=sorted_y,
                            in_offset=bass.IndirectOffsetOnAxis(ap=rows[:, j, b:b + 1], axis=0)
                        ).then_inc(d_ga[b * NG // B], 16)

            @block.vector
            def _(dve):
                link = Links(dve, s_link)
                over = lambda a: a.unsqueeze(2).to_broadcast([P, B, E])
                link(dve.memset(upto[:, 0:1], 0.0))
                link(dve.memset(all_ones[:, :], 1.0))
                link(dve.tensor_tensor_scan(tile_no[:, :], all_ones[:, 0:NT + 1], all_ones[:, 0:NT + 1], 0.0, ALU.mult, ALU.add))
                dve.wait_ge(s_th, 1)
                dve.wait_ge(s_cst, 1)
                link(dve.tensor_reduce(mx[:, :], lg[:, :, :], AX.X, ALU.max))
                dve.tensor_tensor(p_[:, :, :], lg[:, :, :], over(mx[:, :]), ALU.subtract).then_inc(s_d, 1)
                dve.wait_ge(s_ex, 1)
                link(dve.tensor_reduce(mx[:, :], ex[:, :, :], AX.X, ALU.add))
                link(dve.reciprocal(mx[:, :], mx[:, :]))
                link(dve.tensor_tensor(p_[:, :, :], ex[:, :, :], over(mx[:, :]), ALU.mult))

                def first_of_best(out, weight, a):
                    link(dve.tensor_reduce(weight, a, AX.X, ALU.max))
                    link(dve.tensor_tensor(out, a, over(weight), ALU.is_ge))
                    link(dve.tensor_tensor(out, out, prio[:, :].unsqueeze(1).to_broadcast([P, B, E]), ALU.mult))
                    link(dve.tensor_reduce(pm[:, :], out, AX.X, ALU.max))
                    link(dve.tensor_tensor(out, out, over(pm[:, :]), ALU.is_equal))

                first_of_best(one[:, :, :], wt[:, 0, :], p_[:, :, :])
                link(dve.scalar_tensor_tensor(ex[:, :, :], one[:, :, :], -4.0, p_[:, :, :], ALU.mult, ALU.add))
                first_of_best(two[:, :, :], wt[:, 1, :], ex[:, :, :])
                dve.tensor_tensor(mask[:, :, :], one[:, :, :], two[:, :, :], ALU.add).then_inc(s_mask, 1)
                dve.wait_ge(s_cnt, 1)
                link(dve.tensor_copy(count[:, :, :], ps[6][:, B * E:2 * B * E].rearrange("p (b e) -> p e b", e=E)))
                flat = count[:, :, :].rearrange("p e b -> p (e b)")
                link(dve.tensor_tensor_scan(upto[:, 1:1 + E * B], all_ones[:, :], flat, 0.0, ALU.mult, ALU.add))
                start, stop_ = upto[:, 0:E * B:B], upto[:, B:1 + E * B:B]
                link(dve.tensor_tensor(tiles[:, :], stop_, start, ALU.subtract))
                link(dve.tensor_scalar(tiles[:, :], tiles[:, :], 1.0 / P, (P / 2 - 0.5) / P, ALU.mult, ALU.add))
                link(dve.tensor_scalar(tiles[:, :], tiles[:, :], WHOLE, None, ALU.add))
                link(dve.tensor_scalar(tiles[:, :], tiles[:, :], -WHOLE, None, ALU.add))
                link(dve.tensor_tensor_scan(end[:, :], all_ones[:, 0:E], tiles[:, :], 0.0, ALU.mult, ALU.add))
                link(dve.tensor_tensor(base[:, :], end[:, :], tiles[:, :], ALU.subtract))
                link(dve.scalar_tensor_tensor(base[:, :], base[:, :], float(P), start, ALU.mult, ALU.subtract))
                before = upto[:, 0:E * B].rearrange("p (e b) -> p b e", b=B)
                link(dve.tensor_tensor(pos[:, :, :], ps[6][:, 0:B * E].rearrange("p (b e) -> p b e", e=E), before, ALU.add))
                link(dve.tensor_tensor(pos[:, :, :], pos[:, :, :], base[:, :].unsqueeze(1).to_broadcast([P, B, E]), ALU.add))
                for j, choice in enumerate((one, two)):
                    link(dve.tensor_tensor(choice[:, :, :], choice[:, :, :], pos[:, :, :], ALU.mult))
                    link(dve.tensor_reduce(row[:, j, :], choice[:, :, :], AX.X, ALU.add))
                dve.tensor_copy(rows[:, :, :], row[:, :, :]).then_inc(s_row, 1)
                link(dve.tensor_tensor(past[:, :, :], tile_no[:, :].unsqueeze(2).to_broadcast([P, NT + 1, E]),
                                       end[:, :].unsqueeze(1).to_broadcast([P, NT + 1, E]), ALU.is_gt))
                link(dve.tensor_reduce(owner[:, :], past[:, :, :], AX.X, ALU.add))
                dve.tensor_scalar(owners[:, :], owner[:, :], float(E - 1), None, ALU.min).then_inc(s_own, 1)

                def gated(u):
                    dve.wait_ge(s_si, u.n + 1)
                    dve.wait_ge(s_up, 2 * u.n + 2)
                    if u.before(2):
                        dve.wait_ge(s_ht, u.n - 1)
                    dve.tensor_tensor(h[:, u.g % 2, :], sa[:, u.g % 2, :], bU[u.g % 2][1][:, :],
                                      ALU.mult).then_inc(s_mu, 1)

                def result(u):
                    dve.wait_ge(s_y, u.n + 1)
                    if u.before(XB):
                        dve.wait_ge(d_y[u.g], 16 * u.b)
                    dve.tensor_copy(ys[:, u.g, :], bY[u.g % 2][:, 0:C]).then_inc(s_ye, 1)
                skewed(dve, NT // PER, PER, [(gated, UP), (result, DOWN)], PEEL)
                for b in range(B):
                    if b % (B // NG) == 0:
                        dve.wait_ge(d_ga[b * NG // B], 16 * 2 * B // NG)
                    link(dve.scalar_tensor_tensor(X[:, b, :], got[:, 0, b, :], wt[:, 0, b:b + 1], X[:, b, :],
                                                  ALU.mult, ALU.add))
                    dve.scalar_tensor_tensor(X[:, b, :], got[:, 1, b, :], wt[:, 1, b:b + 1], X[:, b, :],
                                             ALU.mult, ALU.add).then_inc(s_fin, 1)
                dve.wait_ge(s_fin, B)


def _launch_arrays(i):
    f = np.float32
    a = {k: np.asarray(v) for k, v in i.items()}
    io = {}
    io["xT"] = a["x"].reshape(TOK, C).T
    io["wa"] = a["L0_attn_W"].T
    rep = lambda v: np.broadcast_to(v.reshape(1, -1), (P, v.size))
    blk = lambda v: v.reshape(-1, P).T
    n = "L1_xattn_"
    small = [blk(a["L0_attn_b"])] + [blk(a[n + k]) for k in ("qln_w", "qln_b", "kln_w", "kln_b", "qxln_w", "qxln_b",
                                                            "kxln_w", "kxln_b", "ln_w", "ln_b", "q_in_scale",
                                                            "k_in_scale", "v_in_scale", "qx_in_scale", "proj_smooth")]
    small += [rep(a[n + k]) for k in ("wq_scale", "wk_scale", "wv_scale", "wqx_scale", "proj_in_scale", "proj_w_scale")]
    small += [rep(a["L0_xattn_D"]), rep(a["L0_ffn_imp_center"]), rep(a["L0_ffn_imp_slope"])]
    io["small"] = np.concatenate(small, axis=1)
    ctx = a["ctx_2048"].reshape(TOK, C)
    io["ctxR"] = ctx.T.reshape(CB, P, TOK)[:, ::-1]
    pad = np.zeros((CH, P - 1 + C), f)
    pad[:, P - 1:] = a["L0_xattn_ssm_kernel"]
    io["toep"] = np.stack([pad[:, m:m + C] for m in range(P)], axis=1)
    io["wf"] = np.concatenate([a["L0_ffn_select_weight"].transpose(1, 0, 2).reshape(C, SEL),
                               a["L0_ffn_lora_update"].transpose(1, 0, 2).reshape(C, UPD),
                               a["L0_ffn_select_mean_diff"].T], axis=1)
    io["deb"] = a["L0_ffn_debias_w"].T
    io["lw"] = np.concatenate([a["L0_ffn_lora_degen"].transpose(0, 2, 1).reshape(UPD, C), a["L0_ffn_bias_w"]])
    QB, PAD = HQ // HKV, P // HKV
    wq = np.zeros((C, QB, HKV, PAD), f)
    wq[..., :HD] = a["L1_attn_Wq"].reshape(HKV, QB, HD, C).transpose(3, 1, 0, 2)
    wk = np.zeros((C, HKV, PAD), f)
    wk[..., :HD] = a["L1_attn_Wk"].reshape(HKV, HD, C).transpose(2, 0, 1)
    io["d_wq"], io["d_wk"] = wq.reshape(C, QB * P), wk.reshape(C, P)
    io["d_wv"], io["d_wo"] = a["L1_attn_Wv"].T, a["L1_attn_Wo"].T
    pairs = lambda w, h: w.reshape(-1, 2, h * D, C)
    item = lambda *ws: np.concatenate(ws, axis=1).transpose(0, 2, 1)
    side = lambda w: w.reshape(w.shape[0], -1, C)
    kv = a[n + "w_kv_x"].reshape(2, G * D, C)
    for name, q, k, v in (("wself", a[n + "wq"], a[n + "wk"], a[n + "wv"]), ("wcross", a[n + "wqx"], kv[0], kv[1])):
        even, odd = item(side(pairs(q, 2))), item(side(pairs(k, 1)), side(pairs(v, 1)))
        io[name] = np.stack([even, odd], axis=1).reshape(G, C, UW)
    io["wproj"] = a[n + "wproj"].T.reshape(2, 2 * G, D, C)
    io["ctxT"] = ctx.T
    io["w_gate"] = a["L1_ffn_w_gate"]
    io["w1"], io["w3"], io["w2"] = a["L1_ffn_w1"], a["L1_ffn_w3"], a["L1_ffn_w2"]
    return {k: np.ascontiguousarray(v) for k, v in io.items()}


STOP = 99


def kernel(**inputs):
    import concourse.bacc as bacc
    from concourse.bass_utils import run_bass_kernel_spmd

    nc = bacc.Bacc("TRN2", target_bir_lowering=False, num_devices=1)
    arrays = _launch_arrays(inputs)
    io = {k: nc.dram_tensor(k + "_dram", v.shape, mybir.dt.from_np(v.dtype), kind="ExternalInput").ap()
          for k, v in arrays.items()}
    io["out"] = nc.dram_tensor("out_dram", (B, S, C), F32, kind="ExternalOutput").ap()
    build(nc, io, STOP)
    r = run_bass_kernel_spmd(nc, [{k + "_dram": v for k, v in arrays.items()}], core_ids=[0])
    return r.results[0]["out_dram"]
```

```python
import numpy as np
import concourse.bass as bass
from concourse import mybir
from contextlib import ExitStack

F32, F32R, BF16 = mybir.dt.float32, mybir.dt.float32r, mybir.dt.bfloat16
I32, U16 = mybir.dt.int32, mybir.dt.uint16
ACT = mybir.ActivationFunctionType
ALU = mybir.AluOpType
AX = mybir.AxisListType

B, S, C = 16, 128, 256
P = 128
CB = C // P
TOK = B * S
W512 = 512
NTG = TOK // W512
LN_EPS = 1e-5
WARM_UP = 8
CH, CD = 16, 8
NE0, NS0 = 8, 8
SEL, UPD = NE0 * NS0, NE0 * NS0
FW = SEL + UPD + NE0
HQ, HKV, HD = 16, 4, 16
G, D = 8, 128
UW = 4 * D
FP8_MAX = 448.0
FP8_MIN_NORMAL = 2.0 ** -6
ROUND = 1.5 * 2.0 ** 20
E, I = 8, 512
IB = I // P
SOFTCAP = 30.0
ROW_ID, ROW_WEIGHTS = C, C + 1
ROW = C + 16
WHOLE = 1.5 * 2.0 ** 23

SMALL = {}
_at = 0
for _name, _n in (("ab", 4), ("qw", 1), ("qb", 1), ("kw", 1), ("kb", 1), ("qxw", 1), ("qxb", 1),
                  ("kxw", 1), ("kxb", 1), ("lnw", 2), ("lnb", 2), ("sq", 2), ("sk", 2), ("sv", 2),
                  ("sqx", 2), ("smooth", 32), ("wsq", 1), ("wsk", 1), ("wsv", 1), ("wsqx", 1),
                  ("pin", 1), ("pw", 1), ("dskip", CH), ("center", NE0), ("slope", NE0)):
    SMALL[_name] = (_at, _at + _n)
    _at += _n
NSMALL = _at


class Links:

    def __init__(self, eng, sem):
        self.eng, self.sem, self.n = eng, sem, 0

    def __call__(self, ins):
        ins.then_inc(self.sem, 1)
        self.n += 1
        self.eng.wait_ge(self.sem, self.n)
        return ins


class Unit:

    def __init__(self, b, g, per, peeled, b_par, turn):
        self.b, self.g, self.n, self.peeled, self.b_par, self.turn = b, g, b * per + g, peeled, b_par, turn

    def before(self, k):
        return not self.peeled or self.n >= k


def skewed(eng, outer, per, stages, peel=1):
    def step(b, g, i=None, j=0):
        for stage, lag in stages:
            at, back = (g - lag) % per, -((g - lag) // per)
            if i is not None:
                stage(Unit(i * peel + (j - back), at, per, False, (j - back) % 2, i + (j - back) // 2))
            elif 0 <= b - back < outer:
                stage(Unit(b - back, at, per, True, (b - back) % 2, (b - back) // 2))

    loops = outer // peel - 1
    for b in range(peel):
        for g in range(per):
            step(b, g)
    if loops:
        with eng.Fori(1, loops + 1) as i:
            for j in range(peel):
                for g in range(per):
                    step(None, g, i, j)
    for b in range(peel * (loops + 1), outer):
        for g in range(per):
            step(b, g)
    for g in range(max(lag for _, lag in stages)):
        step(outer + g // per, g % per)


def build(nc, io, stop=99):
    ctx = ExitStack()
    with ctx:
        held = []

        def sem(name):
            held.append(nc.alloc_semaphore(name=name))
            return held[-1]

        def layer(f, *a, **k):
            f(*a, **k, **args)
            nc.clear_and_free_semaphores(list(held))
            held.clear()
            nc.all_engine_barrier()

        def sbuf(c, name, shape, dt):
            return c.enter_context(nc.sbuf_tensor(name, shape, dt))

        X = sbuf(ctx, "X", [P, B, C], F32)
        XT = sbuf(ctx, "XT", [P, CB, TOK], F32)
        small = sbuf(ctx, "small", [P, NSMALL], F32)
        ident = sbuf(ctx, "ident", [P, P], F32)
        row_stats = sbuf(ctx, "row_stats", [P, B, 6], F32)
        ps = [ctx.enter_context(nc.psum_tensor(f"ps{i}", [P, W512], F32)) for i in range(8)]

        def col(name, k=0):
            a = SMALL[name][0] + k
            return small[:, a:a + 1]

        def cols(name):
            return small[:, slice(*SMALL[name])]

        if stop > 5:
            io["sorted_x"] = nc.dram_tensor("sorted_x", (moe_tiles() * P, ROW), F32, kind="Internal").ap()
            io["sums"] = nc.dram_tensor("sums", (TOK + P, C), F32, kind="Internal").ap()
        args = dict(nc=nc, io=io, sem=sem, sbuf=sbuf, X=X, XT=XT, small=small, ident=ident, ps=ps,
                    col=col, cols=cols)
        with ExitStack() as conv_ctx:
            ct = sbuf(conv_ctx, "ct", [P, CB, TOK], F32)
            d_ct = nc.alloc_semaphore(name="context_loaded")
            layer(scan_layer, ct, d_ct)
            layer(norm_layer, "n0", from_channels=True)
            layer(conv_layer, ct, d_ct)
        layer(norm_layer, "n1", from_channels=True)
        if stop > 2:
            layer(routed_layer)
            layer(norm_layer, "n2")
        with ExitStack() as quant_ctx:
            quant = Quant(quant_ctx, sbuf) if stop > 3 else None
            if stop > 3:
                layer(causal_layer, row_stats, quant)
                layer(norm_layer, "n3", back=False, stats=row_stats)
            if stop > 4:
                layer(quant_layer, row_stats, quant)
        if stop > 4:
            experts = Experts(ctx, sbuf, nc) if stop > 5 else None
            layer(norm_layer, "n4", experts=experts, stats=row_stats)
        if stop > 5:
            layer(moe_layer, experts)
            layer(norm_layer, "n5", back=False, through=(io["sums"], io["out"]))
            return

        out_done = sem("out_done")
        with nc.Block() as block:
            @block.sync
            def _(sp):
                sp.dma_start(io["out"].rearrange("b t c -> t b c"), X[:, :, :]).then_inc(out_done, 16)
                sp.wait_ge(out_done, 16)


def norm_layer(tag, nc, io, sem, sbuf, X, XT, small, ident, ps, col, cols, from_channels=False,
               back=True, dst=None, eps=LN_EPS, experts=None, affine=None, through=None, stats=None):
    gate = experts and experts.gate
    dst = X if dst is None else dst
    ctx = ExitStack()
    HB = B // 2
    with ctx:
        st = stats if stats is not None else sbuf(ctx, tag + "_st", [P, B, 6], F32)
        total, diff, var, rstd, shift, power = (sbuf(ctx, f"{tag}_m{k}", [P, B], F32) for k in range(6))
        s_tok = sem(tag + "_tok")
        s_var = sem(tag + "_var")
        s_rstd = sem(tag + "_rstd")
        s_shift = sem(tag + "_shift")
        s_norm = sem(tag + "_norm")
        s_norma = sem(tag + "_norma")
        s_back = sem(tag + "_back")
        s_free = sem(tag + "_free")
        s_cst = sem(tag + "_cst")
        s_gate = sem(tag + "_gate")
        s_link = sem(tag + "_link")
        d_gate = sem(tag + "_dgate")
        d_in, d_out = [sem(f"{tag}_din{k}") for k in range(2)], sem(tag + "_dout")
        BY_DVE = HB - 2

        def tile(b):
            if from_channels:
                return ps[b // 2][:, (b % 2) * C:(b % 2 + 1) * C]
            return X[:, b, :]

        with nc.Block() as block:
            if through:
                @block.sync
                def _(sp):
                    halves = [slice(half * HB, half * HB + HB) for half in range(2)]
                    for half, h in enumerate(halves):
                        sp.dma_start(X[:, h, :], through[0][half * HB * P:(half + 1) * HB * P, :].rearrange(
                            "(b p) c -> p b c", p=P)).then_inc(d_in[half], 16)
                    for half, h in enumerate(halves):
                        sp.wait_ge(s_norm, half * BY_DVE + BY_DVE)
                        sp.wait_ge(s_norma, half * 2 + 2)
                        sp.dma_start(through[1][h, :, :].rearrange("b t c -> t b c"), X[:, h, :]).then_inc(d_out, 16)
                    sp.wait_ge(d_out, 32)

            if gate is not None:
                @block.sync
                def _(sp):
                    sp.dma_start(gate[:, :, :], io["w_gate"].rearrange("(k p) n -> p k n", p=P)).then_inc(d_gate, 16)
                    experts.load_up(sp, io, range(0, E // 2))

            @block.tensor
            def _(pe):
                if from_channels:
                    for b in range(B):
                        for k in range(CB):
                            mm = pe.transpose(tile(b)[:, k * P:(k + 1) * P], XT[:, k, b * S:(b + 1) * S], ident[:, :])
                        if b % 2:
                            mm.then_inc(s_tok, 1)

                def logits(tg):
                    pe.wait_ge(s_free, tg * CB + CB)
                    for b in range(tg * 4, tg * 4 + 4):
                        for k in range(CB):
                            mm = pe.matmul(ps[0][:, b * E:(b + 1) * E], XT[:, k, b * S:(b + 1) * S], gate[:, k, :],
                                           start=(k == 0), stop=(k == CB - 1))
                    return mm

                if back and not from_channels:
                    for _ in range(WARM_UP):
                        pe.matmul(ps[7][:, :], ident[:, :], ident[:, :].unsqueeze(1).to_broadcast([P, 4, P]),
                                  start=True, stop=True)
                if gate is not None:
                    pe.wait_ge(d_gate, 16)
                if back:
                    for tg in range(NTG):
                        half, odd = tg // 2, tg % 2
                        pe.wait_ge(s_norm, half * BY_DVE + (BY_DVE if odd else 4))
                        if odd:
                            pe.wait_ge(s_norma, half * 2 + 2)
                        for k in range(CB):
                            for j in range(4):
                                b = tg * 4 + j
                                mm = pe.transpose(ps[tg * 2 + k][:, j * P:(j + 1) * P],
                                                  dst[:, b, k * P:(k + 1) * P], ident[:, :])
                            mm.then_inc(s_back, 1)
                        if gate is not None and tg:
                            logits(tg - 1)
                    if gate is not None:
                        logits(NTG - 1).then_inc(s_gate, 1)
                        pe.wait_ge(s_gate, 1)

            @block.scalar
            def _(act):
                def evacuate(tg):
                    for k in range(CB):
                        act.wait_ge(s_back, tg * 2 + k + 1)
                        out, bank = XT[:, k, tg * W512:(tg + 1) * W512], ps[tg * 2 + k][:, :]
                        if affine:
                            ins = act.activation(out, bank, ACT.Identity, bias=col(affine[1], k), scale=col(affine[0], k))
                        else:
                            ins = act.activation(out, bank, ACT.Copy)
                        ins.then_inc(s_free, 1)

                for half in range(2):
                    act.wait_ge(s_shift, half + 1)
                    for b in range(half * HB + BY_DVE, half * HB + HB):
                        act.activation(dst[:, b, :], tile(b), ACT.Identity, bias=shift[:, b:b + 1],
                                       scale=rstd[:, b:b + 1]).then_inc(s_norma, 1)
                    if back:
                        evacuate(half * 2)
                        evacuate(half * 2 + 1)
                act.wait_ge(s_norma, 4)
                if back:
                    act.wait_ge(s_free, NTG * CB)

            @block.gpsimd
            def _(pool):
                pool.memset(power[:, :], -0.5).then_inc(s_cst, 1)
                pool.wait_ge(s_cst, 1)
                for half in range(2):
                    h = slice(half * HB, half * HB + HB)
                    pool.wait_ge(s_var, half + 1)
                    pool.tensor_tensor(rstd[:, h], var[:, h], power[:, h], ALU.pow).then_inc(s_rstd, 1)

            @block.vector
            def _(dve):
                link = Links(dve, s_link)

                def statistics(half):
                    if through:
                        dve.wait_ge(d_in[half], 16)
                    if stats is None:
                        for b in range(half * HB, half * HB + HB):
                            if from_channels and b % 2 == 0:
                                dve.wait_ge(s_tok, b // 2 + 1)
                            ins = dve.bn_stats(st[:, b, :], tile(b))
                        link(ins)
                    h = slice(half * HB, half * HB + HB)
                    even, odd = st[:, h, 1], st[:, h, 4]
                    dve.tensor_tensor(total[:, h], even, odd, ALU.add)
                    dve.tensor_tensor(var[:, h], st[:, h, 2], st[:, h, 5], ALU.add)
                    link(dve.tensor_tensor(diff[:, h], even, odd, ALU.subtract))
                    link(dve.tensor_tensor(diff[:, h], diff[:, h], diff[:, h], ALU.mult))
                    link(dve.scalar_tensor_tensor(var[:, h], diff[:, h], C / 4.0, var[:, h], ALU.mult, ALU.add))
                    dve.tensor_scalar(var[:, h], var[:, h], 1.0 / C, eps, ALU.mult, ALU.add).then_inc(s_var, 1)

                def scaling(half):
                    h = slice(half * HB, half * HB + HB)
                    dve.wait_ge(s_rstd, half + 1)
                    dve.scalar_tensor_tensor(shift[:, h], total[:, h], -0.5, rstd[:, h], ALU.mult, ALU.mult
                                             ).then_inc(s_shift, 1)
                    dve.wait_ge(s_shift, half + 1)
                    for b in range(half * HB, half * HB + BY_DVE):
                        dve.tensor_scalar(dst[:, b, :], tile(b), rstd[:, b:b + 1], shift[:, b:b + 1],
                                          ALU.mult, ALU.add).then_inc(s_norm, 1)
                statistics(0)
                statistics(1)
                scaling(0)
                scaling(1)
                dve.wait_ge(s_norm, 2 * BY_DVE)


def scan_layer(ct, d_ct, nc, io, sem, sbuf, X, XT, small, ident, ps, col, cols):
    ctx = ExitStack()
    with ctx:
        xin = sbuf(ctx, "xin", [P, CB, TOK], F32)
        wa = sbuf(ctx, "wa", [P, CB, 2 * C], F32)
        gate = sbuf(ctx, "gate", [P, 2, CB, W512], F32)
        val = sbuf(ctx, "val", [P, 2, CB, W512], F32)
        hid = sbuf(ctx, "hid", [P, 2, CB, W512], F32)
        d_x, d_w = [sem(f"a_dx{k}") for k in range(NTG)], sem("a_dw")
        s_id, s_mm, s_act, s_zero, s_scan, s_add = (sem("a_" + n) for n in
                                                    ("id", "mm", "act", "zero", "scan", "add"))
        with nc.Block() as block:
            @block.sync
            def _(sp):
                sp.dma_start(wa[:, :, :], io["wa"].rearrange("(k p) n -> p k n", p=P)).then_inc(d_w, 16)
                sp.dma_start(small[:, :], io["small"]).then_inc(d_w, 16)
                for tg in range(NTG):
                    sp.dma_start(xin[:, :, tg * W512:(tg + 1) * W512],
                                 io["xT"].rearrange("(k p) n -> p k n", p=P)[:, :, tg * W512:(tg + 1) * W512]
                                 ).then_inc(d_x[tg], 16)
                sp.dma_start(ct[:, :, :], io["ctxR"].rearrange("k p n -> p k n")).then_inc(d_ct, 16)

            @block.tensor
            def _(pe):
                pe.wait_ge(d_w, 32)
                for tg in range(NTG):
                    pe.wait_ge(d_x[tg], 16)
                    if tg >= 2:
                        pe.wait_ge(s_act, 4 * (tg - 1))
                    for m in range(4):
                        for k in range(CB):
                            mm = pe.matmul(ps[(tg % 2) * 4 + m][:, :], wa[:, k, m * P:(m + 1) * P],
                                           xin[:, k, tg * W512:(tg + 1) * W512], start=(k == 0), stop=(k == CB - 1))
                        mm.then_inc(s_mm, 1)

            @block.scalar
            def _(act):
                for tg in range(NTG):
                    if tg >= 2:
                        act.wait_ge(s_scan, 2 * (tg - 1))
                    for m in range(4):
                        act.wait_ge(s_mm, 4 * tg + m + 1)
                        out = (gate if m < CB else val)[:, tg % 2, m % CB, :]
                        act.activation(out, ps[(tg % 2) * 4 + m][:, :], ACT.Sigmoid if m < CB else ACT.Tanh,
                                       bias=col("ab", m)).then_inc(s_act, 1)

            @block.gpsimd
            def _(pool):
                pool.memset(ident[:, :], 0.0).then_inc(s_id, 1)
                pool.wait_ge(s_id, 1)
                pool.affine_select(out=ident[:, :], in_=ident[:, :], compare_op=ALU.not_equal, fill=1.0,
                                   base=0, pattern=[[-1, P]], channel_multiplier=1).then_inc(s_id, 1)
                pool.wait_ge(s_id, 2)
                for tg in range(NTG):
                    pool.wait_ge(s_act, 4 * tg + CB)
                    g = gate[:, tg % 2, :, :].rearrange("p k (b s) -> p k b s", s=S)
                    pool.memset(g[:, :, :, 0], 0.0).then_inc(s_zero, 1)
                    pool.wait_ge(s_scan, 2 * (tg + 1))
                    pool.tensor_tensor(XT[:, :, tg * W512:(tg + 1) * W512], hid[:, tg % 2, :, :],
                                       xin[:, :, tg * W512:(tg + 1) * W512], ALU.add).then_inc(s_add, 1)
                pool.wait_ge(s_add, NTG)

            @block.vector
            def _(dve):
                for tg in range(NTG):
                    dve.wait_ge(s_zero, tg + 1)
                    dve.wait_ge(s_act, 4 * tg + 4)
                    if tg >= 2:
                        dve.wait_ge(s_add, tg - 1)
                    for k in range(CB):
                        dve.tensor_tensor_scan(hid[:, tg % 2, k, :], gate[:, tg % 2, k, :], val[:, tg % 2, k, :],
                                               0.0, ALU.mult, ALU.add).then_inc(s_scan, 1)


def conv_layer(ct, d_c, nc, io, sem, sbuf, X, XT, small, ident, ps, col, cols):
    ctx = ExitStack()
    with ctx:
        res = sbuf(ctx, "res", [P, CB, TOK], F32)
        tz = sbuf(ctx, "tz", [P, 4, C], F32)
        rev = sbuf(ctx, "rev", [P, P], F32)
        kv = sbuf(ctx, "kv", [P, 2, CB, W512], F32)
        prod = sbuf(ctx, "prod", [P, CB, W512], F32)
        d_t = [sem(f"b_dt{k}") for k in range(4)]
        s_rev, s_tz, s_kv, s_mm, s_prod, s_red, s_add = (sem("b_" + n) for n in
                                                        ("rev", "tz", "kv", "mm", "prod", "red", "add"))
        HB = B // 2
        ct_v = ct[:, :, :].rearrange("p k (b t) -> p k b t", t=S)
        xt_v = XT[:, :, :].rearrange("p k (b t) -> p k b t", t=S)
        res_v = res[:, :, :].rearrange("p k (b t) -> p k b t", t=S)

        def head(u):
            return u.b * 4 + u.g // 2

        with nc.Block() as block:
            @block.sync
            def _(sp):
                def load(u):
                    if u.g % 2 == 0:
                        if u.before(8):
                            sp.wait_ge(s_mm, u.n - 6)
                        sp.dma_start(tz[:, u.g // 2, :], io["toep"][bass.ds(head(u), 1), :, :].rearrange(
                            "a p n -> (a p) n")).then_inc(d_t[u.g // 2], 16)
                skewed(sp, CH // 4, 8, [(load, 0)])

            @block.gpsimd
            def _(pool):
                pool.memset(rev[:, :], 0.0).then_inc(s_rev, 1)
                pool.wait_ge(s_rev, 1)
                pool.affine_select(out=rev[:, :], in_=rev[:, :], compare_op=ALU.not_equal, fill=1.0,
                                   base=-(P - 1), pattern=[[1, P]], channel_multiplier=1).then_inc(s_rev, 1)
                pool.wait_ge(d_c, 16)

                def products(u):
                    if u.before(2):
                        pool.wait_ge(s_mm, u.n - 1)
                    half = (u.g % 2) * HB
                    for k in range(CB):
                        c = ct_v[:, k, half:half + HB, bass.ds(head(u) * CD, CD)]
                        ins = pool.tensor_tensor(kv[:, u.g % 2, k, :].rearrange("p (b j i) -> p b j i", j=CD, i=CD),
                                                 c.unsqueeze(3).to_broadcast([P, HB, CD, CD]),
                                                 c.unsqueeze(2).to_broadcast([P, HB, CD, CD]), ALU.mult)
                    ins.then_inc(s_kv, 1)
                skewed(pool, CH // 4, 8, [(products, 0)])

            @block.tensor
            def _(pe):
                def conv(u):
                    pe.wait_ge(s_kv, u.n + 1)
                    if u.g % 2 == 0:
                        pe.wait_ge(s_tz, head(u) + 1)
                    if u.before(2):
                        pe.wait_ge(s_prod, 2 * u.n - 2)
                    t, lo, hi = tz[:, u.g // 2, :], ps[(u.g % 2) * 2], ps[(u.g % 2) * 2 + 1]
                    pe.matmul(lo[:, :], t[:, 0:P], kv[:, u.g % 2, 0, :], start=True, stop=True)
                    pe.matmul(hi[:, :], t[:, P:C], kv[:, u.g % 2, 0, :], start=True, stop=False)
                    pe.matmul(hi[:, :], t[:, 0:P], kv[:, u.g % 2, 1, :], start=False, stop=True).then_inc(s_mm, 1)
                skewed(pe, CH // 4, 8, [(conv, 0)])

            @block.vector
            def _(dve):
                dve.wait_ge(s_rev, 2)

                def diagonal(u):
                    if u.g % 2 == 0:
                        dve.wait_ge(d_t[u.g // 2], u.b * 16 + 16)
                        t = tz[:, u.g // 2, 0:P]
                        d = cols("dskip")[:, bass.ds(head(u), 1)]
                        dve.scalar_tensor_tensor(t, rev[:, :], d, t, ALU.mult, ALU.add).then_inc(s_tz, 1)

                def queries(u):
                    dve.wait_ge(s_mm, u.n + 1)
                    half = (u.g % 2) * HB
                    for k in range(CB):
                        if u.before(1):
                            dve.wait_ge(s_red, 2 * u.n - 1 + k)
                        q = xt_v[:, k, half:half + HB, bass.ds(head(u) * CD, CD)]
                        dve.tensor_tensor(prod[:, k, :].rearrange("p (b j i) -> p b j i", j=CD, i=CD),
                                          ps[(u.g % 2) * 2 + k][:, :].rearrange("p (b j i) -> p b j i", j=CD, i=CD),
                                          q.unsqueeze(2).to_broadcast([P, HB, CD, CD]), ALU.mult).then_inc(s_prod, 1)
                    for k in range(CB):
                        dve.wait_ge(s_prod, 2 * u.n + 1 + k)
                        o = res_v[:, k, half:half + HB, bass.ds(head(u) * CD, CD)]
                        dve.tensor_reduce(o, prod[:, k, :].rearrange("p (b j i) -> p b j i", j=CD, i=CD),
                                          AX.X, ALU.add).then_inc(s_red, 1)
                skewed(dve, CH // 4, 8, [(diagonal, 0), (queries, 3)])
                dve.wait_ge(s_red, 4 * CH)
                dve.tensor_tensor(XT[:, :, :], XT[:, :, :], res[:, :, :], ALU.add).then_inc(s_add, 1)
                dve.wait_ge(s_add, 1)


def routed_layer(nc, io, sem, sbuf, X, XT, small, ident, ps, col, cols):
    ctx = ExitStack()
    with ctx:
        wf = sbuf(ctx, "wf", [P, CB, FW], F32)
        deb = sbuf(ctx, "deb", [P, CB, NE0], F32)
        lw = sbuf(ctx, "lw", [SEL + NE0, C], F32)
        pr = sbuf(ctx, "pr", [P, CB, FW], F32)
        cst = sbuf(ctx, "cst", [P, FW], F32)
        ones = sbuf(ctx, "c_ones", [P, P], F32)
        prio = sbuf(ctx, "prio", [P, NE0], F32)
        u_ = sbuf(ctx, "u_", [P, B, SEL + UPD], F32)
        xm = sbuf(ctx, "xm", [P, B, NE0], F32)
        sq = sbuf(ctx, "sq_", [P, B, C], F32)
        xx = sbuf(ctx, "xx", [P, B], F32)
        sc = sbuf(ctx, "sc", [P, B, NE0], F32)
        gt = sbuf(ctx, "gt", [P, B, NE0], F32)
        eq = sbuf(ctx, "eq", [P, B, NE0], F32)
        mx = sbuf(ctx, "mx", [P, B], F32)
        pm = sbuf(ctx, "pm", [P, B], F32)
        keep = sbuf(ctx, "keep", [P, B], F32)
        mk = sbuf(ctx, "mk", [P, B, UPD + NE0], F32)
        mkt = sbuf(ctx, "mkt", [UPD + NE0, B, P], F32)
        pad = sbuf(ctx, "pad", [P, ROW], F32)
        s_sq = sem("c_sq")
        d_w, d_pad, s_pad = sem("c_dw"), sem("c_dpad"), sem("c_pad")
        s_one, s_pr, s_cm, s_cst, s_mm, s_u, s_z, s_ex, s_mk, s_t, s_te, s_o, s_x, s_link = (
            sem("c_" + n) for n in ("one", "pr", "cm", "cst", "mm", "u", "z", "ex", "mk", "t", "te", "o", "x", "link"))

        def over(a, n):
            return a.unsqueeze(2).to_broadcast([P, B, n])

        with nc.Block() as block:
            @block.sync
            def _(sp):
                sp.dma_start(wf[:, :, :], io["wf"].rearrange("(k p) n -> p k n", p=P)).then_inc(d_w, 16)
                sp.dma_start(deb[:, :, :], io["deb"].rearrange("(k p) n -> p k n", p=P)).then_inc(d_w, 16)
                sp.dma_start(lw[:, :], io["lw"]).then_inc(d_w, 16)
                if "sorted_x" in io:
                    sp.wait_ge(s_pad, 2)
                    sp.dma_start(io["sorted_x"].rearrange("(r p) c -> p r c", p=P),
                                 pad[:, :].unsqueeze(1).to_broadcast([P, moe_tiles(), ROW])).then_inc(d_pad, 16)
                    sp.dma_start(io["sums"][TOK:TOK + P, :], pad[:, 0:C]).then_inc(d_pad, 16)
                    sp.wait_ge(d_pad, 32)

            @block.gpsimd
            def _(pool):
                pool.memset(ones[:, :], 1.0)
                for n in range(NE0):
                    ins = pool.memset(prio[:, n:n + 1], float(NE0 - n))
                ins.then_inc(s_one, 1)
                pool.memset(pad[:, :], 0.0).then_inc(s_pad, 1)
                pool.wait_ge(s_pad, 1)
                pool.iota(pad[:, ROW_ID:ROW_ID + 1].bitcast(I32), pattern=[[0, 1]], base=TOK, channel_multiplier=1
                          ).then_inc(s_pad, 1)

            @block.tensor
            def _(pe):
                pe.wait_ge(d_w, 48)
                pe.wait_ge(s_one, 1)
                pe.wait_ge(s_pr, 3)
                for k in range(CB):
                    mm = pe.matmul(ps[0][:, 0:FW], ones[:, :], pr[:, k, :], start=(k == 0), stop=(k == CB - 1))
                mm.then_inc(s_cm, 1)
                pe.wait_ge(s_cst, 1)
                for b in range(B):
                    for k in range(CB):
                        mm = pe.matmul(ps[b // 2][:, (b % 2) * C:(b % 2) * C + FW], XT[:, k, b * S:(b + 1) * S],
                                       wf[:, k, :], start=(k == 0), stop=(k == CB - 1))
                    if b % 2:
                        mm.then_inc(s_mm, 1)
                pe.wait_ge(s_mk, 1)
                for q in range(B // 4):
                    for j in range(4):
                        mm = pe.transpose(ps[q][0:UPD + NE0, j * P:(j + 1) * P], mk[:, 4 * q + j, :], ident[:, :])
                    mm.then_inc(s_t, 1)
                for b in range(B):
                    pe.wait_ge(s_te, b // 4 + 1)
                    if b >= 8 and b % 2 == 0:
                        pe.wait_ge(s_x, b - 6)
                    mm = pe.matmul(ps[4 + (b // 2) % 4][:, (b % 2) * C:(b % 2 + 1) * C], mkt[:, b, :], lw[:, :],
                                   start=True, stop=True)
                    if b % 2:
                        mm.then_inc(s_o, 1)

            @block.scalar
            def _(act):
                for b in range(B):
                    ins = act.activation(sq[:, b, :], X[:, b, :], ACT.Square, accum_out=xx[:, b:b + 1])
                ins.then_inc(s_sq, 1)
                act.wait_ge(s_z, 1)
                act.activation(gt[:, :, :], sc[:, :, :], ACT.Exp, scale=-1.0).then_inc(s_ex, 1)
                for q in range(B // 4):
                    act.wait_ge(s_t, q + 1)
                    act.activation(mkt[:, 4 * q:4 * q + 4, :],
                                   ps[q][0:UPD + NE0, :].rearrange("p (b s) -> p b s", b=4), ACT.Copy).then_inc(s_te, 1)

            @block.vector
            def _(dve):
                link = Links(dve, s_link)
                dve.wait_ge(d_w, 48)
                m = wf[:, :, SEL + UPD:FW]

                def pairs(a):
                    return a.rearrange("p k (n s) -> p k n s", s=NS0)

                dve.tensor_tensor(pairs(pr[:, :, 0:SEL]), pairs(wf[:, :, 0:SEL]),
                                  m.unsqueeze(3).to_broadcast([P, CB, NE0, NS0]), ALU.mult).then_inc(s_pr, 1)
                dve.tensor_tensor(pairs(pr[:, :, SEL:SEL + UPD]), pairs(wf[:, :, SEL:SEL + UPD]),
                                  deb[:, :, :].unsqueeze(3).to_broadcast([P, CB, NE0, NS0]), ALU.mult).then_inc(s_pr, 1)
                dve.tensor_tensor(pr[:, :, SEL + UPD:FW], m, m, ALU.mult).then_inc(s_pr, 1)
                dve.wait_ge(s_cm, 1)
                dve.tensor_copy(cst[:, :], ps[0][:, 0:FW]).then_inc(s_cst, 1)
                dve.wait_ge(s_cst, 1)
                dve.wait_ge(s_one, 1)
                for q in range(B // 2):
                    dve.wait_ge(s_mm, q + 1)
                    bank = ps[q][:, :].rearrange("p (b c) -> p b c", b=2)
                    dve.tensor_tensor(u_[:, 2 * q:2 * q + 2, :], bank[:, :, 0:SEL + UPD],
                                      cst[:, 0:SEL + UPD].unsqueeze(1).to_broadcast([P, 2, SEL + UPD]), ALU.subtract)
                    ins = dve.tensor_copy(xm[:, 2 * q:2 * q + 2, :], bank[:, :, SEL + UPD:FW])
                link(ins)
                s2 = sq[:, :, 0:SEL]
                dve.wait_ge(s_sq, 1)
                link(dve.tensor_tensor(s2, u_[:, :, 0:SEL], u_[:, :, 0:SEL], ALU.mult))
                link(dve.tensor_reduce(sc[:, :, :], s2.rearrange("p b (n s) -> p b n s", s=NS0), AX.X, ALU.add))
                mm_ = cst[:, SEL + UPD:FW].unsqueeze(1).to_broadcast([P, B, NE0])
                link(dve.scalar_tensor_tensor(xm[:, :, :], xm[:, :, :], -2.0, mm_, ALU.mult, ALU.add))
                link(dve.tensor_tensor(xm[:, :, :], xm[:, :, :], over(xx[:, :], NE0), ALU.add))
                link(dve.reciprocal(xm[:, :, :], xm[:, :, :]))
                link(dve.tensor_tensor(sc[:, :, :], sc[:, :, :], xm[:, :, :], ALU.mult))
                link(dve.tensor_tensor(sc[:, :, :], sc[:, :, :],
                                       cols("center").unsqueeze(1).to_broadcast([P, B, NE0]), ALU.subtract))
                link(dve.tensor_tensor(sc[:, :, :], sc[:, :, :],
                                       cols("slope").unsqueeze(1).to_broadcast([P, B, NE0]), ALU.mult))
                dve.tensor_scalar(sc[:, :, :], sc[:, :, :], -87.0, None, ALU.max).then_inc(s_z, 1)
                dve.wait_ge(s_ex, 1)
                link(dve.tensor_scalar(gt[:, :, :], gt[:, :, :], 1.0, None, ALU.add))
                link(dve.reciprocal(gt[:, :, :], gt[:, :, :]))
                link(dve.tensor_reduce(mx[:, :], gt[:, :, :], AX.X, ALU.max))
                link(dve.tensor_tensor(eq[:, :, :], gt[:, :, :], over(mx[:, :], NE0), ALU.is_ge))
                link(dve.tensor_tensor(eq[:, :, :], eq[:, :, :],
                                       prio[:, :].unsqueeze(1).to_broadcast([P, B, NE0]), ALU.mult))
                link(dve.tensor_reduce(pm[:, :], eq[:, :, :], AX.X, ALU.max))
                link(dve.tensor_tensor(eq[:, :, :], eq[:, :, :], over(pm[:, :], NE0), ALU.is_equal))
                link(dve.tensor_scalar(keep[:, :], mx[:, :], -1.0, 2.0, ALU.mult, ALU.add))
                link(dve.tensor_tensor(mk[:, :, UPD:UPD + NE0], eq[:, :, :], over(mx[:, :], NE0), ALU.mult))
                for h in range(2):
                    bs = slice(h * 8, h * 8 + 8)
                    ins = dve.tensor_tensor(mk[:, bs, 0:UPD].rearrange("p b (n s) -> p b n s", s=NS0),
                                            u_[:, bs, SEL:SEL + UPD].rearrange("p b (n s) -> p b n s", s=NS0),
                                            mk[:, bs, UPD:UPD + NE0].unsqueeze(3).to_broadcast([P, 8, NE0, NS0]), ALU.mult)
                ins.then_inc(s_mk, 1)
                for b in range(B):
                    dve.wait_ge(s_o, b // 2 + 1)
                    dve.scalar_tensor_tensor(X[:, b, :], X[:, b, :], keep[:, b:b + 1],
                                             ps[4 + (b // 2) % 4][:, (b % 2) * C:(b % 2 + 1) * C],
                                             ALU.mult, ALU.add).then_inc(s_x, 1)
                dve.wait_ge(s_x, B)


def causal_layer(row_stats, quant, nc, io, sem, sbuf, X, XT, small, ident, ps, col, cols):
    ctx = ExitStack()
    with ctx:
        QB = HQ // HKV
        PAD = P // HKV
        wq = sbuf(ctx, "d_wq", [P, CB, QB * P], F32)
        wk = sbuf(ctx, "d_wk", [P, CB, P], F32)
        wv = sbuf(ctx, "d_wv", [P, CB, HKV * HD], F32)
        wo = sbuf(ctx, "d_wo", [P, CB, C], F32)
        identb = sbuf(ctx, "identb", [P, P], BF16)
        mask = sbuf(ctx, "mask", [P, HKV, P], BF16)
        xs = sbuf(ctx, "xs", [P, 2, CB, S], F32)
        qt = sbuf(ctx, "qt_", [P, 2, QB * P], F32)
        kd = sbuf(ctx, "kd", [P, 2, HKV, P], F32)
        v = sbuf(ctx, "d_v", [P, 2, HKV, HD + 1], F32)
        neg = sbuf(ctx, "neg", [P, 2, HKV], F32)
        sb_ = sbuf(ctx, "sb_", [P, 2, HKV, P], F32)
        pt = sbuf(ctx, "pt_", [P, 2, HKV, P], F32)
        rec = sbuf(ctx, "rec", [P, QB, HKV], F32)
        cx = sbuf(ctx, "cx", [P, C], F32)
        cxt = sbuf(ctx, "cxt", [P, CB, P], F32)
        d_w = sem("d_dw")
        split = Split("ss_", False, quant.dst, nc, io, sem, sbuf, ctx)
        s_const = sem("d_const")

        (s_cst, s_xs, s_mm, s_q, s_k, s_s, s_mx, s_sub, s_ex, s_tp, s_cp, s_c, s_rc, s_cn, s_ct, s_cc, s_o, s_x) = (
            sem("d_" + n) for n in ("cst", "xs", "mm", "q", "k", "s", "mx", "sub", "ex", "tp", "cp", "c", "rc", "cn",
                                    "ct", "cc", "o", "x"))
        bQ, bK, bS, bT, bC, bF = ps[0], ps[1], ps[2:4], ps[4:6], ps[6], ps[7]
        PEEL = 2
        PER = 2 * QB

        def batch(u):
            return u.b * 2 + u.g // QB

        with nc.Block() as block:
            @block.sync
            def _(sp):
                sp.dma_start(wq[:, :, :], io["d_wq"].rearrange("(k p) n -> p k n", p=P)).then_inc(d_w, 16)
                sp.dma_start(wk[:, :, :], io["d_wk"].rearrange("(k p) n -> p k n", p=P)).then_inc(d_w, 16)
                sp.dma_start(wv[:, :, :], io["d_wv"].rearrange("(k p) n -> p k n", p=P)).then_inc(d_w, 16)
                sp.dma_start(wo[:, :, :], io["d_wo"].rearrange("(k p) n -> p k n", p=P)).then_inc(d_w, 16)

                def load(u):
                    if u.g == 0:
                        split.load(sp, u.b, u.peeled and u.b == 0, u.peeled and u.b == 0)
                skewed(sp, B // 2, PER, [(load, 0)], PEEL)

            @block.gpsimd
            def _(pool):
                pool.memset(mask[:, :, :], 0.0).then_inc(s_cst, 1)
                pool.memset(identb[:, :], 0.0).then_inc(s_cst, 1)
                pool.memset(kd[:, :, :, :], 0.0).then_inc(s_cst, 1)
                pool.memset(v[:, :, :, :], 1.0).then_inc(s_cst, 1)
                pool.wait_ge(s_cst, 4)
                pool.affine_select(out=mask[:, :, :], in_=mask[:, :, :], compare_op=ALU.is_ge, fill=-1e30,
                                   base=0, pattern=[[0, HKV], [-1, P]], channel_multiplier=1).then_inc(s_cst, 1)
                pool.affine_select(out=identb[:, :], in_=identb[:, :], compare_op=ALU.not_equal, fill=1.0,
                                   base=0, pattern=[[-1, P]], channel_multiplier=1).then_inc(s_cst, 1)

                def low(u):
                    if u.g == 5:
                        split.low(pool, u.b)
                skewed(pool, B // 2, PER, [(low, 0)], PEEL)

            @block.tensor
            def _(pe):
                pe.sem_inc(s_o, 1)
                pe.wait_ge(d_w, 64)
                pe.wait_ge(s_cst, 6)

                def project(u):
                    b, par, t = batch(u), u.g // QB, u.g % QB
                    if t == 0:
                        pe.wait_ge(s_xs, b + 1)
                        if u.before(QB):
                            pe.wait_ge(s_q, b)
                    for k in range(CB):
                        pe.matmul(bQ[:, t * P:(t + 1) * P], wq[:, k, t * P:(t + 1) * P], xs[:, par, k, :],
                                  start=(k == 0), stop=(k == CB - 1))
                    if t < QB - 1:
                        return
                    if u.before(QB):
                        pe.wait_ge(s_k, b)
                    for k in range(CB):
                        pe.matmul(bK[:, 0:P], wk[:, k, :], xs[:, par, k, :], start=(k == 0), stop=(k == CB - 1))
                    for k in range(CB):
                        mm = pe.matmul(bK[:, P:P + HKV * HD], xs[:, par, k, :], wv[:, k, :],
                                       start=(k == 0), stop=(k == CB - 1))
                    mm.then_inc(s_mm, 1)

                def scores(u):
                    t, par = u.g % QB, u.g // QB
                    pe.wait_ge(s_q, batch(u) + 1)
                    pe.wait_ge(s_k, batch(u) + 1)
                    if u.before(2):
                        pe.wait_ge(s_sub, u.n - 1)
                    pe.matmul(bS[u.g % 2][:, :], qt[:, par, t * P:(t + 1) * P],
                              kd[:, par, :, :].rearrange("p h k -> p (h k)"), start=True, stop=False)
                    pe.matmul(bS[u.g % 2][:, :], identb[:, :], mask[:, :, :].rearrange("p h k -> p (h k)"),
                              start=False, stop=True).then_inc(s_s, 1)

                def turn(u):
                    pe.wait_ge(s_ex, u.n + 1)
                    if u.before(2):
                        pe.wait_ge(s_cp, u.n - 1)
                    for h in range(HKV):
                        mm = pe.transpose(bT[u.g % 2][:, h * P:(h + 1) * P], sb_[:, u.g % 2, h, :], ident[:, :])
                    mm.then_inc(s_tp, 1)

                def context(u):
                    t, par = u.g % QB, u.g // QB
                    pe.wait_ge(s_cp, u.n + 1)
                    if t == 0 and u.before(QB):
                        pe.wait_ge(s_cn, batch(u))
                    for h in range(HKV):
                        at = (t * HKV + h) * (HD + 1)
                        mm = pe.matmul(bC[:, at:at + HD + 1], pt[:, u.g % 2, h, :], v[:, par, h, :],
                                       start=True, stop=True)
                    mm.then_inc(s_c, 1)

                def turn_context(u):
                    if u.g % QB != QB - 1:
                        return
                    b = batch(u)
                    pe.wait_ge(s_cn, b + 1)
                    pe.wait_ge(s_x, b + 1)
                    for k in range(CB):
                        mm = pe.transpose(bF[:, k * P:(k + 1) * P], cx[:, k * P:(k + 1) * P], ident[:, :])
                    mm.then_inc(s_ct, 1)

                def out(u):
                    if u.g % QB != QB - 1:
                        return
                    b = batch(u)
                    pe.wait_ge(s_cc, b + 1)
                    for k in range(CB):
                        mm = pe.matmul(bF[:, C:2 * C], cxt[:, k, :], wo[:, k, :], start=(k == 0), stop=(k == CB - 1))
                    mm.then_inc(s_o, 1)
                skewed(pe, B // 2, PER, [(scores, 7), (turn, 8), (context, 9), (turn_context, 11), (out, 12), (project, 2)], PEEL)

            @block.scalar
            def _(act):
                def columns(u):
                    if u.g % QB:
                        return
                    b, par = batch(u), u.g // QB
                    if u.before(2 * QB):
                        act.wait_ge(s_mm, b - 1)
                    act.activation(xs[:, par, :, :], XT[:, :, bass.ds(b * S, S)], ACT.Copy).then_inc(s_xs, 1)

                def queries(u):
                    if u.g % QB != QB - 1:
                        return
                    b, par = batch(u), u.g // QB
                    act.wait_ge(s_mm, b + 1)
                    if u.before(2 * QB):
                        act.wait_ge(s_s, QB * (b - 1))
                    act.activation(qt[:, par, :], bQ[:, :], ACT.Copy).then_inc(s_q, 1)

                def exps(u):
                    act.wait_ge(s_sub, u.n + 1)
                    act.activation(sb_[:, u.g % 2, :, :], sb_[:, u.g % 2, :, :], ACT.Exp,
                                   scale=float(HD) ** -0.5).then_inc(s_ex, 1)

                def turned(u):
                    act.wait_ge(s_tp, u.n + 1)
                    if u.before(2):
                        act.wait_ge(s_c, u.n - 1)
                    act.activation(pt[:, u.g % 2, :, :], bT[u.g % 2][:, :].rearrange("p (h k) -> p h k", h=HKV),
                                   ACT.Copy).then_inc(s_cp, 1)

                def context(u):
                    if u.g % QB != QB - 1:
                        return
                    act.wait_ge(s_ct, batch(u) + 1)
                    act.wait_ge(s_o, batch(u) + 1)
                    act.activation(cxt[:, :, :], bF[:, 0:C].rearrange("p (k s) -> p k s", k=CB),
                                   ACT.Copy).then_inc(s_cc, 1)

                def high(u):
                    if u.g == 4:
                        split.high(act, u.b)
                skewed(act, B // 2, PER, [(exps, 8), (queries, 3), (columns, 0), (turned, 8), (context, 11), (high, 0)], PEEL)

            @block.vector
            def _(dve):
                dve.sem_inc(s_x, 1)
                quant.constants(dve, col, cols).then_inc(s_const, 1)
                dve.wait_ge(s_const, 1)
                dve.wait_ge(s_cst, 4)

                def keys(u):
                    if u.g % QB != QB - 1:
                        return
                    b, par = batch(u), u.g // QB
                    dve.wait_ge(s_mm, b + 1)
                    if u.before(2 * QB):
                        dve.wait_ge(s_c, QB * (b - 1))
                    for h in range(HKV):
                        rows = slice(h * PAD, (h + 1) * PAD)
                        dve.tensor_copy(kd[rows, par, h, :], bK[rows, 0:P])
                    dve.tensor_copy(v[:, par, :, 0:HD],
                                    bK[:, P:P + HKV * HD].rearrange("p (h d) -> p h d", h=HKV)).then_inc(s_k, 1)

                def maxima(u):
                    dve.wait_ge(s_s, u.n + 1)
                    bank = bS[u.g % 2][:, :].rearrange("p (h k) -> p h k", h=HKV)
                    dve.tensor_reduce(neg[:, u.g % 2, :], bank, AX.X, ALU.max).then_inc(s_mx, 1)
                    dve.wait_ge(s_mx, u.n + 1)
                    if u.before(2):
                        dve.wait_ge(s_tp, u.n - 1)
                    dve.tensor_tensor(sb_[:, u.g % 2, :, :], bank,
                                      neg[:, u.g % 2, :].unsqueeze(2).to_broadcast([P, HKV, P]),
                                      ALU.subtract).then_inc(s_sub, 1)

                def normal(u):
                    if u.g % QB != QB - 1:
                        return
                    b = batch(u)
                    dve.wait_ge(s_c, u.n + 1)
                    c = bC[:, 0:HQ * (HD + 1)].rearrange("p (t h d) -> p t h d", t=QB, h=HKV)
                    dve.reciprocal(rec[:, :, :], c[:, :, :, HD]).then_inc(s_rc, 1)
                    dve.wait_ge(s_rc, b + 1)
                    if u.before(QB):
                        dve.wait_ge(s_ct, b)
                    dve.tensor_tensor(cx[:, :].rearrange("p (h t d) -> p t h d", h=HKV, t=QB), c[:, :, :, 0:HD],
                                      rec[:, :, :].unsqueeze(3).to_broadcast([P, QB, HKV, HD]),
                                      ALU.mult).then_inc(s_cn, 1)

                def residual(u):
                    if u.g % QB != QB - 1:
                        return
                    b = batch(u)
                    dve.wait_ge(s_o, b + 2)
                    x = X[:, bass.ds(b, 1), :].rearrange("p a c -> p (a c)")
                    dve.tensor_tensor(x, x, bF[:, C:2 * C], ALU.add).then_inc(s_x, 1)

                def statistics(u):
                    if u.g % QB == QB - 1:
                        b = batch(u)
                        dve.wait_ge(s_x, b + 2)
                        dve.bn_stats(row_stats[:, bass.ds(b, 1), :].rearrange("p a c -> p (a c)"),
                                     X[:, bass.ds(b, 1), :].rearrange("p a c -> p (a c)"))

                def centre(u):
                    if u.g == 2:
                        split.centre(dve, u.b, u.b_par)
                skewed(dve, B // 2, PER, [(keys, 3), (normal, 10), (residual, 13), (maxima, 7), (statistics, 14),
                                          (centre, 0)], PEEL)
                dve.wait_ge(s_x, B + 1)


class Split:

    def __init__(self, tag, cross, dst, nc, io, sem, sbuf, ctx, buffers=1):
        self.buffers = buffers
        self.cross, self.io = cross, io
        self.whi, self.wlo, self.phi, self.plo, self.fold = dst
        self.st = sbuf(ctx, tag + "st", [P, buffers, CB, UW], F32)
        self.pst = sbuf(ctx, tag + "pst", [P, 2, C], F32)
        self.mean = sbuf(ctx, tag + "mean", [P, CB, 4], F32)
        self.d_w = [sem(f"{tag}dw{k}") for k in range(buffers)]
        (self.d_p, self.s_scl, self.s_sum, self.s_avg, self.s_ctr, self.s_hi, self.s_lo, self.s_phi,
         self.s_plo) = (sem(f"{tag}{n}") for n in ("dp", "scl", "sum", "avg", "ctr", "hi", "lo", "phi", "plo"))

    def staged(self, g):
        k, turn = (0, g) if self.buffers == 1 else (g % self.buffers, g // self.buffers)
        return self.st[:, k, :, :], k, turn

    def load(self, sp, g, first, first_rows):
        st, place, _ = self.staged(g)
        if not first:
            sp.wait_ge(self.s_lo, g - self.buffers + 1)
        sp.dma_start(st, self.io["wcross" if self.cross else "wself"][bass.ds(g, 1), :, :].rearrange(
            "a (k p) n -> p (a k) n", p=P)).then_inc(self.d_w[place], 16)
        if not first_rows:
            sp.wait_ge(self.s_plo, g)
        sp.dma_start(self.pst[:, :, :], self.io["wproj"][int(self.cross), bass.ds(2 * g, 2), :, :].rearrange(
            "h p n -> p h n")).then_inc(self.d_p, 16)

    def centre(self, dve, g, odd):
        st, place, turn = self.staged(g)
        if self.buffers > 1 and g:
            dve.wait_ge(self.s_ctr, g)
        dve.wait_ge(self.d_w[place], 16 * turn + 16)
        heads = 2 if odd else 4
        for k in range(CB):
            if odd and self.cross:
                continue
            parts = ((0, UW, 3 if self.cross else 0),) if not odd else ((0, 2 * D, 1), (2 * D, UW, 2))
            for a, z, j in parts:
                ins = dve.tensor_scalar(st[:, k, a:z], st[:, k, a:z], self.fold[:, j, k:k + 1], None, ALU.mult)
        if odd and self.cross:
            dve.sem_inc(self.s_scl, 1)
        else:
            ins.then_inc(self.s_scl, 1)
        dve.wait_ge(self.s_scl, g + 1)
        hd = st[:, :, 0:heads * D].rearrange("p k (h d) -> p k h d", d=D)
        mean = self.mean[:, :, 0:heads]
        dve.tensor_reduce(mean, hd, AX.X, ALU.add).then_inc(self.s_sum, 1)
        dve.wait_ge(self.s_sum, g + 1)
        dve.tensor_scalar(mean, mean, -1.0 / D, None, ALU.mult).then_inc(self.s_avg, 1)
        dve.wait_ge(self.s_avg, g + 1)
        dve.tensor_tensor(hd, hd, mean.unsqueeze(3).to_broadcast([P, CB, heads, D]), ALU.add).then_inc(self.s_ctr, 1)

    def high(self, act, g):
        at = bass.ds(g, 1)
        st, place, turn = self.staged(g)
        act.wait_ge(self.s_ctr, g + 1)
        act.activation(self.whi[:, at, :, :], st.unsqueeze(1), ACT.Copy).then_inc(self.s_hi, 1)
        act.wait_ge(self.d_p, 16 * g + 16)
        act.activation(self.phi[:, at, :, :], self.pst[:, :, :].unsqueeze(1), ACT.Copy).then_inc(self.s_phi, 1)

    def low(self, pool, g):
        at = bass.ds(g, 1)
        st, place, turn = self.staged(g)
        pool.wait_ge(self.s_hi, g + 1)
        pool.tensor_tensor(self.wlo[:, at, :, :], st.unsqueeze(1), self.whi[:, at, :, :].bitcast(F32),
                           ALU.subtract).then_inc(self.s_lo, 1)
        pool.wait_ge(self.s_phi, g + 1)
        pool.tensor_tensor(self.plo[:, at, :, :], self.pst[:, :, :].unsqueeze(1), self.phi[:, at, :, :].bitcast(F32),
                           ALU.subtract).then_inc(self.s_plo, 1)


class Quant:

    def __init__(self, ctx, sbuf):
        self.whi = sbuf(ctx, "whi", [P, G, CB, UW], F32R)
        self.wlo = sbuf(ctx, "wlo", [P, G, CB, UW], F32R)
        self.phi = sbuf(ctx, "phi", [P, G, 2, C], F32R)
        self.plo = sbuf(ctx, "plo", [P, G, 2, C], F32R)
        self.fold = sbuf(ctx, "fold", [P, 4, CB], F32)
        self.inv = sbuf(ctx, "inv", [P, 4, CB], F32)
        self.invsm = sbuf(ctx, "invsm", [P, 4 * G], F32)
        self.aff = sbuf(ctx, "aff", [P, 2, 4], F32)
        self.pscale = sbuf(ctx, "pscale", [P, 1], F32)
        self.dst = (self.whi, self.wlo, self.phi, self.plo, self.fold)

    def constants(self, dve, col, cols):
        for j, (si, sw) in enumerate((("sq", "wsq"), ("sk", "wsk"), ("sv", "wsv"), ("sqx", "wsqx"))):
            dve.tensor_scalar(self.fold[:, j, :], cols(si), col(sw), None, ALU.mult)
            dve.reciprocal(self.inv[:, j, :], cols(si))
        dve.reciprocal(self.invsm[:, :], cols("smooth"))
        dve.tensor_scalar(self.pscale[:, :], col("pin"), col("pw"), None, ALU.mult)
        for h, names in enumerate((("qw", "qb", "kw", "kb"), ("qxw", "qxb", "kxw", "kxb"))):
            for j, name in enumerate(names):
                k = (float(D) ** -0.5 if j < 2 else 1.0) * (1.0 if j % 2 else float(D) ** 0.5)
                ins = dve.tensor_scalar(self.aff[:, h, j:j + 1], col(name), k, None, ALU.mult)
        return ins


def quant_layer(row_stats, quant, nc, io, sem, sbuf, **args):
    args = dict(nc=nc, io=io, sem=sem, sbuf=sbuf, **args)
    XT, cols, col = args["XT"], args["cols"], args["col"]
    ctx = ExitStack()
    with ctx:
        xq = sbuf(ctx, "xq", [P, 4, CB, TOK], BF16)
        s_y, s_clamp, s_power, s_magic, s_t, s_z = (sem("e_" + n) for n in ("y", "clamp", "power", "magic", "t", "z"))
        with ExitStack() as inner:
            lnx = sbuf(inner, "lnx", [P, B, C], F32)
            norm_layer("ln", dst=lnx, affine=("lnw", "lnb"), **args)
        with ExitStack() as inner:
            y = sbuf(inner, "y0", [P, 2, TOK], BF16)
            p2 = sbuf(inner, "p20", [P, 2, TOK], BF16)
            m = sbuf(inner, "m0", [P, 2, TOK], BF16)
            t = sbuf(inner, "t0", [P, 2, TOK], F32)
            with nc.Block() as block:
                @block.scalar
                def _(act):
                    for n in range(4 * CB):
                        if n >= 2:
                            act.wait_ge(s_t, 2 * n - 2)
                        act.activation(y[:, n % 2, :], XT[:, n % CB, :], ACT.Copy,
                                       scale=quant.inv[:, n // CB, n % CB:n % CB + 1]).then_inc(s_y, 1)

                @block.vector
                def _(dve):
                    for n in range(4 * CB):
                        dve.wait_ge(s_y, n + 1)
                        if n >= 2:
                            dve.wait_ge(s_z, 2 * n - 2)
                        at = [(n % 2, slice(h * TOK // 2, (h + 1) * TOK // 2)) for h in range(2)]
                        for k, h in at:
                            dve.tensor_scalar(y[:, k, h], y[:, k, h], FP8_MAX, -FP8_MAX, ALU.min, ALU.max).then_inc(s_clamp, 1)
                        for half, (k, h) in enumerate(at):
                            dve.wait_ge(s_clamp, 2 * n + half + 1)
                            dve.tensor_scalar(p2[:, k, h].bitcast(U16), y[:, k, h].bitcast(U16), 0x7F80, None,
                                              ALU.bitwise_and).then_inc(s_power, 1)
                        for half, (k, h) in enumerate(at):
                            dve.wait_ge(s_power, 2 * n + half + 1)
                            dve.tensor_scalar(m[:, k, h], p2[:, k, h], FP8_MIN_NORMAL, ROUND, ALU.max, ALU.mult
                                              ).then_inc(s_magic, 1)
                        for half, (k, h) in enumerate(at):
                            dve.wait_ge(s_magic, 2 * n + half + 1)
                            dve.tensor_tensor(t[:, k, h], y[:, k, h], m[:, k, h], ALU.add).then_inc(s_t, 1)

                @block.gpsimd
                def _(pool):
                    for n in range(4 * CB):
                        for half in range(2):
                            h = slice(half * TOK // 2, (half + 1) * TOK // 2)
                            pool.wait_ge(s_t, 2 * n + half + 1)
                            pool.tensor_tensor(xq[:, n // CB, n % CB, h], t[:, n % 2, h], m[:, n % 2, h],
                                               ALU.subtract).then_inc(s_z, 1)
                    pool.wait_ge(s_z, 8 * CB)
        split = Split("xs_", True, quant.dst, nc, io, sem, sbuf, ctx, buffers=2)
        d_c = sem("cross_dc")
        for cross in (False, True):
            attention_pass(cross, xq, row_stats, quant, split, d_c, **args)


def attention_pass(cross, xq, row_stats, quant, split, d_c, nc, io, sem, sbuf, X, XT, small, ident, ps, col, cols):
    tag = "cross_" if cross else "self_"
    ctx = ExitStack()
    NQ = 1 if cross else 3
    QW = 2 * D
    fold, invsm, aff, pscale = quant.fold, quant.invsm, quant.aff, quant.pscale
    whi, wlo, phi, plo = quant.whi, quant.wlo, quant.phi, quant.plo
    LEAD = 2
    with ctx:
        if cross:
            chi = sbuf(ctx, "chi", [P, 2, CB, S], F32R)
            clo = sbuf(ctx, "clo", [P, 2, CB, S], F32R)
        xs = sbuf(ctx, tag + "xs", [P, 2, NQ, CB, S], F32R)
        stat = sbuf(ctx, tag + "stat", [P, 2, 12], F32)
        var = sbuf(ctx, tag + "var", [P, 2, 4], F32)
        half = sbuf(ctx, tag + "half", [P, 4], F32)
        deps = sbuf(ctx, tag + "deps", [P, 4], F32)
        HN = (4, 2)
        rstd = sbuf(ctx, tag + "rstd", [P, 2, 4], F32)
        qkv = sbuf(ctx, tag + "qkv", [P, G, 4, D], F32)
        qkt = sbuf(ctx, tag + "qkt", [P, 2, 3, S], F32)
        neg = sbuf(ctx, tag + "neg", [P, 2, 2], F32)
        pr = sbuf(ctx, tag + "pr", [P, 2, 2, S], F32)
        tot = sbuf(ctx, tag + "tot", [P, 2, 2], F32)
        rec = sbuf(ctx, tag + "rec", [P, 2, 2], F32)
        pt = sbuf(ctx, tag + "pt", [P, 2, 2 * S], F32)
        y = sbuf(ctx, tag + "y", [P, 2, 2 * S], BF16)
        m = sbuf(ctx, tag + "m", [P, 2, 2 * S], BF16)
        t = sbuf(ctx, tag + "t", [P, 2, 2 * S], F32)
        z = sbuf(ctx, tag + "z", [P, 2, 2 * S], F32R)
        names = ("cst", "xs", "chi", "clo", "proj", "stat", "var", "rstd", "qn", "tr", "qkt", "sc", "neg", "ex", "rec", "pn",
                 "tp", "pt", "o", "y", "yc", "p2", "m", "t", "z", "w", "x")
        (s_cst, s_xs, s_chi, s_clo, s_proj, s_stat, s_var, s_rstd, s_qn, s_tr, s_qkt, s_sc, s_neg, s_ex, s_rec, s_pn,
         s_tp, s_pt, s_o, s_y, s_yc, s_p2, s_m, s_t, s_z, s_w, s_x) = (sem(f"{tag}u_{n}") for n in names)
        bP, bT, bS, bR, bO, bW = ps[0:2], ps[2], ps[3:5], ps[5], ps[6], ps[7]
        PEEL = 2

        with nc.Block() as block:
            @block.sync
            def _(sp):
                if not cross:
                    sp.dma_start(XT[:, :, :], io["ctxT"].rearrange("(k p) n -> p k n", p=P)).then_inc(d_c, 16)
                    split.load(sp, 0, True, True)
                else:
                    for g in range(1, G):
                        split.load(sp, g, g < split.buffers, False)

            @block.tensor
            def _(pe):
                pe.wait_ge(s_cst, 3)

                def project(u):
                    xb, bank, odd = xs[:, u.b_par, :, :, :], bP[u.g % 2], u.g % 2
                    if u.g == 0:
                        pe.wait_ge(s_xs, u.b + 1)
                        if cross:
                            pe.wait_ge(s_clo, u.b + 1)
                    if u.before(2):
                        pe.wait_ge(s_qn, u.n - 1)
                    if cross and u.peeled and u.n < G:
                        pe.wait_ge(split.s_lo, u.n + 1)
                    if odd and cross:
                        for k in range(CB):
                            hi, lo = chi[:, u.b_par, k, :], clo[:, u.b_par, k, :]
                            pe.matmul(bank[:, :], hi, whi[:, u.g, k, :], start=(k == 0), stop=False)
                            pe.matmul(bank[:, :], hi, wlo[:, u.g, k, :], start=False, stop=False)
                            mm = pe.matmul(bank[:, :], lo, whi[:, u.g, k, :], start=False, stop=(k == CB - 1))
                    else:
                        for a, e, j in ((0, QW, 1), (QW, UW, 2)) if odd else ((0, UW, 0),):
                            for k in range(CB):
                                pe.matmul(bank[:, a:e], xb[:, j, k, :], whi[:, u.g, k, a:e], start=(k == 0), stop=False)
                                mm = pe.matmul(bank[:, a:e], xb[:, j, k, :], wlo[:, u.g, k, a:e], start=False,
                                               stop=(k == CB - 1))
                    mm.then_inc(s_proj, 1)

                def turn_qk(u):
                    pe.wait_ge(s_qn, u.n + 2 - u.g % 2)
                    if u.before(1):
                        pe.wait_ge(s_qkt, u.n)
                    pair, w = u.g - u.g % 2, u.g % 2
                    for h, src in enumerate((qkv[:, pair, 2 * w, :], qkv[:, pair, 2 * w + 1, :], qkv[:, pair + 1, w, :])):
                        mm = pe.transpose(bT[:, h * S:(h + 1) * S], src, ident[:, :])
                    mm.then_inc(s_tr, 1)

                def scores(u):
                    pe.wait_ge(s_qkt, u.n + 1)
                    if u.before(2):
                        pe.wait_ge(s_ex, u.n - 1)
                    for h in range(2):
                        mm = pe.matmul(bS[u.g % 2][:, h * S:(h + 1) * S], qkt[:, u.g % 2, h, :], qkt[:, u.g % 2, 2, :],
                                       start=True, stop=True)
                    mm.then_inc(s_sc, 1)

                def turn_p(u):
                    pe.wait_ge(s_pn, u.n + 1)
                    if u.before(1):
                        pe.wait_ge(s_pt, u.n)
                    for h in range(2):
                        mm = pe.transpose(bR[:, h * S:(h + 1) * S], pr[:, u.g % 2, h, :], ident[:, :])
                    mm.then_inc(s_tp, 1)

                def values(u):
                    pe.wait_ge(s_pt, u.n + 1)
                    if u.before(1):
                        pe.wait_ge(s_y, u.n)
                    pe.matmul(bO[:, 0:2 * S], qkv[:, u.g | 1, 2 + u.g % 2, :], pt[:, u.g % 2, :], start=True, stop=True).then_inc(s_o, 1)

                def output(u):
                    pe.wait_ge(s_z, u.n + 1)
                    if u.g == 0 and u.before(G):
                        pe.wait_ge(s_x, u.b)
                    if cross and u.peeled and u.n < G:
                        pe.wait_ge(split.s_plo, u.n + 1)
                    for h in range(2):
                        for w in (phi, plo):
                            mm = pe.matmul(bW[:, 0:C], z[:, u.g % 2, h * S:(h + 1) * S], w[:, u.g, h, :],
                                           start=(u.g == 0 and h == 0 and w is phi),
                                           stop=(u.g == G - 1 and h == 1 and w is plo))
                    mm.then_inc(s_w, 1)
                skewed(pe, B, G, [(output, LEAD + 9), (project, LEAD), (scores, LEAD + 3), (values, LEAD + 6), (turn_qk, LEAD + 2), (turn_p, LEAD + 5)], PEEL)

            @block.scalar
            def _(act):
                def columns(u):
                    if u.g:
                        return
                    if u.before(2 * G):
                        act.wait_ge(s_proj, (u.b - 1) * G)
                    j = slice(3, 4) if cross else slice(0, 3)
                    act.activation(xs[:, u.b_par, :, :, :], xq[:, j, :, bass.ds(u.b * S, S)], ACT.Copy).then_inc(s_xs, 1)
                    if cross:
                        if u.peeled and u.b == 0:
                            act.wait_ge(d_c, 16)
                        act.activation(chi[:, u.b_par, :, :], XT[:, :, bass.ds(u.b * S, S)], ACT.Copy).then_inc(s_chi, 1)

                def splitting(u):
                    if u.peeled and u.n < G:
                        split.high(act, u.n)

                def turned_qk(u):
                    act.wait_ge(s_tr, u.n + 1)
                    if u.before(2):
                        act.wait_ge(s_sc, u.n - 1)
                    a = aff[:, int(cross), :]
                    act.activation(qkt[:, u.g % 2, 0:2, :], bT[:, 0:2 * S].rearrange("p (h s) -> p h s", h=2),
                                   ACT.Identity, bias=a[:, 1:2], scale=a[:, 0:1])
                    act.activation(qkt[:, u.g % 2, 2, :], bT[:, 2 * S:3 * S], ACT.Identity, bias=a[:, 3:4],
                                   scale=a[:, 2:3]).then_inc(s_qkt, 1)

                def exps(u):
                    act.wait_ge(s_neg, u.n + 1)
                    if u.before(2):
                        act.wait_ge(s_tp, u.n - 1)
                    for h in range(2):
                        ins = act.activation(pr[:, u.g % 2, h, :], bS[u.g % 2][:, h * S:(h + 1) * S], ACT.Exp,
                                             bias=neg[:, u.g % 2, h:h + 1], accum_out=tot[:, u.g % 2, h:h + 1])
                    ins.then_inc(s_ex, 1)

                def turned_p(u):
                    act.wait_ge(s_tp, u.n + 1)
                    if u.before(2):
                        act.wait_ge(s_o, u.n - 1)
                    act.activation(pt[:, u.g % 2, :], bR[:, 0:2 * S], ACT.Copy).then_inc(s_pt, 1)

                def scaled(u):
                    act.wait_ge(s_o, u.n + 1)
                    if u.before(2):
                        act.wait_ge(s_t, u.n - 1)
                    for h in range(2):
                        head = 2 * G * int(cross) + 2 * u.g + h
                        ins = act.activation(y[:, u.g % 2, h * S:(h + 1) * S], bO[:, h * S:(h + 1) * S], ACT.Copy,
                                             scale=invsm[:, head:head + 1])
                    ins.then_inc(s_y, 1)
                stages = [(scaled, LEAD + 7), (columns, LEAD - 2), (exps, LEAD + 4), (turned_qk, LEAD + 2), (turned_p, LEAD + 5)]
                if cross:
                    stages += [(splitting, 0)]
                skewed(act, B, G, stages, PEEL)

            @block.gpsimd
            def _(pool):
                pool.memset(half[:, :], -0.5).then_inc(s_cst, 1)
                pool.memset(rstd[:, :, :], 1.0).then_inc(s_cst, 1)
                pool.memset(deps[:, :], D * LN_EPS).then_inc(s_cst, 1)
                pool.wait_ge(s_cst, 3)

                def normalise(u):
                    pool.wait_ge(s_rec, u.n + 1)
                    pool.tensor_tensor(pr[:, u.g % 2, :, :], pr[:, u.g % 2, :, :],
                                       rec[:, u.g % 2, :].unsqueeze(2).to_broadcast([P, 2, S]), ALU.mult).then_inc(s_pn, 1)

                def deviation(u):
                    pool.wait_ge(s_stat, u.n + 1)
                    v = var[:, u.g % 2, :]
                    w = HN[u.g % 2]
                    pool.tensor_tensor(v[:, 0:w], stat[:, u.g % 2, 2:3 * w:3], deps[:, 0:w], ALU.add).then_inc(s_var, 1)
                    pool.wait_ge(s_var, u.n + 1)
                    if u.before(2):
                        pool.wait_ge(s_qn, u.n - 1)
                    pool.tensor_tensor(rstd[:, u.g % 2, 0:w], v[:, 0:w], half[:, 0:w], ALU.pow).then_inc(s_rstd, 1)

                def rounded(u):
                    pool.wait_ge(s_t, u.n + 1)
                    if u.before(2):
                        pool.wait_ge(s_w, u.n - 1)
                    pool.tensor_tensor(z[:, u.g % 2, :], t[:, u.g % 2, :], m[:, u.g % 2, :], ALU.subtract).then_inc(s_z, 1)

                def context_low(u):
                    if u.g == 0:
                        at = bass.ds(u.b * S, S)
                        pool.wait_ge(s_chi, u.b + 1)
                        pool.tensor_tensor(clo[:, u.b_par, :, :], XT[:, :, at], chi[:, u.b_par, :, :].bitcast(F32),
                                           ALU.subtract).then_inc(s_clo, 1)

                def splitting(u):
                    if u.peeled and u.n < G:
                        split.low(pool, u.n)
                stages = [(rounded, LEAD + 8), (deviation, LEAD), (normalise, LEAD + 4)]
                if cross:
                    stages += [(context_low, LEAD - 2), (splitting, 0)]
                skewed(pool, B, G, stages, PEEL)

            @block.vector
            def _(dve):
                dve.wait_ge(s_cst, 3)

                def statistics(u):
                    dve.wait_ge(s_proj, u.n + 1)
                    if u.before(2):
                        dve.wait_ge(s_var, u.n - 1)
                    for h in range(HN[u.g % 2] // 2):
                        pair = bP[u.g % 2][:, h * QW:(h + 1) * QW].rearrange("p (h d) -> p d h", h=2)
                        ins = dve.bn_stats(stat[:, u.g % 2, 6 * h:6 * h + 6], pair)
                    ins.then_inc(s_stat, 1)

                def apply(u):
                    dve.wait_ge(s_rstd, u.n + 1)
                    if u.before(G):
                        dve.wait_ge(s_o, u.n - u.g % 2 - G + 2)
                    dve.tensor_tensor(qkv[:, u.g, :, :], bP[u.g % 2][:, :].rearrange("p (h d) -> p h d", h=4),
                                      rstd[:, u.g % 2, :].unsqueeze(2).to_broadcast([P, 4, D]), ALU.mult).then_inc(s_qn, 1)

                def maxima(u):
                    dve.wait_ge(s_sc, u.n + 1)
                    if u.before(2):
                        dve.wait_ge(s_ex, u.n - 1)
                    dve.tensor_reduce(neg[:, u.g % 2, :], bS[u.g % 2][:, 0:2 * S].rearrange("p (h s) -> p h s", h=2),
                                      AX.X, ALU.max, negate=True).then_inc(s_neg, 1)

                def reciprocals(u):
                    dve.wait_ge(s_ex, u.n + 1)
                    if u.before(2):
                        dve.wait_ge(s_pn, u.n - 1)
                    dve.reciprocal(rec[:, u.g % 2, :], tot[:, u.g % 2, :]).then_inc(s_rec, 1)

                def clamp(u):
                    dve.wait_ge(s_y, u.n + 1)
                    dve.tensor_scalar(y[:, u.g % 2, :], y[:, u.g % 2, :], FP8_MAX, -FP8_MAX, ALU.min, ALU.max
                                      ).then_inc(s_yc, 1)

                def power(u):
                    dve.wait_ge(s_yc, u.n + 1)
                    if u.before(2):
                        dve.wait_ge(s_z, u.n - 1)
                    dve.tensor_scalar(m[:, u.g % 2, :].bitcast(U16), y[:, u.g % 2, :].bitcast(U16), 0x7F80, None,
                                      ALU.bitwise_and).then_inc(s_p2, 1)

                def magic(u):
                    dve.wait_ge(s_p2, u.n + 1)
                    dve.tensor_scalar(m[:, u.g % 2, :], m[:, u.g % 2, :], FP8_MIN_NORMAL, ROUND, ALU.max, ALU.mult
                                      ).then_inc(s_m, 1)

                def rounding(u):
                    dve.wait_ge(s_m, u.n + 1)
                    dve.tensor_tensor(t[:, u.g % 2, :], y[:, u.g % 2, :], m[:, u.g % 2, :], ALU.add).then_inc(s_t, 1)

                def residual(u):
                    if u.g != G - 1:
                        return
                    dve.wait_ge(s_w, u.n + 1)
                    x = X[:, bass.ds(u.b, 1), :].rearrange("p a c -> p (a c)")
                    dve.scalar_tensor_tensor(x, bW[:, 0:C], pscale[:, 0:1], x, ALU.mult, ALU.add).then_inc(s_x, 1)

                def row_statistics(u):
                    if u.g == G - 1:
                        dve.wait_ge(s_x, u.b + 1)
                        dve.bn_stats(row_stats[:, bass.ds(u.b, 1), :].rearrange("p a c -> p (a c)"),
                                     X[:, bass.ds(u.b, 1), :].rearrange("p a c -> p (a c)"))

                def splitting(u):
                    if u.peeled and u.n < G:
                        split.centre(dve, u.n, u.g % 2)
                stages = [(apply, 1), (clamp, 7), (residual, 9), (statistics, 0), (power, 7), (reciprocals, 4), (magic, 7),
                          (maxima, 3), (rounding, 7)]
                if cross:
                    stages.append((row_statistics, 10))
                stages = [(stage, LEAD + lag) for stage, lag in stages]
                skewed(dve, B, G, stages + [(splitting, 0)] if cross else stages, PEEL)
                dve.wait_ge(s_x, B)


class Experts:

    def __init__(self, ctx, sbuf, nc):
        self.gate = sbuf(ctx, "moe_gate", [P, CB, E], F32)
        self.low = sbuf(ctx, "w_low", [P, 2, E, 2 * I], F32R)
        self.high = sbuf(ctx, "w_high", [P, 2, E, 2 * I], F32R)
        self.w2 = sbuf(ctx, "w2", [P, E, 2 * I], F32)
        self.up_loaded = nc.alloc_semaphore(name="experts_up_loaded")
        self.w2_loaded = nc.alloc_semaphore(name="experts_w2_loaded")

    def load_up(self, sp, io, experts):
        for e in experts:
            for i, name in enumerate(("w1", "w3")):
                sp.dma_start(self.low[:, i, e, :].bitcast(F32).rearrange("p (k n) -> p k n", k=CB),
                             io[name][e].rearrange("(k p) n -> p k n", p=P)).then_inc(self.up_loaded, 16)

    def load_w2(self, sp, io):
        for e in range(E):
            sp.dma_start(self.w2[:, e, :].rearrange("p (k n) -> p k n", k=IB),
                         io["w2"][e].rearrange("(k p) n -> p k n", p=P)).then_inc(self.w2_loaded, 16)


def moe_tiles():
    return (2 * TOK + E * (P - 1)) // P


def moe_layer(experts, nc, io, sem, sbuf, X, XT, small, ident, ps, col, cols):
    ctx = ExitStack()
    NT = moe_tiles()
    low, high, w2 = experts.low, experts.high, experts.w2
    PIECE = 2
    XB, YB = 6, 2
    sorted_x, sums = io["sorted_x"], io["sums"]
    with ctx:
        spare = XT[:, :, :].rearrange("p k n -> p (k n)")
        HB = B // 2
        taken = HB * ROW
        xrow = [spare[:, 0:taken].rearrange("p (b c) -> p b c", b=HB),
                sbuf(ctx, "f_xrow", [P, HB, ROW], F32)[:, :, :]]
        buf = []
        for n, inner in ((B, E),) * 7 + ((E, B), (1, E * B), (1, P), (1, P), (NT + 1, E)):
            buf.append(spare[:, taken:taken + n * inner].rearrange("p (b e) -> p b e", e=inner))
            taken += n * inner
        lg, ex, p_, one, two, mask, pos, count, all_ones, tri, ones, past = buf
        all_ones, tri, ones = all_ones[:, 0, :], tri[:, 0, :], ones[:, 0, :]
        h, ht = (spare[:, i * 2 * I:(i + 1) * 2 * I].rearrange("p (b c) -> p b c", b=2) for i in range(2))
        ys = xrow[1].rearrange("p b c -> p (b c)")[:, 0:YB * C].rearrange("p (b c) -> p b c", b=YB)
        flat_x = X[:, :, :].rearrange("p b c -> p (b c)")
        xin = flat_x[:, 0:XB * ROW].rearrange("p (b c) -> p b c", b=XB)
        sa = flat_x[:, XB * ROW:XB * ROW + 2 * I].rearrange("p (b c) -> p b c", b=2)
        xhi = sbuf(ctx, "f_xhi", [P, 2, C], F32R)
        xlo = sbuf(ctx, "f_xlo", [P, 2, C], F32R)
        wrow = sbuf(ctx, "f_wrow", [P, 2, E], F32)
        weight = sbuf(ctx, "f_weight", [P, 2], F32)
        mx = sbuf(ctx, "f_mx", [P, B], F32)
        pm = sbuf(ctx, "f_pm", [P, B], F32)
        prio = sbuf(ctx, "f_prio", [P, E], F32)
        upto = sbuf(ctx, "f_upto", [P, 1 + E * B], F32)
        tiles = sbuf(ctx, "f_tiles", [P, E], F32)
        end = sbuf(ctx, "f_end", [P, E], F32)
        base = sbuf(ctx, "f_base", [P, E], F32)
        row = sbuf(ctx, "f_row", [P, 2, B], F32)
        rows = sbuf(ctx, "f_rows", [P, 2, B], I32)
        tile_no = sbuf(ctx, "f_tile_no", [P, NT + 1], F32)
        owner = sbuf(ctx, "f_owner", [P, NT + 1], F32)
        owners = sbuf(ctx, "f_owners", [P, NT + 1], I32)
        d_init, d_sc, d_add = (sem("f_" + n) for n in ("dinit", "dsc", "dadd"))
        d_x = [sem(f"f_dx{i}") for i in range(XB)]
        (s_hi, s_lo, s_xh, s_cst, s_row, s_xrow, s_th, s_d, s_ex, s_mask, s_cnt, s_rows, s_own, s_xt, s_xe, s_up, s_si, s_mu, s_ht,
         s_he, s_y, s_wr, s_wt, s_ye, s_go, s_link) = (sem("f_" + n) for n in (
             "hi", "lo", "xh", "cst", "row", "xrow", "th", "d", "ex", "mask", "cnt", "rows", "own", "xt", "xe", "up", "si", "mu",
             "ht", "he", "y", "wr", "wt", "ye", "go", "link"))
        bX, bU, bH, bY = ps[0], (ps[1:3], ps[3:5]), ps[5], ps[6:8]
        PER, PEEL = 3, 2
        TURN_X, UP, DOWN, ADD = 2, 3, 4, 5

        def slot(u):
            return u.b_par * PER + u.g

        with nc.Block() as block:
            @block.sync
            def _(sp):
                sp.dma_start(sums[0:TOK, :].rearrange("(b p) c -> p b c", p=P), X[:, :, :]).then_inc(d_init, 16)
                experts.load_up(sp, io, range(E // 2, E))
                experts.load_w2(sp, io)
                sp.wait_ge(d_init, 16)
                sp.wait_ge(d_sc, 2 * B * 16)

                def load(u):
                    if u.before(XB):
                        sp.wait_ge(d_add, 16 * (u.n - XB + 1))
                    sp.dma_start(xin[:, slot(u), :], sorted_x[bass.ds(u.n * P, P), :]).then_inc(d_x[slot(u)], 16)
                skewed(sp, NT // PER, PER, [(load, 0)], PEEL)
                sp.wait_ge(d_add, 16 * NT)

            @block.tensor
            def _(pe):
                pe.wait_ge(s_cst, 4)
                pe.wait_ge(s_mask, 1)
                choice = mask[:, :, :].rearrange("p b e -> p (b e)")
                pe.matmul(ps[6][:, 0:B * E], tri[:, :], choice, start=True, stop=True)
                pe.matmul(ps[6][:, B * E:2 * B * E], ones[:, :], choice, start=True, stop=True).then_inc(s_cnt, 1)
                pe.wait_ge(s_own, 1)
                pe.wait_ge(s_lo, 2 * E // PIECE)
                pe.wait_ge(experts.w2_loaded, 16 * E)
                loaded = [pe.alloc_register(f"expert{i}") for i in range(PER + 1)]
                expert = {}


                def load_experts(u):
                    if u.g == 0:
                        pe.load(loaded, owners[0:1, bass.ds(u.n, PER + 1)])
                        for i, register in enumerate(loaded):
                            expert[i] = pe.snap(register, min_val=0, max_val=E - 1)

                def turn_x(u):
                    pe.wait_ge(d_x[slot(u)], 16 * u.turn + 16)
                    if u.before(1):
                        pe.wait_ge(s_xe, u.n)
                    for k in range(CB):
                        mm = pe.transpose(bX[:, k * P:(k + 1) * P], xin[:, slot(u), k * P:(k + 1) * P], ident[:, :])
                    mm.then_inc(s_xt, 1)

                def up(u):
                    pe.wait_ge(s_xe, u.n + 1)
                    if u.before(2):
                        pe.wait_ge(s_mu, u.n - 1)
                    at = bass.ds(expert[(u.g + UP) % PER + 1], 1)
                    for i in range(2):
                        for k in range(CB):
                            x_hi, x_lo = (a[:, slot(u) % 2, k * P:(k + 1) * P] for a in (xhi, xlo))
                            w_hi, w_lo = (a[:, i, at, k * I:(k + 1) * I] for a in (high, low))
                            bank = bU[slot(u) % 2][i][:, :]
                            pe.matmul(bank, x_hi, w_hi, start=(k == 0), stop=False)
                            pe.matmul(bank, x_hi, w_lo, start=False, stop=False)
                            mm = pe.matmul(bank, x_lo, w_hi, start=False, stop=(k == CB - 1))
                        mm.then_inc(s_up, 1)

                def turn_h(u):
                    pe.wait_ge(s_mu, u.n + 1)
                    if u.before(1):
                        pe.wait_ge(s_he, u.n)
                    for j in range(IB):
                        mm = pe.transpose(bH[:, j * P:(j + 1) * P], h[:, slot(u) % 2, j * P:(j + 1) * P], ident[:, :])
                    mm.then_inc(s_ht, 1)

                def down(u):
                    place = (u.g + DOWN) % PER
                    if u.peeled and u.n == NT - 1 and place == 0:
                        place = PER
                    pe.wait_ge(s_he, u.n + 1)
                    if u.before(2):
                        pe.wait_ge(s_ye, u.n - 1)
                    for j in range(IB):
                        mm = pe.matmul(bY[slot(u) % 2][:, 0:C], ht[:, slot(u) % 2, j * P:(j + 1) * P],
                                       w2[:, bass.ds(expert[place], 1), j * C:(j + 1) * C], start=(j == 0), stop=(j == IB - 1))
                    mm.then_inc(s_y, 1)
                skewed(pe, NT // PER, PER, [(load_experts, UP), (turn_h, DOWN), (turn_x, TURN_X), (up, UP), (down, DOWN)], PEEL)

            @block.scalar
            def _(act):
                act.activation(lg[:, :, :], ps[0][:, 0:B * E].rearrange("p (b e) -> p b e", e=E), ACT.Tanh,
                               scale=1.0 / SOFTCAP).then_inc(s_th, 1)
                act.wait_ge(s_d, 1)
                act.activation(ex[:, :, :], p_[:, :, :], ACT.Exp, scale=SOFTCAP).then_inc(s_ex, 1)
                for b in range(B):
                    act.activation(xrow[b // HB][:, b % HB, 0:C], X[:, b, :], ACT.Copy).then_inc(s_xrow, 1)
                act.wait_ge(d_init, 16)
                act.wait_ge(experts.up_loaded, 16 * 2 * E)
                for e in range(0, E, PIECE):
                    for i in range(2):
                        act.activation(high[:, i, e:e + PIECE, :], low[:, i, e:e + PIECE, :].bitcast(F32), ACT.Copy
                                       ).then_inc(s_hi, 1)

                def turned_x(u):
                    act.wait_ge(s_xt, u.n + 1)
                    if u.before(2):
                        act.wait_ge(s_up, 2 * u.n - 2)
                    act.activation(xhi[:, slot(u) % 2, :], bX[:, 0:C], ACT.Copy).then_inc(s_xh, 1)

                def silu(u):
                    act.wait_ge(s_up, 2 * u.n + 1)
                    if u.before(2):
                        act.wait_ge(s_mu, u.n - 1)
                    act.activation(sa[:, slot(u) % 2, :], bU[slot(u) % 2][0][:, :], ACT.Silu).then_inc(s_si, 1)

                def turned_h(u):
                    act.wait_ge(s_ht, u.n + 1)
                    if u.before(2):
                        act.wait_ge(s_y, u.n - 1)
                    act.activation(ht[:, slot(u) % 2, :], bH[:, :], ACT.Copy).then_inc(s_he, 1)
                skewed(act, NT // PER, PER, [(turned_h, DOWN), (turned_x, TURN_X), (silu, UP)], PEEL)

            @block.gpsimd
            def _(pool):
                for rows_ in xrow:
                    pool.memset(rows_[:, :, C:ROW], 0.0).then_inc(s_row, 1)
                pool.wait_ge(s_row, 2)
                for half, rows_ in enumerate(xrow):
                    pool.iota(rows_[:, :, ROW_ID].bitcast(I32), pattern=[[P, HB]], base=half * HB * P, channel_multiplier=1
                              ).then_inc(s_row, 1)
                for n in range(E):
                    ins = pool.memset(prio[:, n:n + 1], float(E - n))
                ins.then_inc(s_cst, 1)
                pool.memset(ones[:, :], 1.0).then_inc(s_cst, 1)
                pool.memset(tri[:, :], 1.0).then_inc(s_cst, 1)
                pool.wait_ge(s_cst, 3)
                pool.affine_select(out=tri[:, :], in_=tri[:, :], compare_op=ALU.is_ge, fill=0.0,
                                   base=-1, pattern=[[1, P]], channel_multiplier=-1).then_inc(s_cst, 1)
                pool.wait_ge(s_rows, 3)
                pool.wait_ge(s_xrow, B)
                pool.wait_ge(s_row, 4)
                for j in range(2):
                    for b in range(B):
                        pool.indirect_dma_start(
                            out=sorted_x, out_offset=bass.IndirectOffsetOnAxis(ap=rows[:, j, b:b + 1], axis=0),
                            in_=xrow[b // HB][:, b % HB, :], in_offset=None).then_inc(d_sc, 16)
                pool.wait_ge(d_sc, 2 * B * 16)
                pool.wait_ge(d_init, 16)

                def add(u):
                    if u.before(1):
                        pool.wait_ge(d_add, 16 * u.n)
                    pool.wait_ge(s_ye, u.n + 1)
                    pool.sem_inc(s_go, 1)
                    pool.indirect_dma_start(
                        out=sums, out_offset=bass.IndirectOffsetOnAxis(
                            ap=xin[:, slot(u), ROW_ID:ROW_ID + 1].bitcast(I32), axis=0),
                        in_=ys[:, slot(u) % 2, :], in_offset=None, compute_op=ALU.add).then_inc(d_add, 16)
                skewed(pool, NT // PER, PER, [(add, ADD)], PEEL)

            @block.vector
            def _(dve):
                link = Links(dve, s_link)
                over = lambda a: a.unsqueeze(2).to_broadcast([P, B, E])
                link(dve.memset(upto[:, 0:1], 0.0))
                link(dve.memset(all_ones[:, :], 1.0))
                link(dve.tensor_tensor_scan(tile_no[:, :], all_ones[:, 0:NT + 1], all_ones[:, 0:NT + 1], -1.0, ALU.mult, ALU.add))
                dve.wait_ge(s_th, 1)
                dve.wait_ge(s_cst, 1)
                dve.wait_ge(s_row, 2)
                link(dve.tensor_reduce(mx[:, :], lg[:, :, :], AX.X, ALU.max))
                dve.tensor_tensor(p_[:, :, :], lg[:, :, :], over(mx[:, :]), ALU.subtract).then_inc(s_d, 1)
                dve.wait_ge(s_ex, 1)
                link(dve.tensor_reduce(mx[:, :], ex[:, :, :], AX.X, ALU.add))
                link(dve.reciprocal(mx[:, :], mx[:, :]))
                link(dve.tensor_tensor(p_[:, :, :], ex[:, :, :], over(mx[:, :]), ALU.mult))

                def first_of_best(out, a):
                    link(dve.tensor_reduce(mx[:, :], a, AX.X, ALU.max))
                    link(dve.tensor_tensor(out, a, over(mx[:, :]), ALU.is_ge))
                    link(dve.tensor_tensor(out, out, prio[:, :].unsqueeze(1).to_broadcast([P, B, E]), ALU.mult))
                    link(dve.tensor_reduce(pm[:, :], out, AX.X, ALU.max))
                    link(dve.tensor_tensor(out, out, over(pm[:, :]), ALU.is_equal))

                first_of_best(one[:, :, :], p_[:, :, :])
                link(dve.scalar_tensor_tensor(ex[:, :, :], one[:, :, :], -4.0, p_[:, :, :], ALU.mult, ALU.add))
                first_of_best(two[:, :, :], ex[:, :, :])
                dve.tensor_tensor(mask[:, :, :], one[:, :, :], two[:, :, :], ALU.add).then_inc(s_mask, 1)
                dve.wait_ge(s_mask, 1)
                for half, rows_ in enumerate(xrow):
                    b = slice(half * HB, half * HB + HB)
                    dve.tensor_tensor(rows_[:, :, ROW_WEIGHTS:ROW_WEIGHTS + E], mask[:, b, :], p_[:, b, :], ALU.mult
                                      ).then_inc(s_rows, 1)
                dve.wait_ge(s_cnt, 1)
                link(dve.tensor_copy(count[:, :, :], ps[6][:, B * E:2 * B * E].rearrange("p (b e) -> p e b", e=E)))
                flat = count[:, :, :].rearrange("p e b -> p (e b)")
                link(dve.tensor_tensor_scan(upto[:, 1:1 + E * B], all_ones[:, :], flat, 0.0, ALU.mult, ALU.add))
                start, stop_ = upto[:, 0:E * B:B], upto[:, B:1 + E * B:B]
                link(dve.tensor_tensor(tiles[:, :], stop_, start, ALU.subtract))
                link(dve.tensor_scalar(tiles[:, :], tiles[:, :], 1.0 / P, (P / 2 - 0.5) / P, ALU.mult, ALU.add))
                link(dve.tensor_scalar(tiles[:, :], tiles[:, :], WHOLE, None, ALU.add))
                link(dve.tensor_scalar(tiles[:, :], tiles[:, :], -WHOLE, None, ALU.add))
                link(dve.tensor_tensor_scan(end[:, :], all_ones[:, 0:E], tiles[:, :], 0.0, ALU.mult, ALU.add))
                link(dve.tensor_tensor(base[:, :], end[:, :], tiles[:, :], ALU.subtract))
                link(dve.scalar_tensor_tensor(base[:, :], base[:, :], float(P), start, ALU.mult, ALU.subtract))
                before = upto[:, 0:E * B].rearrange("p (e b) -> p b e", b=B)
                link(dve.tensor_tensor(pos[:, :, :], ps[6][:, 0:B * E].rearrange("p (b e) -> p b e", e=E), before, ALU.add))
                link(dve.tensor_tensor(pos[:, :, :], pos[:, :, :], base[:, :].unsqueeze(1).to_broadcast([P, B, E]), ALU.add))
                for j, choice in enumerate((one, two)):
                    link(dve.tensor_tensor(choice[:, :, :], choice[:, :, :], pos[:, :, :], ALU.mult))
                    link(dve.tensor_reduce(row[:, j, :], choice[:, :, :], AX.X, ALU.add))
                dve.tensor_copy(rows[:, :, :], row[:, :, :]).then_inc(s_rows, 1)
                link(dve.tensor_tensor(past[:, :, :], tile_no[:, :].unsqueeze(2).to_broadcast([P, NT + 1, E]),
                                       end[:, :].unsqueeze(1).to_broadcast([P, NT + 1, E]), ALU.is_gt))
                link(dve.tensor_reduce(owner[:, :], past[:, :, :], AX.X, ALU.add))
                dve.tensor_scalar(owners[:, :], owner[:, :], float(E - 1), None, ALU.min).then_inc(s_own, 1)
                link(dve.tensor_scalar(owner[:, :], owner[:, :], -1.0, float(E), ALU.mult, ALU.add))
                link(dve.tensor_tensor(past[:, :, :], owner[:, :].unsqueeze(2).to_broadcast([P, NT + 1, E]),
                                       prio[:, :].unsqueeze(1).to_broadcast([P, NT + 1, E]), ALU.is_equal))

                for e in range(0, E, PIECE):
                    for i in range(2):
                        dve.wait_ge(s_hi, e // PIECE * 2 + i + 1)
                        dve.tensor_tensor(low[:, i, e:e + PIECE, :], low[:, i, e:e + PIECE, :].bitcast(F32),
                                          high[:, i, e:e + PIECE, :].bitcast(F32), ALU.subtract).then_inc(s_lo, 1)

                def low_x(u):
                    dve.wait_ge(s_xh, u.n + 1)
                    if u.before(2):
                        dve.wait_ge(s_up, 2 * u.n - 2)
                    dve.tensor_tensor(xlo[:, slot(u) % 2, :], bX[:, 0:C], xhi[:, slot(u) % 2, :].bitcast(F32), ALU.subtract
                                      ).then_inc(s_xe, 1)

                def gated(u):
                    dve.wait_ge(s_si, u.n + 1)
                    dve.wait_ge(s_up, 2 * u.n + 2)
                    if u.before(2):
                        dve.wait_ge(s_ht, u.n - 1)
                    dve.tensor_tensor(h[:, slot(u) % 2, :], sa[:, slot(u) % 2, :], bU[slot(u) % 2][1][:, :],
                                      ALU.mult).then_inc(s_mu, 1)

                def weights(u):
                    dve.wait_ge(s_xt, u.n + 1)
                    dve.tensor_tensor(wrow[:, slot(u) % 2, :].unsqueeze(1), xin[:, slot(u), ROW_WEIGHTS:ROW_WEIGHTS + E].unsqueeze(1),
                                      past[:, bass.ds(u.n + 1, 1), :], ALU.mult).then_inc(s_wr, 1)
                    dve.wait_ge(s_wr, u.n + 1)
                    dve.tensor_reduce(weight[:, slot(u) % 2:slot(u) % 2 + 1], wrow[:, slot(u) % 2, :], AX.X, ALU.add).then_inc(s_wt, 1)

                def result(u):
                    dve.wait_ge(s_wt, u.n + 1)
                    dve.wait_ge(s_y, u.n + 1)
                    if u.before(YB):
                        dve.wait_ge(d_add, 16 * (u.n - YB + 1))
                    dve.tensor_scalar(ys[:, slot(u) % 2, :], bY[slot(u) % 2][:, 0:C], weight[:, slot(u) % 2:slot(u) % 2 + 1], None, ALU.mult
                                      ).then_inc(s_ye, 1)
                skewed(dve, NT // PER, PER, [(low_x, TURN_X), (gated, UP), (result, DOWN), (weights, UP)], PEEL)


def _launch_arrays(i):
    f = np.float32
    a = {k: np.asarray(v) for k, v in i.items()}
    io = {}
    io["xT"] = a["x"].reshape(TOK, C).T
    io["wa"] = a["L0_attn_W"].T
    rep = lambda v: np.broadcast_to(v.reshape(1, -1), (P, v.size))
    blk = lambda v: v.reshape(-1, P).T
    n = "L1_xattn_"
    small = [blk(a["L0_attn_b"])] + [blk(a[n + k]) for k in ("qln_w", "qln_b", "kln_w", "kln_b", "qxln_w", "qxln_b",
                                                            "kxln_w", "kxln_b", "ln_w", "ln_b", "q_in_scale",
                                                            "k_in_scale", "v_in_scale", "qx_in_scale", "proj_smooth")]
    small += [rep(a[n + k]) for k in ("wq_scale", "wk_scale", "wv_scale", "wqx_scale", "proj_in_scale", "proj_w_scale")]
    small += [rep(a["L0_xattn_D"]), rep(a["L0_ffn_imp_center"]), rep(a["L0_ffn_imp_slope"])]
    io["small"] = np.concatenate(small, axis=1)
    ctx = a["ctx_2048"].reshape(TOK, C)
    io["ctxR"] = ctx.T.reshape(CB, P, TOK)[:, ::-1]
    pad = np.zeros((CH, P - 1 + C), f)
    pad[:, P - 1:] = a["L0_xattn_ssm_kernel"]
    io["toep"] = np.stack([pad[:, m:m + C] for m in range(P)], axis=1)
    io["wf"] = np.concatenate([a["L0_ffn_select_weight"].transpose(1, 0, 2).reshape(C, SEL),
                               a["L0_ffn_lora_update"].transpose(1, 0, 2).reshape(C, UPD),
                               a["L0_ffn_select_mean_diff"].T], axis=1)
    io["deb"] = a["L0_ffn_debias_w"].T
    io["lw"] = np.concatenate([a["L0_ffn_lora_degen"].transpose(0, 2, 1).reshape(UPD, C), a["L0_ffn_bias_w"]])
    QB, PAD = HQ // HKV, P // HKV
    wq = np.zeros((C, QB, HKV, PAD), f)
    wq[..., :HD] = a["L1_attn_Wq"].reshape(HKV, QB, HD, C).transpose(3, 1, 0, 2)
    wk = np.zeros((C, HKV, PAD), f)
    wk[..., :HD] = a["L1_attn_Wk"].reshape(HKV, HD, C).transpose(2, 0, 1)
    io["d_wq"], io["d_wk"] = wq.reshape(C, QB * P), wk.reshape(C, P)
    io["d_wv"], io["d_wo"] = a["L1_attn_Wv"].T, a["L1_attn_Wo"].T
    pairs = lambda w, h: w.reshape(-1, 2, h * D, C)
    item = lambda *ws: np.concatenate(ws, axis=1).transpose(0, 2, 1)
    side = lambda w: w.reshape(w.shape[0], -1, C)
    kv = a[n + "w_kv_x"].reshape(2, G * D, C)
    for name, q, k, v in (("wself", a[n + "wq"], a[n + "wk"], a[n + "wv"]), ("wcross", a[n + "wqx"], kv[0], kv[1])):
        even, odd = item(side(pairs(q, 2))), item(side(pairs(k, 1)), side(pairs(v, 1)))
        io[name] = np.stack([even, odd], axis=1).reshape(G, C, UW)
    io["wproj"] = a[n + "wproj"].T.reshape(2, 2 * G, D, C)
    io["ctxT"] = ctx.T
    io["w_gate"] = a["L1_ffn_w_gate"]
    io["w1"], io["w3"], io["w2"] = a["L1_ffn_w1"], a["L1_ffn_w3"], a["L1_ffn_w2"]
    return {k: np.ascontiguousarray(v) for k, v in io.items()}


STOP = 99


def kernel(**inputs):
    import concourse.bacc as bacc
    from concourse.bass_utils import run_bass_kernel_spmd

    nc = bacc.Bacc("TRN2", target_bir_lowering=False, num_devices=1)
    arrays = _launch_arrays(inputs)
    io = {k: nc.dram_tensor(k + "_dram", v.shape, mybir.dt.from_np(v.dtype), kind="ExternalInput").ap()
          for k, v in arrays.items()}
    io["out"] = nc.dram_tensor("out_dram", (B, S, C), F32, kind="ExternalOutput").ap()
    build(nc, io, STOP)
    r = run_bass_kernel_spmd(nc, [{k + "_dram": v for k, v in arrays.items()}], core_ids=[0])
    return r.results[0]["out_dram"]
```
